# Optimizing a Trainium2 kernel written in Bass

```python
import numpy as np
import jax
import jax.numpy as jnp

def _softmax(x, axis=-1):
    return jax.nn.softmax(x, axis=axis)

def _gelu(x):
    return jax.nn.gelu(x, approximate=True)

def _silu(x):
    return jax.nn.silu(x)

def _sigmoid(x):
    return jax.nn.sigmoid(x)

def _layernorm(x, axis=-1, eps=1e-05):
    m = jnp.mean(x, axis=axis, keepdims=True)
    v = jnp.var(x, axis=axis, keepdims=True)
    return (x - m) / jnp.sqrt(v + eps)

def _scatter_add(tgt, idx, src, axis=0):
    return tgt.at[idx].add(src)

def _segment_sum(src, seg, n):
    return jax.ops.segment_sum(src, seg, n)
kernel_name = 'mk_recurrent_d1_jaxref_r4_d57f1f'

def setup_inputs(seed: int=0):
    np.random.seed(seed)
    _w = jnp.asarray

    def _L0_attn_setup():
        import jax, jax.numpy as jnp
        import numpy as np
        from jax import lax
        B, T, D = (2, 256, 512)
        HK, HV = (8, 16)
        DK, DV = (128, 128)
        KW = 4
        EPS = 1e-06
        KEY_DIM = HK * DK
        VALUE_DIM = HV * DV
        CONV_DIM = 2 * KEY_DIM + VALUE_DIM

        def _causal_conv_silu(x, w):
            k = w.shape[1]
            xp = jnp.pad(x, ((0, 0), (0, 0), (k - 1, 0)))
            y = sum((w[:, j][None, :, None] * xp[:, :, j:j + x.shape[2]] for j in range(k)))
            return jax.nn.silu(y)

        def _l2norm(x):
            return x * lax.rsqrt(jnp.sum(x * x, -1, keepdims=True) + 1e-06)
        key = jax.random.key(seed)
        ks = jax.random.split(key, 9)
        w = lambda k, shape, s=0.02: jax.random.normal(k, shape, jnp.float32) * s
        return {'hidden_states': jax.random.normal(ks[0], (B, T, D), jnp.float32), 'W_qkv': w(ks[1], (D, CONV_DIM)), 'W_z': w(ks[2], (D, VALUE_DIM)), 'W_b': w(ks[3], (D, HV)), 'W_a': w(ks[4], (D, HV)), 'conv_w': w(ks[5], (CONV_DIM, KW), 0.5), 'dt_bias': jnp.ones((HV,), jnp.float32), 'A_log': jnp.log(jax.random.uniform(ks[6], (HV,), jnp.float32, 0.001, 16.0)), 'norm_weight': jnp.ones((DV,), jnp.float32), 'W_out': w(ks[7], (VALUE_DIM, D))}
    _L0_attn_in = _L0_attn_setup()

    def _L0_ffn_setup():
        import jax, jax.numpy as jnp
        import numpy as np
        B, S, D = (2, 1024, 512)
        E, DFF = (8, 2048)
        TOP_K = 2
        key = jax.random.key(seed)
        ks = jax.random.split(key, 4)
        scale_in = 1.0 / np.sqrt(D)
        scale_ff = 1.0 / np.sqrt(DFF)
        return {'hidden_states': jax.random.normal(ks[0], (B, S, D), dtype=jnp.float32), 'gate_w': jax.random.normal(ks[1], (E, D), dtype=jnp.float32) * scale_in, 'w1': jax.random.normal(ks[2], (E, D, DFF), dtype=jnp.float32) * scale_in, 'b1': jnp.zeros((E, DFF), dtype=jnp.float32), 'w2': jax.random.normal(ks[3], (E, DFF, D), dtype=jnp.float32) * scale_ff, 'b2': jnp.zeros((E, D), dtype=jnp.float32)}
    _L0_ffn_in = _L0_ffn_setup()
    _d = {'L0_attn_hidden_states': _L0_attn_in['hidden_states'], 'L0_attn_W_qkv': _L0_attn_in['W_qkv'], 'L0_attn_W_z': _L0_attn_in['W_z'], 'L0_attn_W_b': _L0_attn_in['W_b'], 'L0_attn_W_a': _L0_attn_in['W_a'], 'L0_attn_conv_w': _L0_attn_in['conv_w'], 'L0_attn_dt_bias': _L0_attn_in['dt_bias'], 'L0_attn_A_log': _L0_attn_in['A_log'], 'L0_attn_norm_weight': _L0_attn_in['norm_weight'], 'L0_attn_W_out': _L0_attn_in['W_out'], 'L0_ffn_gate_w': _L0_ffn_in['gate_w'], 'L0_ffn_w1': _L0_ffn_in['w1'], 'L0_ffn_b1': _L0_ffn_in['b1'], 'L0_ffn_w2': _L0_ffn_in['w2'], 'L0_ffn_b2': _L0_ffn_in['b2']}
    _x0 = _d['L0_attn_hidden_states']
    _d['L0_attn_hidden_states'] = jax.random.normal(jax.random.fold_in(jax.random.key(seed), 1), (1, 2048, 512), dtype=_x0.dtype)
    del _x0
    return _d

def reference(L0_attn_hidden_states, L0_attn_W_qkv, L0_attn_W_z, L0_attn_W_b, L0_attn_W_a, L0_attn_conv_w, L0_attn_dt_bias, L0_attn_A_log, L0_attn_norm_weight, L0_attn_W_out, L0_ffn_gate_w, L0_ffn_w1, L0_ffn_b1, L0_ffn_w2, L0_ffn_b2):

    def _L0_attn_ref(hidden_states, W_qkv, W_z, W_b, W_a, conv_w, dt_bias, A_log, norm_weight, W_out):
        import jax, jax.numpy as jnp
        import numpy as np
        from jax import lax
        B, T, D = (2, 256, 512)
        HK, HV = (8, 16)
        DK, DV = (128, 128)
        KW = 4
        EPS = 1e-06
        KEY_DIM = HK * DK
        VALUE_DIM = HV * DV
        CONV_DIM = 2 * KEY_DIM + VALUE_DIM

        def _causal_conv_silu(x, w):
            k = w.shape[1]
            xp = jnp.pad(x, ((0, 0), (0, 0), (k - 1, 0)))
            y = sum((w[:, j][None, :, None] * xp[:, :, j:j + x.shape[2]] for j in range(k)))
            return jax.nn.silu(y)

        def _l2norm(x):
            return x * lax.rsqrt(jnp.sum(x * x, -1, keepdims=True) + 1e-06)
        Bb, Tt, _ = hidden_states.shape
        mixed = hidden_states @ W_qkv
        mixed = _causal_conv_silu(mixed.transpose(0, 2, 1), conv_w).transpose(0, 2, 1)
        q, k, v = jnp.split(mixed, [KEY_DIM, 2 * KEY_DIM], axis=-1)
        q = q.reshape(Bb, Tt, HK, DK)
        k = k.reshape(Bb, Tt, HK, DK)
        v = v.reshape(Bb, Tt, HV, DV)
        z = (hidden_states @ W_z).reshape(Bb, Tt, HV, DV)
        beta = jax.nn.sigmoid(hidden_states @ W_b)
        g = -jnp.exp(A_log) * jax.nn.softplus(hidden_states @ W_a + dt_bias)
        rep = HV // HK
        q = jnp.repeat(q, rep, axis=2)
        k = jnp.repeat(k, rep, axis=2)
        q = _l2norm(q) * DK ** (-0.5)
        k = _l2norm(k)
        qs = q.transpose(1, 0, 2, 3)
        ks = k.transpose(1, 0, 2, 3)
        vs = v.transpose(1, 0, 2, 3)
        gs = g.transpose(1, 0, 2)
        bs = beta.transpose(1, 0, 2)

        def step(S, inp):
            qt, kt, vt, gt, bt = inp
            S = S * jnp.exp(gt)[..., None, None]
            v_adj = (vt - jnp.einsum('bhk,bhkv->bhv', kt, S)) * bt[..., None]
            S = S + kt[..., None] * v_adj[..., None, :]
            o = jnp.einsum('bhk,bhkv->bhv', qt, S)
            return (S, o)
        S0 = jnp.zeros((Bb, HV, DK, DV), jnp.float32)
        _, o = lax.scan(step, S0, (qs, ks, vs, gs, bs))
        o = o.transpose(1, 0, 2, 3)
        var = jnp.mean(o * o, -1, keepdims=True)
        o = o * lax.rsqrt(var + EPS) * norm_weight
        o = o * jax.nn.silu(z)
        return o.reshape(Bb, Tt, VALUE_DIM) @ W_out

    def _L0_ffn_ref(hidden_states, gate_w, w1, b1, w2, b2):
        import jax, jax.numpy as jnp
        import numpy as np
        B, S, D = (2, 1024, 512)
        E, DFF = (8, 2048)
        TOP_K = 2
        b, s, d = hidden_states.shape
        x = hidden_states.reshape(-1, d)
        router_logits = x @ gate_w.T
        _, sel = jax.lax.top_k(router_logits.sum(axis=0), TOP_K)
        rw = jax.nn.softmax(router_logits[:, sel].astype(jnp.float32), axis=1)
        rw = rw.astype(x.dtype)
        w1s, b1s = (w1[sel], b1[sel])
        w2s, b2s = (w2[sel], b2[sel])
        h = jax.nn.gelu(jnp.einsum('nd,kdf->knf', x, w1s) + b1s[:, None, :])
        y = jnp.einsum('knf,kfd->knd', h, w2s) + b2s[:, None, :]
        out = jnp.einsum('nk,knd->nd', rw, y)
        return out.reshape(b, s, -1)
    x = L0_attn_hidden_states
    xn = _layernorm(x, axis=-1)
    s = _L0_attn_ref(xn, L0_attn_W_qkv, L0_attn_W_z, L0_attn_W_b, L0_attn_W_a, L0_attn_conv_w, L0_attn_dt_bias, L0_attn_A_log, L0_attn_norm_weight, L0_attn_W_out)
    g = _silu(_L0_ffn_ref(xn, L0_ffn_gate_w, L0_ffn_w1, L0_ffn_b1, L0_ffn_w2, L0_ffn_b2))
    x = x + s * g
    return x

_drawn_inputs = setup_inputs


def setup_inputs(seed=0):
    import zlib

    import numpy as np

    out = dict(_drawn_inputs(seed))
    spreads = {'L0_attn_dt_bias': (1.0, 0.6),
     'L0_attn_norm_weight': (1.0, 0.6),
     'L0_ffn_b1': (0.0, 0.8),
     'L0_ffn_b2': (0.0, 0.8)}
    factors = {'L0_attn_W_b': 8.0, 'L0_attn_W_a': 8.0, 'L0_attn_A_log': 8.0}
    for name, (base, spread) in spreads.items():
        noise = np.random.default_rng([zlib.crc32(name.encode()), seed]).standard_normal(out[name].shape)
        drawn = base * np.exp(spread * noise) if base else spread * noise
        out[name] = jnp.asarray(drawn.astype(out[name].dtype))
    for name, factor in factors.items():
        out[name] = (out[name] * factor).astype(out[name].dtype)
    return out
```

```python
from contextlib import ExitStack

import concourse.bass as bass
import numpy as np
from concourse import mybir

P = 128
T, D = 2048, 512
KEY_HEADS, HEADS, HD = 8, 16, 128
KW = 4
EXPERTS, DFF, TOP = 8, 2048, 2
LN_EPS, L2_EPS, RMS_EPS = 1e-5, 1e-6, 1e-6
NT = T // P
ND = D // P
SB = 512
NSB = T // SB
CPS = SB // P
REP = HEADS // KEY_HEADS
QUAD = 2
NHC = QUAD * REP
NAB = 2 * HEADS + EXPERTS
NBUF = 3
LEVELS = 7
SERIES = 9
KINDS = {"k": (0, P), "q": (P, P), "v0": (2 * P, P), "v1": (3 * P, P), "z": (4 * P, REP * HD)}
GW = 4 * P + REP * HD


def constants():
    i = np.arange(P)
    parts = {
        "ident": np.eye(P),
        "after": (i[:, None] > i[None, :]),
        "upto": (i[:, None] <= i[None, :]),
        "ones": np.ones((P, P)),
        "kq": np.concatenate([-(i[:, None] < i[None, :]).astype(float), (i[:, None] <= i[None, :])], 1),
        "pairs": (i[:, None] % 2 == 0) & (i[None, :] == i[:, None] + 1),
        "iota": np.broadcast_to(np.arange(EXPERTS), (P, EXPERTS)),
    }
    for lev in range(1, LEVELS):
        s = 1 << lev
        col = np.arange(P // 2) // s
        parts[f"rows{lev}"] = (i[:, None] // (2 * s) == col[None, :]) & ((i[:, None] // s) % 2 == 1)
    at, where = 0, {}
    for name, a in parts.items():
        where[name] = (at, at + a.shape[1])
        at += a.shape[1]
    return np.concatenate([np.asarray(a, np.float32) for a in parts.values()], 1), where


class Program:

    def __init__(self, nc, ctx):
        self.nc, self.ctx = nc, ctx
        self.queue = {e: [] for e in ("pe", "act", "dve", "pool", "sp")}
        self.sem = {e: ctx.enter_context(nc.semaphore(f"s_{e}")) for e in ("pe", "act", "dve", "pool")}
        self.count = {}
        self.done = {}
        self.seen = {}

    def wait(self, engine, *steps):
        for step in steps:
            sem, value = self.done[step]
            if self.seen.get((engine, sem), 0) < value:
                self.seen[engine, sem] = value
                self.queue[engine].append(lambda e, s=self.sem[sem], v=value: e.wait_ge(s, v))

    def do(self, engine, waits, fn, step):
        self.wait(engine, *waits)
        self.count[engine] = self.count.get(engine, 0) + 1
        self.done[step] = (engine, self.count[engine])
        self.queue[engine].append(lambda e, s=self.sem[engine]: fn(e).then_inc(s, 1))

    def dma(self, waits, fn, step, lane):
        if lane not in self.sem:
            self.sem[lane] = self.ctx.enter_context(self.nc.semaphore(f"s_dma_{lane}"))
        self.wait("sp", *waits)
        self.count[lane] = self.count.get(lane, 0) + 16
        self.done[step] = (lane, self.count[lane])
        self.queue["sp"].append(lambda e, s=self.sem[lane]: fn(e).then_inc(s, 16))

    def fence(self, engines=("pe", "act", "dve", "pool", "sp")):
        for sem, value in self.count.items():
            self.done["fence", sem] = (sem, value)
        for engine in engines:
            self.wait(engine, *[("fence", sem) for sem in self.count])


def merge(*streams):
    keyed = [((i + 0.5) / len(s), n, i, f) for n, s in enumerate(streams) for i, f in enumerate(s)]
    for *_, f in sorted(keyed, key=lambda k: k[:3]):
        f()


def build(nc, x, small_w, group_w, conv_w, dt_bias, a_log, norm_w, w_out, w1, b1, w2, b2, const, where, og_dram, out):
    f32, f32r, u32 = mybir.dt.float32, mybir.dt.float32r, mybir.dt.uint32
    ALU, ACT, AX = mybir.AluOpType, mybir.ActivationFunctionType, mybir.AxisListType
    MUL, ADD, SUB = ALU.mult, ALU.add, ALU.subtract

    top = ExitStack()
    with top:
        pr = Program(nc, top)
        do, dma = pr.do, pr.dma

        def alloc(ctx, name, free, dtype=f32, side="left"):
            return ctx.enter_context(nc.sbuf_tensor(name, [P, *free], dtype, side=side))

        bank = [top.enter_context(nc.psum_tensor(f"bank{i}", [P, 512], f32)) for i in range(8)]
        bank_free = {i: [] for i in range(8)}

        ncst = const.shape[1]
        cst = alloc(top, "cst", [ncst])
        C = {n: cst[:, a:b] for n, (a, b) in where.items()}
        xn_life = ExitStack()
        xn_hi = alloc(xn_life, "xn_hi", [ND, T], f32r, side="right")
        xn_lo = alloc(xn_life, "xn_lo", [ND, T], f32r, side="right")
        rw = alloc(top, "rw", [TOP, NT])
        expert = alloc(top, "expert", [8], u32)

        def split3(e, ps, lhs, rhs, first, last):
            (lh, ll), (rh, rl) = lhs, rhs
            e.matmul(ps, lh, rh, start=first, stop=False)
            e.matmul(ps, lh, rl, start=False, stop=False)
            return e.matmul(ps, ll, rh, start=False, stop=last)

        def project(ps, lhs, rhs, n):
            def fn(e):
                for i in range(n):
                    r = split3(e, ps, lhs(i), rhs(i), i == 0, i == n - 1)
                return r
            return fn

        att = ExitStack()
        g_hi = alloc(att, "g_hi", [NT, HEADS], f32r)
        g_lo = alloc(att, "g_lo", [NT, HEADS], f32r)
        beta = alloc(att, "beta", [NT, HEADS])
        decay = alloc(att, "decay", [NT, HEADS])
        neg_decay = alloc(att, "neg_decay", [NT, HEADS])
        remain = alloc(att, "remain", [NT, HEADS])
        total = alloc(att, "total", [NT, HEADS])
        after_r = alloc(att, "after_r", [P], f32r)
        taps = alloc(att, "taps", [4 * KEY_HEADS, KW])
        half_pow = alloc(att, "half_pow", [8])
        neg_half_pow = alloc(att, "neg_half_pow", [NT])

        p1 = ExitStack()
        x_in = alloc(p1, "x_in", [NT, D])
        xn = alloc(p1, "xn", [2, D])
        stats = alloc(p1, "stats", [NT, 6])
        moments = alloc(p1, "moments", [NT, 2])
        rstd = alloc(p1, "rstd", [NT])
        sw = alloc(p1, "sw", [ND, NAB])
        sw_hi = alloc(p1, "sw_hi", [ND, NAB], f32r)
        sw_lo = alloc(p1, "sw_lo", [ND, NAB], f32r)
        ab = alloc(p1, "ab", [NT, NAB])
        hvec = {n: alloc(p1, n, [HEADS]) for n in ("dtb", "alog", "arate")}
        t_ = [alloc(p1, f"tmp{i}", [NT, HEADS]) for i in range(4)]
        g = alloc(p1, "g", [NT, HEADS])
        scores = alloc(p1, "scores", [EXPERTS])
        best = alloc(p1, "best", [8])
        expert_f = alloc(p1, "expert_f", [8])
        pick = alloc(p1, "pick", [TOP, EXPERTS])
        picked = alloc(p1, "picked", [NT, EXPERTS])
        lmax = alloc(p1, "lmax", [NT])
        lsum = alloc(p1, "lsum", [NT])

        dma([], lambda e: e.dma_start(cst[:, :], const[:, :]), "constants", "const")
        for q in range(4):
            n = NT // 4
            dma([], lambda e, q=q, n=n: e.dma_start(
                x_in[:, q * n:(q + 1) * n, :], x[0, q * n * P:(q + 1) * n * P, :].rearrange("(a p) d -> p a d", p=P)),
                ("x", q), f"x{q}")
        dma([], lambda e: e.dma_start(sw[:, :, :], small_w.rearrange("(k p) n -> p k n", p=P)), "small weights", "sw")
        dma([], lambda e: e.dma_start(hvec["dtb"][:, :], dt_bias[:].partition_broadcast(P)), "dt_bias", "dtb")
        dma([], lambda e: e.dma_start(hvec["alog"][:, :], a_log[:].partition_broadcast(P)), "A_log", "alog")
        dma([], lambda e: e.dma_start(taps[:, :, :], conv_w[:, :, :]), "conv weights", "taps")

        do("pool", [], lambda e: e.memset(half_pow[:, :], 0.5), "half_pow")
        do("pool", [], lambda e: e.memset(neg_half_pow[:, :], -0.5), "neg_half_pow")
        do("act", ["constants"], lambda e: e.copy(after_r[:, :], C["after"]), "after_r")
        do("dve", ["conv weights"], lambda e: e.tensor_scalar(taps[:, :, :], taps[:, :, :], 0.5, None, MUL), "taps")
        do("act", ["small weights"], lambda e: e.copy(sw_hi[:, :, :], sw[:, :, :]), "sw_hi")
        do("dve", ["sw_hi"], lambda e: e.tensor_tensor(sw_lo[:, :, :], sw[:, :, :], sw_hi[:, :, :].bitcast(f32), SUB), "sw_lo")

        for q in range(4):
            n = NT // 4
            for t in range(q * n, (q + 1) * n):
                do("dve", [("x", q)], lambda e, t=t: e.bn_stats(stats[:, t, :], x_in[:, t, :]), ("stats", t))
                do("dve", [("stats", t)], lambda e, t=t: e.bn_aggr(moments[:, t, :], stats[:, t, :]), ("moments", t))
            r = slice(q * n, (q + 1) * n)
            do("dve", [("moments", q * n + n - 1)],
               lambda e, r=r: e.tensor_scalar(rstd[:, r], moments[:, r, 1], LN_EPS, None, ADD), ("var", q))
            do("pool", [("var", q), "neg_half_pow"],
               lambda e, r=r: e.tensor_tensor(rstd[:, r], rstd[:, r], neg_half_pow[:, r], ALU.pow), ("rstd", q))
        for t in range(NT):
            q, b = t // (NT // 4), t % 2
            war = [("xn^T", t - 2)] if t >= 2 else []
            do("dve", [("rstd", q), *war], lambda e, t=t, b=b: e.tensor_scalar(
                xn[:, b, :], x_in[:, t, :], moments[:, t, 0:1], rstd[:, t:t + 1], SUB, MUL), ("xn", t))

            def transposes(e, b=b):
                for k in range(ND):
                    r = e.transpose(bank[b][:, k * P:(k + 1) * P], xn[:, b, k * P:(k + 1) * P], C["ident"])
                return r
            do("pe", [("xn", t), "constants", *([("xn_lo", t - 2)] if t >= 2 else [])], transposes, ("xn^T", t))
            src = bank[b][:, :].rearrange("p (k c) -> p k c", k=ND)
            dst = slice(t * P, (t + 1) * P)
            do("act", [("xn^T", t)], lambda e, s=src, d=dst: e.copy(xn_hi[:, :, d], s), ("xn_hi", t))
            do("dve", [("xn_hi", t)], lambda e, s=src, d=dst: e.tensor_tensor(
                xn_lo[:, :, d], s, xn_hi[:, :, d].bitcast(f32), SUB), ("xn_lo", t))
            ps = bank[2 + t // 8][:, (t % 8) * 64:(t % 8) * 64 + NAB]
            do("pe", [("xn_lo", t), "sw_lo"], project(
                ps, lambda i, d=dst: (xn_hi[:, i, d], xn_lo[:, i, d]),
                lambda i: (sw_hi[:, i, :], sw_lo[:, i, :]), ND), ("ab psum", t))
        for hb in range(2):
            do("act", [("ab psum", hb * 8 + 7)], lambda e, hb=hb: e.copy(
                ab[:, hb * 8:hb * 8 + 8, :],
                bank[2 + hb][:, :].rearrange("p (t c) -> p t c", t=8)[:, :, 0:NAB]), ("ab", hb))
        AB = [("ab", 0), ("ab", 1)]
        b_, a_, lg = ab[:, :, 0:HEADS], ab[:, :, HEADS:2 * HEADS], ab[:, :, 2 * HEADS:NAB]

        do("act", AB, lambda e: e.activation(beta[:, :, :], b_, ACT.Exp, scale=-1.0), "exp(-b)")
        do("dve", ["exp(-b)"], lambda e: e.tensor_scalar(beta[:, :, :], beta[:, :, :], 1.0, None, ADD), "1+exp(-b)")
        do("dve", ["1+exp(-b)"], lambda e: e.reciprocal(beta[:, :, :], beta[:, :, :]), "beta")

        def bc(v):
            return v[:, :].rearrange("p (o h) -> p o h", o=1).to_broadcast([P, NT, HEADS])
        y, w, s, acc = t_
        do("act", ["A_log"], lambda e: e.activation(hvec["arate"][:, :], hvec["alog"][:, :], ACT.Exp), "exp(A_log)")
        do("dve", [*AB, "dt_bias"], lambda e: e.tensor_tensor(y[:, :, :], a_, bc(hvec["dtb"]), ADD), "y")
        do("act", ["y"], lambda e: e.activation(w[:, :, :], y[:, :, :], ACT.Abs), "|y|")
        do("act", ["|y|"], lambda e: e.activation(w[:, :, :], w[:, :, :], ACT.Exp, scale=-1.0), "w")
        do("dve", ["w"], lambda e: e.tensor_scalar(s[:, :, :], w[:, :, :], 2.0, None, ADD), "w+2")
        do("dve", ["w+2"], lambda e: e.reciprocal(s[:, :, :], s[:, :, :]), "1/(w+2)")
        do("dve", ["1/(w+2)"], lambda e: e.tensor_tensor(s[:, :, :], w[:, :, :], s[:, :, :], MUL), "s")
        do("dve", ["s"], lambda e: e.tensor_tensor(w[:, :, :], s[:, :, :], s[:, :, :], MUL), "s^2")
        do("dve", ["s^2"], lambda e: e.tensor_scalar(acc[:, :, :], w[:, :, :], 1.0 / (2 * SERIES + 1), 1.0 / (2 * SERIES - 1), MUL, ADD), ("series", SERIES))
        for k in range(SERIES - 1, 0, -1):
            do("dve", [("series", k + 1)], lambda e: e.tensor_tensor(acc[:, :, :], acc[:, :, :], w[:, :, :], MUL), ("series*", k))
            do("dve", [("series*", k)], lambda e, k=k: e.tensor_scalar(acc[:, :, :], acc[:, :, :], 1.0 / (2 * k - 1), None, ADD), ("series", k))
        do("dve", [("series", 1)], lambda e: e.scalar_tensor_tensor(acc[:, :, :], acc[:, :, :], 2.0, s[:, :, :], MUL, MUL), "log1p")
        do("dve", ["log1p"], lambda e: e.scalar_tensor_tensor(acc[:, :, :], y[:, :, :], 0.0, acc[:, :, :], ALU.max, ADD), "softplus")
        do("dve", ["softplus", "exp(A_log)"], lambda e: e.tensor_tensor(acc[:, :, :], acc[:, :, :], bc(hvec["arate"]), MUL), "-g")
        do("dve", ["-g"], lambda e: e.tensor_scalar(g[:, :, :], acc[:, :, :], -1.0, None, MUL), "g")
        do("act", ["g"], lambda e: e.copy(g_hi[:, :, :], g[:, :, :]), "g_hi")
        do("dve", ["g_hi"], lambda e: e.tensor_tensor(g_lo[:, :, :], g[:, :, :], g_hi[:, :, :].bitcast(f32), SUB), "g_lo")
        flat = g[:, :, :].rearrange("p t h -> p (t h)")
        for n, (mask, dst) in enumerate((("upto", decay), ("after", remain), ("ones", total))):
            ps = bank[4 + n][:, 0:NT * HEADS]
            do("pe", ["g", "constants"], lambda e, m=mask, ps=ps: e.matmul(ps, C[m], flat, start=True, stop=True), ("sum", mask))
            do("act", [("sum", mask)], lambda e, ps=ps, d=dst: e.activation(
                d[:, :, :].rearrange("p t h -> p (t h)"), ps, ACT.Exp), ("exp sum", mask))
        do("dve", [("exp sum", "upto")], lambda e: e.tensor_scalar(neg_decay[:, :, :], decay[:, :, :], -1.0, None, MUL), "neg_decay")
        gates = ["neg_decay", ("exp sum", "after"), ("exp sum", "ones"), "beta", "g_lo", "after_r"]

        def score(e):
            for t in range(NT):
                r = e.matmul(bank[7][:, 0:EXPERTS], C["ones"], lg[:, t, :], start=t == 0, stop=t == NT - 1)
            return r
        do("pe", [*AB, "constants"], score, "scores psum")
        do("dve", ["scores psum"], lambda e: e.tensor_copy(scores[:, :], bank[7][:, 0:EXPERTS]), "scores")
        do("dve", ["scores"], lambda e: e.max(best[:, :], scores[:, :]), "best")
        do("dve", ["best"], lambda e: e.max_index(expert[:, :], best[:, :], scores[:, :]), "expert")
        do("dve", ["expert"], lambda e: e.tensor_copy(expert_f[:, :], expert[:, :]), "expert_f")
        for k in range(TOP):
            do("dve", ["expert_f"], lambda e, k=k: e.tensor_scalar(
                pick[:, k, :], C["iota"], expert_f[:, k:k + 1], None, ALU.is_equal), ("pick", k))
            do("dve", [("pick", k)], lambda e, k=k: e.tensor_tensor(
                picked[:, :, :], lg, pick[:, k:k + 1, :].to_broadcast([P, NT, EXPERTS]), MUL), ("picked", k))
            do("dve", [("picked", k)], lambda e, k=k: e.reduce_sum(rw[:, k, :], picked[:, :, :], AX.X), ("logit", k))
        do("dve", [("logit", 0), ("logit", 1)], lambda e: e.tensor_tensor(lmax[:, :], rw[:, 0, :], rw[:, 1, :], ALU.max), "logit max")
        for k in range(TOP):
            do("dve", ["logit max"], lambda e, k=k: e.tensor_tensor(rw[:, k, :], rw[:, k, :], lmax[:, :], SUB), ("centred", k))
            do("act", [("centred", k)], lambda e, k=k: e.activation(rw[:, k, :], rw[:, k, :], ACT.Exp), ("exp logit", k))
        do("dve", [("exp logit", 0), ("exp logit", 1)], lambda e: e.tensor_tensor(lsum[:, :], rw[:, 0, :], rw[:, 1, :], ADD), "logit sum")
        do("dve", ["logit sum"], lambda e: e.reciprocal(lsum[:, :], lsum[:, :]), "1/logit sum")
        for k in range(TOP):
            do("dve", ["1/logit sum"], lambda e, k=k: e.tensor_tensor(rw[:, k, :], rw[:, k, :], lsum[:, :], MUL), ("rw", k))
        pr.fence()
        p1.close()

        p2 = ExitStack()
        w_raw = alloc(p2, "w_raw", [2, ND, REP * HD])
        w_hi = {k: alloc(p2, f"w_hi_{k}", [ND, n], f32r) for k, (_, n) in KINDS.items()}
        w_lo = {k: alloc(p2, f"w_lo_{k}", [ND, n], f32r) for k, (_, n) in KINDS.items()}
        pre = alloc(p2, "pre", [2, SB + KW - 1])
        halo = alloc(p2, "halo", [4, KW - 1])
        conv = alloc(p2, "conv", [2, SB])
        th = alloc(p2, "th", [2, SB])
        kqT = alloc(p2, "kqT", [NBUF, CPS, 2, P])
        vT = alloc(p2, "vT", [2, SB])
        square = alloc(p2, "square", [SB])
        k_tok = alloc(p2, "k_tok", [NBUF, CPS, HD])
        v_tok = alloc(p2, "v_tok", [NBUF, CPS, REP, HD])
        z_gate = alloc(p2, "z_gate", [NBUF, CPS, REP, HD])
        norms = alloc(p2, "norms", [NBUF, 2, CPS])
        k_len = alloc(p2, "k_len", [NBUF, CPS])
        inv_n = alloc(p2, "inv_n", [NBUF, CPS])
        q_eps = alloc(p2, "q_eps", [NBUF, CPS])
        cw = alloc(p2, "cw", [NBUF, CPS, REP])
        gm_hi = alloc(p2, "gm_hi", [NHC, P], f32r)
        gm_lo = alloc(p2, "gm_lo", [NHC, P], f32r)
        E = alloc(p2, "E", [NHC, P])
        kq = alloc(p2, "kq", [QUAD, 2, P])
        PT = alloc(p2, "PT", [2, NHC, P])
        Cn = alloc(p2, "Cn", [NHC, P])
        X = alloc(p2, "X", [NHC, P])
        XT = alloc(p2, "XT", [2, NHC, P])
        Y = alloc(p2, "Y", [NHC, P // 2])
        S = alloc(p2, "S", [REP, HD])
        R = alloc(p2, "R", [REP, HD])
        U = alloc(p2, "U", [REP, HD])
        UR = alloc(p2, "UR", [REP, HD])
        QS = alloc(p2, "QS", [REP, HD])
        O = alloc(p2, "O", [2, QUAD, REP, HD])
        squares = alloc(p2, "squares", [NHC, HD])
        ms = alloc(p2, "ms", [2, NHC])
        og = alloc(p2, "og", [2, QUAD, REP, HD])

        ring = [0]

        def bulk():
            ring[0] += 1
            return ring[0] % 2

        def load_group(gr):
            steps = []
            for n, (kind, (at, width)) in enumerate(KINDS.items()):
                slot = (gr * len(KINDS) + n) % 2
                prev = (gr * len(KINDS) + n) - 2

                def load(kind=kind, at=at, width=width, slot=slot, prev=prev, n=n):
                    war = [("w lo", prev)] if prev >= 0 else []
                    dma(war, lambda e: e.dma_start(w_raw[:, slot, :, 0:width], group_w[gr, :, :, at:at + width]),
                        ("w raw", gr, kind), f"w{slot}")

                def split(kind=kind, width=width, slot=slot, n=n):
                    raw = w_raw[:, slot, :, 0:width]
                    war = [("last projection", gr - 1, kind)] if gr else []
                    do("act", [("w raw", gr, kind), *war], lambda e: e.copy(w_hi[kind][:, :, :], raw), ("w hi", gr, kind))
                    do("pool", [("w hi", gr, kind)], lambda e: e.tensor_tensor(
                        w_lo[kind][:, :, :], raw, w_hi[kind][:, :, :].bitcast(f32), SUB), ("w lo", gr, kind))
                    pr.done["w lo", gr * len(KINDS) + n] = pr.done["w lo", gr, kind]
                steps += [load, split]
            return steps

        def stage_a(u):
            gr, sb, ub = u // NSB, u % NSB, u % NBUF
            toks = slice(sb * SB, (sb + 1) * SB)
            last = sb == NSB - 1
            conv_slot = {"k": 0, "q": 1, "v0": 0, "v1": 1}
            tile_of = {"k": 0, "q": 1, "v0": 2, "v1": 3}

            def proj(kind):
                b = bulk()
                do("pe", [("w lo", gr, kind), *bank_free[b]], project(
                    bank[b][:, :], lambda i: (w_hi[kind][:, i, :], w_lo[kind][:, i, :]),
                    lambda i: (xn_hi[:, i, toks], xn_lo[:, i, toks]), ND), ("proj", u, kind))
                if last:
                    pr.done["last projection", gr, kind] = pr.done["proj", u, kind]
                s = conv_slot[kind]
                t = tile_of[kind]
                war = [("history", s)] if ("history", s) in pr.done else []
                do("act", [("proj", u, kind), *war], lambda e: e.copy(pre[:, s, KW - 1:], bank[b][:, :]), ("pre", u, kind))
                bank_free[b] = [("pre", u, kind)]
                if sb == 0:
                    do("dve", war, lambda e: e.memset(pre[:, s, 0:KW - 1], 0.0), ("past", u, kind))
                else:
                    do("dve", [("history of", t)], lambda e: e.tensor_copy(pre[:, s, 0:KW - 1], halo[:, t, :]), ("past", u, kind))
                wt = taps[:, 4 * gr + t, :]
                war = [("silu", s)] if ("silu", s) in pr.done else []
                do("dve", [("pre", u, kind), ("past", u, kind), *war], lambda e: e.tensor_scalar(
                    conv[:, s, :], pre[:, s, 0:SB], wt[:, 0:1], None, MUL), ("tap", u, kind, 0))
                for j in range(1, KW):
                    do("dve", [("tap", u, kind, j - 1)], lambda e, j=j: e.scalar_tensor_tensor(
                        conv[:, s, :], pre[:, s, j:j + SB], wt[:, j:j + 1], conv[:, s, :], MUL, ADD), ("tap", u, kind, j))
                do("dve", [], lambda e: e.tensor_copy(halo[:, t, :], pre[:, s, SB:SB + KW - 1]), ("history of", t))
                pr.done["history", s] = pr.done["history of", t]
                do("act", [("tap", u, kind, KW - 1)], lambda e: e.activation(th[:, s, :], conv[:, s, :], ACT.Tanh), ("tanh", u, kind))
                if kind in "kq":
                    dst = kqT[:, ub, :, "kq".index(kind), :]
                    war = [("C done", 2 * (u - NBUF) + 1), ("kq psum", 2 * (u - NBUF) + 1)] if u >= NBUF else []
                    src = lambda a: a.rearrange("p (c t) -> p c t", c=CPS)
                else:
                    dst = vT[:, s, :]
                    war = [("v transposed", s)] if ("v transposed", s) in pr.done else []
                    src = lambda a: a
                do("dve", [("tanh", u, kind), *war], lambda e: e.scalar_tensor_tensor(
                    dst, src(th[:, s, :]), 1.0, src(conv[:, s, :]), ADD, MUL), ("act", u, kind))
                pr.done["silu", s] = pr.done["act", u, kind]

            def norm(kind):
                n = "kq".index(kind)
                war = [("square read",)] if ("square read",) in pr.done else []
                do("act", [("act", u, kind), *war], lambda e: e.activation(
                    square[:, :].rearrange("p (c t) -> p c t", c=CPS), kqT[:, ub, :, n, :], ACT.Square), ("square", u, kind))
                b = bulk()

                def sums(e):
                    for c in range(CPS):
                        r = e.matmul(bank[b][:, c:c + 1], square[:, c * P:(c + 1) * P], C["ones"][:, 0:1], start=True, stop=True)
                    return r
                do("pe", [("square", u, kind), *bank_free[b]], sums, ("norm psum", u, kind))
                pr.done["square read",] = pr.done["norm psum", u, kind]
                war = [("D done", 2 * (u - NBUF) + 1), ("v_tok", u - NBUF, 1), ("v_tok", u - NBUF, 0)] if u >= NBUF else []
                do("dve", [("norm psum", u, kind), *war], lambda e: e.tensor_scalar(
                    norms[:, ub, n, :], bank[b][:, 0:CPS], L2_EPS, None, ADD), ("norm", u, kind))
                bank_free[b] = [("norm", u, kind)]
                if kind == "k":
                    do("pool", [("norm", u, "k")], lambda e: e.tensor_tensor(
                        k_len[:, ub, :], norms[:, ub, 0, :], half_pow[:, 0:CPS], ALU.pow), ("k_len", u))
                    do("dve", [("norm", u, "k")], lambda e: e.reciprocal(inv_n[:, ub, :], norms[:, ub, 0, :]), ("inv_n", u))
                    h0 = REP * gr
                    do("dve", [("inv_n", u)], lambda e: e.tensor_tensor(
                        cw[:, ub, :, :], beta[:, sb * CPS:(sb + 1) * CPS, h0:h0 + REP],
                        inv_n[:, ub, :].rearrange("p (c o) -> p c o", o=1).to_broadcast([P, CPS, REP]), MUL), ("c", u))
                else:
                    do("dve", [("norm", u, "q")], lambda e: e.tensor_scalar(
                        q_eps[:, ub, :], norms[:, ub, 1, :], 4 * RMS_EPS * HD, None, MUL), ("q_eps", u))

            def tokens_k():
                b = bulk()

                def fn(e):
                    for c in range(CPS):
                        r = e.transpose(bank[b][:, c * P:(c + 1) * P], kqT[:, ub, c, 0, :], C["ident"])
                    return r
                do("pe", [("act", u, "k"), *bank_free[b]], fn, ("k^T^T", u))
                war = [("C done", 2 * (u - NBUF) + 1)] if u >= NBUF else []
                do("act", [("k^T^T", u), *war], lambda e: e.copy(
                    k_tok[:, ub, :, :], bank[b][:, :].rearrange("p (c d) -> p c d", c=CPS)), ("k_tok", u))
                bank_free[b] = [("k_tok", u)]

            def tokens_v(h):
                b = bulk()
                s = conv_slot[f"v{h}"]

                def fn(e):
                    for c in range(CPS):
                        r = e.transpose(bank[b][:, c * P:(c + 1) * P], vT[:, s, c * P:(c + 1) * P], C["ident"])
                    return r
                do("pe", [("act", u, f"v{h}"), *bank_free[b]], fn, ("v^T^T", u, h))
                pr.done["v transposed", s] = pr.done["v^T^T", u, h]
                war = [("C done", 2 * (u - NBUF) + 1)] if u >= NBUF else []

                def scaled(e):
                    for c in range(CPS):
                        r = e.mul(v_tok[:, ub, c, h, :], bank[b][:, c * P:(c + 1) * P], k_len[:, ub, c:c + 1])
                    return r
                do("act", [("v^T^T", u, h), ("k_len", u), *war], scaled, ("v_tok", u, h))
                bank_free[b] = [("v_tok", u, h)]

            def z(half):
                b = bulk()

                def fn(e):
                    for c in range(2):
                        t = slice(sb * SB + (2 * half + c) * P, sb * SB + (2 * half + c + 1) * P)
                        r = project(bank[b][:, c * REP * HD:(c + 1) * REP * HD],
                                    lambda i: (xn_hi[:, i, t], xn_lo[:, i, t]),
                                    lambda i: (w_hi["z"][:, i, :], w_lo["z"][:, i, :]), ND)(e)
                    return r
                do("pe", [("w lo", gr, "z"), *bank_free[b]], fn, ("z psum", u, half))
                if last:
                    pr.done["last projection", gr, "z"] = pr.done["z psum", u, half]
                dst = z_gate[:, ub, 2 * half:2 * half + 2, :, :].rearrange("p c h d -> p (c h d)")
                war = [("D done", 2 * (u - NBUF) + half)] if u >= NBUF else []
                do("act", [("z psum", u, half), *war], lambda e: e.activation(dst, bank[b][:, :], ACT.Tanh, scale=0.5), ("z tanh", u, half))
                do("dve", [("z tanh", u, half)], lambda e: e.scalar_tensor_tensor(
                    dst, dst, 1.0, bank[b][:, :], ADD, MUL), ("z_gate", u, half))
                bank_free[b] = [("z_gate", u, half)]

            return [lambda: proj("k"), lambda: proj("q"), lambda: proj("v0"), lambda: norm("k"), tokens_k,
                    lambda: proj("v1"), lambda: norm("q"), lambda: z(0), lambda: tokens_v(0), lambda: z(1),
                    lambda: tokens_v(1)]

        def stage_b(qd):
            u, half, pb = qd // 2, qd % 2, qd % 2
            gr, sb, ub = u // NSB, u % NSB, u % NBUF
            cs = [half * QUAD + i for i in range(QUAD)]
            c0, h0 = sb * CPS + cs[0], REP * gr
            B_D, B_KQ, B_Y, B_Z = 2, 3, 4, 5
            steps = []
            step = steps.append

            def rates(src):
                return src[:, c0:c0 + QUAD, h0:h0 + REP].rearrange("p c (h o) -> p c h o", o=1).to_broadcast([P, QUAD, REP, P])

            def masked():
                for name, dst, src in (("gm_hi", gm_hi, g_hi), ("gm_lo", gm_lo, g_lo)):
                    war = [("D psum", qd - 1)] if qd else []
                    do("pool", [*gates, *war], lambda e, dst=dst, src=src: e.tensor_tensor(
                        dst[:, :, :].rearrange("p (c h) t -> p c h t", c=QUAD),
                        C["upto"].rearrange("p (a b t) -> p a b t", a=1, b=1).to_broadcast([P, QUAD, REP, P]),
                        rates(src.bitcast(f32)), MUL), (name, qd))
            step(masked)

            def decays():
                def fn(e):
                    e.matmul(bank[B_D][:, :], after_r[:, :], gm_hi[:, :, :].rearrange("p a t -> p (a t)"), start=True, stop=False)
                    return e.matmul(bank[B_D][:, :], after_r[:, :], gm_lo[:, :, :].rearrange("p a t -> p (a t)"), start=False, stop=True)
                do("pe", [("gm_lo", qd), *bank_free[B_D]], fn, ("D psum", qd))
                war = [("PT", qd - 1), ("Cn", qd - 1)] if qd else []
                do("act", [("D psum", qd), *war], lambda e: e.activation(
                    E[:, :, :].rearrange("p a t -> p (a t)"), bank[B_D][:, :], ACT.Exp), ("E", qd))
                bank_free[B_D] = [("E", qd)]

                def fn(e):
                    for i, c in enumerate(cs):
                        r = e.matmul(bank[B_KQ][:, i * 2 * P:(i + 1) * 2 * P], kqT[:, ub, c, 0, :],
                                     kqT[:, ub, c, :, :].rearrange("p a t -> p (a t)"), start=True, stop=True)
                    return r
                do("pe", [("act", u, "k"), ("act", u, "q"), *bank_free[B_KQ]], fn, ("kq psum", qd))
                do("dve", [("kq psum", qd), *war], lambda e: e.tensor_tensor(
                    kq[:, :, :, :].rearrange("p c a t -> p c (a t)"), bank[B_KQ][:, :].rearrange("p (c a) -> p c a", c=QUAD),
                    C["kq"].rearrange("p (o a) -> p o a", o=1).to_broadcast([P, QUAD, 2 * P]), MUL), ("kq", qd))
                bank_free[B_KQ] = [("kq", qd)]
            step(decays)

            def matrices():
                def fn(e):
                    for i, c in enumerate(cs):
                        for h in range(REP):
                            r = e.scalar_tensor_tensor(Cn[:, REP * i + h, :], E[:, REP * i + h, :], cw[:, ub, c, h:h + 1],
                                                       kq[:, i, 0, :], MUL, MUL)
                    return r
                war = [("Y psum", qd - 1, LEVELS - 1)] if qd else []
                do("dve", [("E", qd), ("kq", qd), ("c", u), *war], fn, ("Cn", qd))
                war = [("C done", qd - 2)] if qd >= 2 else []

                def fn(e):
                    for i in range(QUAD):
                        r = e.tensor_tensor(PT[:, pb, REP * i:REP * i + REP, :], E[:, REP * i:REP * i + REP, :],
                                            kq[:, i, 1:2, :].to_broadcast([P, REP, P]), MUL)
                    return r
                do("pool", [("E", qd), ("kq", qd), *war], fn, ("PT", qd))
                do("dve", [("Cn", qd), *war], lambda e: e.tensor_tensor(
                    XT[:, pb, :, :], Cn[:, :, :], C["pairs"].rearrange("p (o t) -> p o t", o=1).to_broadcast([P, NHC, P]), MUL),
                   ("pairs", qd))
                do("dve", [("pairs", qd)], lambda e: e.tensor_tensor(
                    XT[:, pb, :, :], XT[:, pb, :, :], C["ident"].rearrange("p (o t) -> p o t", o=1).to_broadcast([P, NHC, P]), ADD),
                   ("XT", qd, 0))
            step(matrices)

            def flip(src, dst, need, name, war=()):
                def fn(e):
                    for a in range(NHC):
                        r = e.transpose(bank[B_D][:, a * P:(a + 1) * P], src[:, a, :], C["ident"])
                    return r
                do("pe", [need, *bank_free[B_D]], fn, (name, "psum"))
                do("act", [(name, "psum"), *war], lambda e: e.copy(dst.rearrange("p a t -> p (a t)"), bank[B_D][:, :]), name)
                bank_free[B_D] = [name]

            step(lambda: flip(XT[:, pb, :, :], X[:, :, :], ("XT", qd, 0), ("X", qd, 0)))
            for lev in range(1, LEVELS):
                s = 1 << lev
                nb = P // (2 * s)

                def up(lev=lev, s=s, nb=nb):
                    def halves(a):
                        return a.rearrange("p (b i s) -> p b i s", b=nb, i=2)[:, :, 0, :]

                    def fn(e):
                        for a in range(NHC):
                            r = e.matmul(bank[B_Y][:, a * P // 2:(a + 1) * P // 2], Cn[:, a, :], halves(X[:, a, :]), start=True, stop=True)
                        return r
                    do("pe", [("X", qd, lev - 1), ("Cn", qd), *bank_free[B_Y]], fn, ("Y psum", qd, lev))
                    war = [("Z psum", qd, lev - 1)] if lev > 1 else ([("Z psum", qd - 1, LEVELS - 1)] if qd else [])
                    do("dve", [("Y psum", qd, lev), *war], lambda e: e.tensor_tensor(
                        Y[:, :, :], bank[B_Y][:, 0:NHC * P // 2].rearrange("p (a m) -> p a m", a=NHC),
                        C[f"rows{lev}"].rearrange("p (o m) -> p o m", o=1).to_broadcast([P, NHC, P // 2]), MUL), ("Y", qd, lev))
                    bank_free[B_Y] = [("Y", qd, lev)]

                def join(lev=lev, s=s, nb=nb):
                    def fn(e):
                        for a in range(NHC):
                            r = e.matmul(bank[B_Z][:, a * P // 2:(a + 1) * P // 2], XT[:, pb, a, :], Y[:, a, :], start=True, stop=True)
                        return r
                    do("pe", [("Y", qd, lev), ("XT", qd, lev - 1), *bank_free[B_Z]], fn, ("Z psum", qd, lev))
                    view = X[:, :, :].rearrange("p a (b i s) -> p (a b) i s", b=nb, i=2)[:, :, 0, :]
                    z = bank[B_Z][:, 0:NHC * P // 2].rearrange("p (ab s) -> p ab s", s=s)
                    do("dve", [("Z psum", qd, lev)], lambda e: e.tensor_tensor(view, view, z, ADD), ("X", qd, lev))
                    bank_free[B_Z] = [("X", qd, lev)]
                step(up)
                step(join)
                step(lambda lev=lev: flip(X[:, :, :], XT[:, pb, :, :], ("X", qd, lev), ("XT", qd, lev)))
            return steps

        def stage_c(qd):
            u, half, pb = qd // 2, qd % 2, qd % 2
            gr, sb, ub = u // NSB, u % NSB, u % NBUF
            B_K, B_Q = 6, 7
            steps = []
            step = steps.append
            if sb == 0 and half == 0:
                war = [("state psum", qd - 1, QUAD - 1), ("S", qd - 1, QUAD - 1), ("queries", qd - 1, QUAD - 1)] if qd else []
                step(lambda: do("dve", war, lambda e: e.memset(S[:, :, :], 0.0), ("S", qd, -1)))
            else:
                step(lambda: pr.done.__setitem__(("S", qd, -1), pr.done["S", qd - 1, QUAD - 1]))
            for i in range(QUAD):
                c = half * QUAD + i
                cg, h0 = sb * CPS + c, REP * gr
                before = (qd, i - 1) if i else ((qd - 1, QUAD - 1) if qd else None)

                def recall(i=i, c=c, cg=cg, before=before):
                    Sf = S[:, :, :].rearrange("p h d -> p (h d)")
                    do("pe", [("S", qd, i - 1), *bank_free[B_K]], lambda e: e.matmul(
                        bank[B_K][:, 0:REP * HD], kqT[:, ub, c, 0, :], Sf, start=True, stop=True), ("keys", qd, i))
                    do("pe", [*bank_free[B_Q]], lambda e: e.matmul(
                        bank[B_Q][:, 0:REP * HD], kqT[:, ub, c, 1, :], Sf, start=True, stop=True), ("queries", qd, i))

                    def fn(e):
                        for h in range(REP):
                            r = e.scalar_tensor_tensor(R[:, h, :], bank[B_K][:, h * HD:(h + 1) * HD], neg_decay[:, cg, h0 + h:h0 + h + 1],
                                                       v_tok[:, ub, c, h, :], MUL, ADD)
                        return r
                    war = [("W psum", *before)] if before else []
                    do("dve", [("keys", qd, i), ("v_tok", u, 0), ("v_tok", u, 1), *war], fn, ("R", qd, i))

                    def fn(e):
                        for h in range(REP):
                            r = e.mul(QS[:, h, :], bank[B_Q][:, h * HD:(h + 1) * HD], decay[:, cg, h0 + h:h0 + h + 1])
                        return r
                    war = [("O", *before)] if before else []
                    do("act", [("queries", qd, i), *war], fn, ("QS", qd, i))
                step(recall)

                def solve(i=i, c=c, cg=cg, before=before):
                    def fn(e):
                        for h in range(REP):
                            r = e.matmul(bank[B_K][:, (REP + h) * HD:(REP + h + 1) * HD], XT[:, pb, REP * i + h, :], R[:, h, :], start=True, stop=True)
                        return r
                    do("pe", [("R", qd, i), ("XT", qd, LEVELS - 1)], fn, ("W psum", qd, i))

                    def fn(e):
                        for h in range(REP):
                            r = e.mul(U[:, h, :], bank[B_K][:, (REP + h) * HD:(REP + h + 1) * HD], cw[:, ub, c, h:h + 1])
                        return r
                    war = [("O psum", *before), ("UR", *before)] if before else []
                    do("act", [("W psum", qd, i), *war], fn, ("U", qd, i))

                    def fn(e):
                        for h in range(REP):
                            r = e.tensor_scalar(UR[:, h, :], U[:, h, :], remain[:, cg, h0 + h:h0 + h + 1], None, MUL)
                        return r
                    war = [("state psum", *before)] if before else []
                    do("dve", [("U", qd, i), *war], fn, ("UR", qd, i))
                step(solve)

                def update(i=i, c=c, cg=cg):
                    def fn(e):
                        for h in range(REP):
                            r = e.matmul(bank[B_Q][:, (REP + h) * HD:(REP + h + 1) * HD], PT[:, pb, REP * i + h, :], U[:, h, :], start=True, stop=True)
                        return r
                    do("pe", [("U", qd, i), ("PT", qd), ("QS", qd, i)], fn, ("O psum", qd, i))
                    do("pe", [("UR", qd, i), ("k_tok", u)], lambda e: e.matmul(
                        bank[B_K][:, 0:REP * HD], k_tok[:, ub, c, :], UR[:, :, :].rearrange("p h d -> p (h d)"), start=True, stop=True),
                        ("state psum", qd, i))

                    def fn(e):
                        for h in range(REP):
                            r = e.scalar_tensor_tensor(S[:, h, :], S[:, h, :], total[:, cg, h0 + h:h0 + h + 1],
                                                       bank[B_K][:, h * HD:(h + 1) * HD], MUL, ADD)
                        return r
                    do("dve", [("state psum", qd, i), ("queries", qd, i)], fn, ("S", qd, i))
                    bank_free[B_K] = [("S", qd, i)]
                    war = [("og", qd - 2), ("ms", qd - 2)] if qd >= 2 else []
                    do("dve", [("O psum", qd, i), ("QS", qd, i), *war], lambda e: e.tensor_tensor(
                        O[:, pb, i, :, :].rearrange("p h d -> p (h d)"), QS[:, :, :].rearrange("p h d -> p (h d)"),
                        bank[B_Q][:, REP * HD:2 * REP * HD], ADD), ("O", qd, i))
                    bank_free[B_Q] = [("O", qd, i)]
                    if i == QUAD - 1:
                        pr.done["C done", qd] = pr.done["state psum", qd, i]
                step(update)
            return steps

        def stage_d(qd):
            u, half, pb = qd // 2, qd % 2, qd % 2
            gr, sb, ub = u // NSB, u % NSB, u % NBUF

            def power():
                def fn(e):
                    for i in range(QUAD):
                        for h in range(REP):
                            r = e.activation(squares[:, REP * i + h, :], O[:, pb, i, h, :], ACT.Square, accum_out=ms[:, pb, REP * i + h:REP * i + h + 1])
                    return r
                do("act", [("O", qd, 0), ("O", qd, 1), *([("ms", qd - 1)] if qd else []), *([("og", qd - 2)] if qd >= 2 else [])], fn, ("ms", qd))
                m3 = ms[:, pb, :].rearrange("p (c h) -> p c h", c=QUAD)
                qe = q_eps[:, ub, half * QUAD:(half + 1) * QUAD].rearrange("p (c o) -> p c o", o=1).to_broadcast([P, QUAD, REP])
                do("dve", [("ms", qd), ("q_eps", u)], lambda e: e.scalar_tensor_tensor(m3, m3, 4.0 / HD, qe, MUL, ADD), ("ms+", qd))
                do("pool", [("ms+", qd)], lambda e: e.tensor_tensor(ms[:, pb, :], ms[:, pb, :], neg_half_pow[:, 0:NHC], ALU.pow), ("factor", qd))

            def gate():
                def fn(e):
                    for i in range(QUAD):
                        for h in range(REP):
                            r = e.scalar_tensor_tensor(og[:, pb, i, h, :], O[:, pb, i, h, :], ms[:, pb, REP * i + h:REP * i + h + 1],
                                                       z_gate[:, ub, half * QUAD + i, h, :], MUL, MUL)
                    return r
                do("dve", [("factor", qd), ("z_gate", u, half), *([("og stored", qd - 2)] if qd >= 2 else [])], fn, ("og", qd))
                pr.done["D done", qd] = pr.done["og", qd]
                t0 = sb * SB + half * QUAD * P
                dst = og_dram[t0:t0 + QUAD * P, REP * gr * HD:REP * (gr + 1) * HD].rearrange("(c p) d -> p c d", p=P)
                dma([("og", qd)], lambda e: e.dma_start(dst, og[:, pb, :, :, :].rearrange("p c h d -> p c (h d)")),
                    ("og stored", qd), f"og{pb}")
            return [power, gate]

        NU, NQ = KEY_HEADS * NSB, KEY_HEADS * NSB * 2
        for f in load_group(0) + stage_a(0):
            f()
        a_steps = []
        for slot in range(-1, NQ + 1):
            if slot % 2 == 1:
                u = (slot + 3) // 2
                full = stage_a(u) if u < NU else []
                if full and u % NSB == 0:
                    full = [*load_group(u // NSB), *full]
                n = len(full) // 2
                first, second = full[:n], full[n:]
            now = first if slot % 2 == 1 else second
            merge(*[s for s in (
                now,
                stage_b(slot + 1) if slot + 1 < NQ else [],
                stage_c(slot) if 0 <= slot < NQ else [],
                stage_d(slot - 1) if 0 <= slot - 1 < NQ else []) if s])
        pr.fence()
        p2.close()
        att.close()

        gate_acc = alloc(top, "gate_acc", [NT, D])
        p3 = ExitStack()
        FP = 8
        FW = DFF // FP
        NF = FW // P
        raw = alloc(p3, "ffn_raw", [2, ND * FW])
        fw = {(n, s): alloc(p3, f"ffn_w{n}_{s}", [2, ND * FW], f32r) for n in (1, 2) for s in ("hi", "lo")}

        def rows(a, m):
            return a.rearrange("p (k n) -> p k n", k=ND if m == 1 else NF)
        bias1 = alloc(p3, "bias1", [TOP, DFF // P])
        bias2 = alloc(p3, "bias2", [TOP, D])
        hid = alloc(p3, "hid", [2, SB])
        h_hi = alloc(p3, "h_hi", [2, NF, SB], f32r)
        h_lo = alloc(p3, "h_lo", [2, NF, SB], f32r)
        th3 = alloc(p3, "th3", [D])
        index = {}

        def load_index(e):
            index.update({k: e.value_load(expert[0:1, k:k + 1], min_val=0, max_val=EXPERTS - 1) for k in range(TOP)})
        pr.wait("sp", "expert")
        pr.queue["sp"].append(load_index)
        for k in range(TOP):
            dma([], lambda e, k=k: e.dma_start(bias1[:, k, :], b1[bass.ds(index[k], 1), :, :].rearrange("e p n -> p (e n)")), ("bias1", k), f"b1{k}")
            dma([], lambda e, k=k: e.dma_start(bias2[:, k, :], b2[bass.ds(index[k], 1), :].rearrange("e n -> (e n)").partition_broadcast(P)),
                ("bias2", k), f"b2{k}")
        parts = [(k, f) for k in range(TOP) for f in range(FP)]
        n_raw = [0]

        def load_part(n):
            k, f = parts[n]
            steps = []
            for m in (1, 2):
                slot = (2 * n + m - 1) % 2

                def load(m=m, slot=slot):
                    i = 2 * n + m - 1
                    war = [("ffn lo", i - 2)] if i >= 2 else []
                    if m == 1:
                        src = lambda: w1[bass.ds(index[k], 1), :, f * FW:(f + 1) * FW].rearrange("e (a p) n -> p (e a) n", p=P)
                    else:
                        src = lambda: w2[bass.ds(index[k], 1), f * FW:(f + 1) * FW, :].rearrange("e (a p) n -> p (e a) n", p=P)
                    dma(war, lambda e: e.dma_start(rows(raw[:, slot, :], m), src()), ("ffn raw", i), f"ffn{slot}")

                def split(m=m, slot=slot):
                    i = 2 * n + m - 1
                    war = [("part done", n - 2, m)] if n >= 2 else []
                    hi, lo = fw[m, "hi"][:, n % 2, :], fw[m, "lo"][:, n % 2, :]
                    do("act", [("ffn raw", i), *war], lambda e: e.copy(hi, raw[:, slot, :]), ("ffn hi", i))
                    do("pool", [("ffn hi", i)], lambda e: e.tensor_tensor(lo, raw[:, slot, :], hi.bitcast(f32), SUB), ("ffn lo", i))
                steps += [load, split]
            return steps

        for t in range(NT):
            do("dve", [("bias2", 0), ("rw", 0)], lambda e, t=t: e.tensor_scalar(
                gate_acc[:, t, :], bias2[:, 0, :], rw[:, 0, t:t + 1], None, MUL), ("bias a", t))
            do("dve", [("bias2", 1), ("rw", 1), ("bias a", t)], lambda e, t=t: e.scalar_tensor_tensor(
                gate_acc[:, t, :], bias2[:, 1, :], rw[:, 1, t:t + 1], gate_acc[:, t, :], MUL, ADD), ("acc", t))
        for i in range(8):
            bank_free[i] = []

        def hidden(n, sb):
            k, f = parts[n]
            hb = (n * NSB + sb) % 2
            toks = slice(sb * SB, (sb + 1) * SB)
            steps = []
            for ft in range(NF):
                def tile(ft=ft):
                    b = (NF * sb + ft) % 4
                    fs = slice(ft * P, (ft + 1) * P)
                    do("pe", [("ffn lo", 2 * n), *bank_free[b]], project(
                        bank[b][:, :], lambda i: (rows(fw[1, "hi"][:, n % 2, :], 1)[:, i, fs], rows(fw[1, "lo"][:, n % 2, :], 1)[:, i, fs]),
                        lambda i: (xn_hi[:, i, toks], xn_lo[:, i, toks]), ND), ("hidden psum", n, sb, ft))
                    if sb == NSB - 1:
                        pr.done["part done", n, 1] = pr.done["hidden psum", n, sb, ft]
                    war = [("h_lo", ft % 2)] if ("h_lo", ft % 2) in pr.done else []
                    do("act", [("hidden psum", n, sb, ft), ("bias1", k), *war], lambda e: e.activation(
                        hid[:, ft % 2, :], bank[b][:, :], ACT.Gelu_apprx_tanh, bias=bias1[:, k, f * NF + ft:f * NF + ft + 1]),
                       ("gelu", n, sb, ft))
                    bank_free[b] = [("gelu", n, sb, ft)]
                    war = [("y read", hb)] if ("y read", hb) in pr.done else []
                    do("act", [("gelu", n, sb, ft), *war], lambda e: e.copy(h_hi[:, hb, ft, :], hid[:, ft % 2, :]), ("h_hi", n, sb, ft))
                    do("dve", [("h_hi", n, sb, ft)], lambda e: e.tensor_tensor(
                        h_lo[:, hb, ft, :], hid[:, ft % 2, :], h_hi[:, hb, ft, :].bitcast(f32), SUB), ("h split", n, sb, ft))
                    pr.done["h_lo", ft % 2] = pr.done["h split", n, sb, ft]
                steps.append(tile)
            return steps

        def down(n, sb):
            k, f = parts[n]
            hb = (n * NSB + sb) % 2
            steps = []
            for c in range(CPS):
                def tile(c=c):
                    b = 4 + c % 4
                    t = sb * CPS + c
                    ts = slice(c * P, (c + 1) * P)
                    do("pe", [("ffn lo", 2 * n + 1), ("h split", n, sb, NF - 1), *bank_free[b]], project(
                        bank[b][:, :], lambda i: (h_hi[:, hb, i, ts], h_lo[:, hb, i, ts]),
                        lambda i: (rows(fw[2, "hi"][:, n % 2, :], 2)[:, i, :], rows(fw[2, "lo"][:, n % 2, :], 2)[:, i, :]), NF), ("y psum", n, t))
                    pr.done["y read", hb] = pr.done["y psum", n, t]
                    if sb == NSB - 1:
                        pr.done["part done", n, 2] = pr.done["y psum", n, t]
                    do("dve", [("y psum", n, t), ("acc", t), ("rw", k)], lambda e: e.scalar_tensor_tensor(
                        gate_acc[:, t, :], bank[b][:, :], rw[:, k, t:t + 1], gate_acc[:, t, :], MUL, ADD), ("acc", t))
                    bank_free[b] = [("acc", t)]
                    if n == len(parts) - 1:
                        war = [("gate", t - 1)] if t else []
                        do("act", [("acc", t), *war], lambda e: e.activation(th3[:, :], gate_acc[:, t, :], ACT.Tanh, scale=0.5), ("gate tanh", t))
                        do("dve", [("gate tanh", t)], lambda e: e.scalar_tensor_tensor(
                            gate_acc[:, t, :], th3[:, :], 1.0, gate_acc[:, t, :], ADD, MUL), ("gate", t))
                steps.append(tile)
            return steps

        for f in load_part(0):
            f()
        blocks = [(n, sb) for n in range(len(parts)) for sb in range(NSB)]
        for f in hidden(*blocks[0]):
            f()
        for m, (n, sb) in enumerate(blocks):
            pre_load = load_part(n + 1) if sb == 1 and n + 1 < len(parts) else []
            merge(*[s for s in (hidden(*blocks[m + 1]) if m + 1 < len(blocks) else [], down(n, sb), pre_load) if s])
        pr.fence()
        p3.close()
        xn_life.close()

        p4 = ExitStack()
        WO = 4
        wo_raw = alloc(p4, "wo_raw", [2, HEADS // WO, D])
        wo_hi = alloc(p4, "wo_hi", [HEADS, D], f32r)
        wo_lo = alloc(p4, "wo_lo", [HEADS, D], f32r)
        nw = alloc(p4, "nw", [1])
        og_in = alloc(p4, "og_in", [2, HEADS * HD])
        x_res = alloc(p4, "x_res", [2, D])
        ogT_hi = alloc(p4, "ogT_hi", [2, HEADS, P], f32r)
        ogT_lo = alloc(p4, "ogT_lo", [2, HEADS, P], f32r)
        y_out = alloc(p4, "y_out", [2, D])
        for i in range(8):
            bank_free[i] = []
        dma([], lambda e: e.dma_start(nw[:, :], norm_w.rearrange("(p o) -> p o", o=1)), "norm weight", "nw")
        dma([], lambda e: e.dma_start(og_in[:, 0, :], og_dram[0:P, :]), ("og in", 0), "ogin0")
        for m in range(WO):
            hs = slice(m * HEADS // WO, (m + 1) * HEADS // WO)
            r = wo_raw[:, m % 2, :, :]
            dma([("wo lo", m - 2)] if m >= 2 else [], lambda e, hs=hs, r=r: e.dma_start(
                r, w_out[hs.start * HD:hs.stop * HD, :].rearrange("(a p) n -> p a n", p=P)), ("wo raw", m), f"wo{m % 2}")
            do("dve", [("wo raw", m), "norm weight"], lambda e, r=r: e.tensor_scalar(r, r, nw[:, 0:1], None, MUL), ("wo scaled", m))
            do("act", [("wo scaled", m)], lambda e, r=r, hs=hs: e.copy(wo_hi[:, hs, :], r), ("wo hi", m))
            do("pool", [("wo hi", m)], lambda e, r=r, hs=hs: e.tensor_tensor(wo_lo[:, hs, :], r, wo_hi[:, hs, :].bitcast(f32), SUB), ("wo lo", m))

        def turn(t):
            tb = t % 2
            steps = []
            if t:
                def load():
                    war = [("og^T", t - 2, 3)] if t >= 2 else []
                    dma(war, lambda e: e.dma_start(og_in[:, tb, :], og_dram[t * P:(t + 1) * P, :]), ("og in", t), f"ogin{tb}")
                steps.append(load)
            for m in range(4):
                def part(m=m):
                    hs = slice(4 * m, 4 * m + 4)

                    def fn(e):
                        for h in range(4):
                            r = e.transpose(bank[m][:, h * P:(h + 1) * P], og_in[:, tb, (4 * m + h) * P:(4 * m + h + 1) * P], C["ident"])
                        return r
                    do("pe", [("og in", t), *bank_free[m]], fn, ("og^T", t, m))
                    war = [("s psum", t - 2)] if t >= 2 else []
                    src = bank[m][:, :].rearrange("p (h t) -> p h t", h=4)
                    do("act", [("og^T", t, m), *war], lambda e: e.copy(ogT_hi[:, tb, hs, :], src), ("ogT hi", t, m))
                    do("dve", [("ogT hi", t, m)], lambda e: e.tensor_tensor(
                        ogT_lo[:, tb, hs, :], src, ogT_hi[:, tb, hs, :].bitcast(f32), SUB), ("ogT lo", t, m))
                    bank_free[m] = [("ogT lo", t, m)]
                steps.append(part)
            return steps

        def finish(t):
            tb = t % 2
            b = 4 + tb

            def residual():
                war = [("out sum", t - 2)] if t >= 2 else []
                dma(war, lambda e: e.dma_start(x_res[:, tb, :], x[0, t * P:(t + 1) * P, :]), ("x res", t), f"xres{tb}")

            def out_projection():
                do("pe", [("ogT lo", t, 3), ("wo lo", WO - 1), *bank_free[b]], project(
                    bank[b][:, :], lambda i: (ogT_hi[:, tb, i, :], ogT_lo[:, tb, i, :]),
                    lambda i: (wo_hi[:, i, :], wo_lo[:, i, :]), HEADS), ("s psum", t))
                war = [("out stored", t - 2)] if t >= 2 else []
                do("dve", [("s psum", t), *war], lambda e: e.scalar_tensor_tensor(
                    y_out[:, tb, :], bank[b][:, :], 0.5, gate_acc[:, t, :], MUL, MUL), ("gated", t))
                bank_free[b] = [("gated", t)]
                do("pool", [("gated", t), ("x res", t)], lambda e: e.tensor_tensor(
                    y_out[:, tb, :], y_out[:, tb, :], x_res[:, tb, :], ADD), ("out sum", t))
                dma([("out sum", t)], lambda e: e.dma_start(out[0, t * P:(t + 1) * P, :], y_out[:, tb, :]), ("out stored", t), f"out{tb}")
            return [residual, out_projection]

        for f in turn(0):
            f()
        for t in range(NT):
            merge(*[s for s in (turn(t + 1) if t + 1 < NT else [], finish(t)) if s])
        pr.wait("sp", ("out stored", NT - 1), ("out stored", NT - 2), ("og stored", NQ - 1), ("og stored", NQ - 2))

        block = top.enter_context(nc.Block())
        for name, key in (("sync", "sp"), ("tensor", "pe"), ("scalar", "act"), ("vector", "dve"), ("gpsimd", "pool")):
            def run(e, key=key):
                for op in pr.queue[key]:
                    op(e)
            dict(sync=block.sync, tensor=block.tensor, scalar=block.scalar, vector=block.vector, gpsimd=block.gpsimd)[name](run)
        p4.close()


def kernel(L0_attn_hidden_states, L0_attn_W_qkv, L0_attn_W_z, L0_attn_W_b, L0_attn_W_a, L0_attn_conv_w, L0_attn_dt_bias,
           L0_attn_A_log, L0_attn_norm_weight, L0_attn_W_out, L0_ffn_gate_w, L0_ffn_w1, L0_ffn_b1, L0_ffn_w2, L0_ffn_b2):
    import concourse.bacc as bacc
    from concourse.bass_utils import run_bass_kernel_spmd

    wqkv = np.asarray(L0_attn_W_qkv)
    wz = np.asarray(L0_attn_W_z)
    kd = KEY_HEADS * HD
    groups = []
    for gr in range(KEY_HEADS):
        qs, ks = slice(gr * HD, (gr + 1) * HD), slice(kd + gr * HD, kd + (gr + 1) * HD)
        vs = slice(2 * kd + REP * gr * HD, 2 * kd + REP * (gr + 1) * HD)
        cols = np.concatenate([wqkv[:, ks], wqkv[:, qs], wqkv[:, vs], wz[:, REP * gr * HD:REP * (gr + 1) * HD]], 1)
        groups.append(cols.reshape(ND, P, GW).transpose(1, 0, 2))
    cw = np.asarray(L0_attn_conv_w)
    tiles = []
    for gr in range(KEY_HEADS):
        for at in (kd + gr * HD, gr * HD, 2 * kd + REP * gr * HD, 2 * kd + (REP * gr + 1) * HD):
            tiles.append(cw[at:at + HD])
    const, where = constants()
    arrays = {
        "x": np.asarray(L0_attn_hidden_states),
        "small_w": np.concatenate([np.asarray(L0_attn_W_b), np.asarray(L0_attn_W_a), np.asarray(L0_ffn_gate_w).T], 1),
        "group_w": np.stack(groups),
        "conv_w": np.stack(tiles, 1),
        "dt_bias": np.asarray(L0_attn_dt_bias),
        "a_log": np.asarray(L0_attn_A_log),
        "norm_w": np.asarray(L0_attn_norm_weight),
        "w_out": np.asarray(L0_attn_W_out),
        "w1": np.asarray(L0_ffn_w1),
        "b1": np.asarray(L0_ffn_b1).reshape(EXPERTS, DFF // P, P).transpose(0, 2, 1),
        "w2": np.asarray(L0_ffn_w2),
        "b2": np.asarray(L0_ffn_b2),
        "const": const,
    }
    arrays = {k: np.ascontiguousarray(v) for k, v in arrays.items()}
    nc = bacc.Bacc("TRN2", target_bir_lowering=False, num_devices=1)
    f32 = mybir.dt.float32
    aps = {k: nc.dram_tensor(k, v.shape, f32, kind="ExternalInput").ap() for k, v in arrays.items()}
    out = nc.dram_tensor("out", (1, T, D), f32, kind="ExternalOutput").ap()
    og_dram = nc.dram_tensor("og_dram", (T, HEADS * HD), f32, kind="Internal").ap()
    build(nc, where=where, og_dram=og_dram, out=out, **aps)
    r = run_bass_kernel_spmd(nc, [arrays], core_ids=[0])
    return r.results[0]["out"]
```

```python
from contextlib import ExitStack

import concourse.bass as bass
import numpy as np
from concourse import mybir

P = 128
T, D = 2048, 512
KEY_HEADS, HEADS, HD = 8, 16, 128
KW = 4
EXPERTS, DFF, TOP = 8, 2048, 2
LN_EPS, L2_EPS, RMS_EPS = 1e-5, 1e-6, 1e-6
NT = T // P
ND = D // P
SB = 512
NSB = T // SB
CPS = SB // P
REP = HEADS // KEY_HEADS
QUAD = 2
NHC = QUAD * REP
NAB = 2 * HEADS + EXPERTS
NBUF = 3
LEVELS = 7
SERIES = 9
KINDS = {"k": (0, P), "q": (P, P), "v0": (2 * P, P), "v1": (3 * P, P), "z": (4 * P, REP * HD)}
GW = 4 * P + REP * HD


def constants():
    i = np.arange(P)
    parts = {
        "ident": np.eye(P),
        "after": (i[:, None] > i[None, :]),
        "upto": (i[:, None] <= i[None, :]),
        "ones": np.ones((P, P)),
        "kq": np.concatenate([-(i[:, None] < i[None, :]).astype(float), (i[:, None] <= i[None, :])], 1),
        "pairs": (i[:, None] % 2 == 0) & (i[None, :] == i[:, None] + 1),
        "iota": np.broadcast_to(np.arange(EXPERTS), (P, EXPERTS)),
    }
    for lev in range(1, LEVELS):
        s = 1 << lev
        col = np.arange(P // 2) // s
        parts[f"rows{lev}"] = (i[:, None] // (2 * s) == col[None, :]) & ((i[:, None] // s) % 2 == 1)
    at, where = 0, {}
    for name, a in parts.items():
        where[name] = (at, at + a.shape[1])
        at += a.shape[1]
    return np.concatenate([np.asarray(a, np.float32) for a in parts.values()], 1), where


class Program:
    HOP, OWN = 0.2, 0.1

    def __init__(self, nc, ctx):
        self.nc, self.ctx = nc, ctx
        self.queue = {e: [] for e in ("pe", "act", "dve", "pool", "sp")}
        self.sem = {e: ctx.enter_context(nc.semaphore(f"s_{e}")) for e in ("pe", "act", "dve", "pool")}
        self.count, self.done, self.seen = {}, {}, {}
        self.clock = {e: 0.0 for e in self.queue}
        self.end = {}

    def wait(self, engine, *steps):
        for step in steps:
            sem, value = self.done[step]
            if self.seen.get((engine, sem), 0) < value:
                self.seen[engine, sem] = value
                self.queue[engine].append(lambda e, s=self.sem[sem], v=value: e.wait_ge(s, v))

    def alias(self, name, step):
        self.done[name], self.end[name] = self.done[step], self.end[step]

    def start(self, engine, waits):
        at = self.clock[engine]
        for w in waits:
            if w not in self.done:
                return None
            at = max(at, self.end[w] + (self.OWN if self.done[w][0] == engine else self.HOP))
        return at

    def issue(self, engine, lane, waits, fn, step, cost):
        at = self.start(engine, waits)
        self.wait(engine, *waits)
        by = 1 if lane is None else 16
        sem = engine if lane is None else lane
        if sem not in self.sem:
            self.sem[sem] = self.ctx.enter_context(self.nc.semaphore(f"s_dma_{lane}"))
        self.count[sem] = self.count.get(sem, 0) + by
        self.done[step] = (sem, self.count[sem])
        self.end[step] = at + cost
        self.clock[engine] = at + (cost if lane is None else 0.05)
        self.queue[engine].append(lambda e, s=self.sem[sem], by=by: fn(e).then_inc(s, by))

    def do(self, engine, waits, fn, step, cost=0.2):
        yield engine, None, waits, fn, step, cost

    def dma(self, waits, fn, step, lane, cost=3.0):
        yield "sp", lane, waits, fn, step, cost

    def run(self, *streams):
        heads = {n: op for n, s in enumerate(streams) if (op := next(s, None)) is not None}
        while heads:
            ready = [(at, n) for n, op in heads.items() if (at := self.start(op[0], op[2])) is not None]
            assert ready, ("no step can go on", {n: op[4] for n, op in heads.items()})
            first = min(at for at, _ in ready)
            n = min((n for at, n in ready if at <= first + 0.02))
            self.issue(*heads[n])
            heads[n] = next(streams[n], None)
            if heads[n] is None:
                del heads[n]

    def fence(self, engines=("pe", "act", "dve", "pool", "sp")):
        for sem, value in self.count.items():
            self.done["fence", sem] = (sem, value)
        for engine in engines:
            self.wait(engine, *[("fence", sem) for sem in self.count])
        now = max(self.clock.values())
        self.clock = {e: now for e in self.clock}


def pe(n, cols, passes):
    return n * passes * cols / 2400


def dve(n, cols):
    return n * (0.07 + cols / 960)


def act(n, cols, scales=0):
    return n * (0.05 + 0.03 * scales + cols / 1200)


def pool(n, cols):
    return n * (0.1 + cols * 1.75e-3)


def build(nc, x, small_w, group_w, conv_w, dt_bias, a_log, norm_w, w_out, w1, b1, w2, b2, const, where, og_dram, out):
    f32, f32r, u32 = mybir.dt.float32, mybir.dt.float32r, mybir.dt.uint32
    ALU, ACT, AX = mybir.AluOpType, mybir.ActivationFunctionType, mybir.AxisListType
    MUL, ADD, SUB = ALU.mult, ALU.add, ALU.subtract

    top = ExitStack()
    with top:
        pr = Program(nc, top)
        do, dma = pr.do, pr.dma

        def now(*steps):
            for s in steps:
                for op in s:
                    pr.issue(*op)

        def alloc(ctx, name, free, dtype=f32, side="left"):
            return ctx.enter_context(nc.sbuf_tensor(name, [P, *free], dtype, side=side))

        bank = [top.enter_context(nc.psum_tensor(f"bank{i}", [P, 512], f32)) for i in range(8)]
        bank_free = {i: [] for i in range(8)}

        ncst = const.shape[1]
        cst = alloc(top, "cst", [ncst])
        C = {n: cst[:, a:b] for n, (a, b) in where.items()}
        xn_life = ExitStack()
        xn_hi = alloc(xn_life, "xn_hi", [ND, T], f32r, side="right")
        xn_lo = alloc(xn_life, "xn_lo", [ND, T], f32r, side="right")
        rw = alloc(top, "rw", [TOP, NT])
        expert = alloc(top, "expert", [8], u32)

        def split3(e, ps, lhs, rhs, first, last):
            (lh, ll), (rh, rl) = lhs, rhs
            e.matmul(ps, lh, rh, start=first, stop=False)
            e.matmul(ps, lh, rl, start=False, stop=False)
            return e.matmul(ps, ll, rh, start=False, stop=last)

        def project(ps, lhs, rhs, n):
            def fn(e):
                for i in range(n):
                    r = split3(e, ps, lhs(i), rhs(i), i == 0, i == n - 1)
                return r
            return fn

        att = ExitStack()
        g_hi = alloc(att, "g_hi", [NT, HEADS], f32r)
        g_lo = alloc(att, "g_lo", [NT, HEADS], f32r)
        beta = alloc(att, "beta", [NT, HEADS])
        decay = alloc(att, "decay", [NT, HEADS])
        neg_decay = alloc(att, "neg_decay", [NT, HEADS])
        remain = alloc(att, "remain", [NT, HEADS])
        total = alloc(att, "total", [NT, HEADS])
        after_r = alloc(att, "after_r", [P], f32r)
        taps = alloc(att, "taps", [4 * KEY_HEADS, KW])
        half_pow = alloc(att, "half_pow", [8])
        neg_half_pow = alloc(att, "neg_half_pow", [NT])

        p1 = ExitStack()
        x_in = alloc(p1, "x_in", [NT, D])
        xn = alloc(p1, "xn", [4, D])
        stats = alloc(p1, "stats", [NT, 6])
        moments = alloc(p1, "moments", [NT, 2])
        rstd = alloc(p1, "rstd", [NT])
        sw = alloc(p1, "sw", [ND, NAB])
        sw_hi = alloc(p1, "sw_hi", [ND, NAB], f32r)
        sw_lo = alloc(p1, "sw_lo", [ND, NAB], f32r)
        ab = alloc(p1, "ab", [NT, NAB])
        hvec = {n: alloc(p1, n, [HEADS]) for n in ("dtb", "alog", "arate")}
        t_ = [alloc(p1, f"tmp{i}", [NT, HEADS]) for i in range(4)]
        g = alloc(p1, "g", [NT, HEADS])
        scores = alloc(p1, "scores", [EXPERTS])
        best = alloc(p1, "best", [8])
        expert_f = alloc(p1, "expert_f", [8])
        pick = alloc(p1, "pick", [TOP, EXPERTS])
        picked = alloc(p1, "picked", [NT, EXPERTS])
        lmax = alloc(p1, "lmax", [NT])
        lsum = alloc(p1, "lsum", [NT])

        def loads():
            n = NT // 4
            for q in range(4):
                dst = x_in[:, q * n:(q + 1) * n, :]
                src = x[0, q * n * P:(q + 1) * n * P, :].rearrange("(a p) d -> p a d", p=P)
                yield from dma([], lambda e, dst=dst, src=src: e.dma_start(dst, src), ("x", q), f"x{q}", 4.0 + 4 * q)
                if q == 0:
                    yield from dma([], lambda e: e.dma_start(cst[:, :], const[:, :]), "constants", "const")
                    yield from dma([], lambda e: e.dma_start(sw[:, :, :], small_w.rearrange("(k p) n -> p k n", p=P)), "small weights", "sw")
            yield from dma([], lambda e: e.dma_start(hvec["dtb"][:, :], dt_bias[:].partition_broadcast(P)), "dt_bias", "dtb")
            yield from dma([], lambda e: e.dma_start(hvec["alog"][:, :], a_log[:].partition_broadcast(P)), "A_log", "alog")
            yield from dma([], lambda e: e.dma_start(taps[:, :, :], conv_w[:, :, :]), "conv weights", "taps")

        def setup():
            yield from do("pool", [], lambda e: e.memset(neg_half_pow[:, :], -0.5), "neg_half_pow")
            yield from do("pool", [], lambda e: e.memset(half_pow[:, :], 0.5), "half_pow")
            yield from do("act", ["small weights"], lambda e: e.copy(sw_hi[:, :, :], sw[:, :, :]), "sw_hi")
            yield from do("pool", ["sw_hi"], lambda e: e.tensor_tensor(sw_lo[:, :, :], sw[:, :, :], sw_hi[:, :, :].bitcast(f32), SUB), "sw_lo")
            yield from do("act", ["constants"], lambda e: e.copy(after_r[:, :], C["after"]), "after_r")
            yield from do("dve", ["conv weights"], lambda e: e.tensor_scalar(taps[:, :, :], taps[:, :, :], 0.5, None, MUL), "taps")

        def layernorm():
            n = NT // 4
            for q in range(4):
                for t in range(q * n, (q + 1) * n):
                    yield from do("dve", [("x", q)], lambda e, t=t: e.bn_stats(stats[:, t, :], x_in[:, t, :]), ("stats", t), dve(1, D))
                    yield from do("dve", [("stats", t)], lambda e, t=t: e.bn_aggr(moments[:, t, :], stats[:, t, :]), ("moments", t), 0.07)
                r = slice(q * n, (q + 1) * n)
                yield from do("dve", [("moments", q * n + n - 1)],
                              lambda e, r=r: e.tensor_scalar(rstd[:, r], moments[:, r, 1], LN_EPS, None, ADD), ("var", q), 0.07)
                yield from do("pool", [("var", q), "neg_half_pow"],
                              lambda e, r=r: e.tensor_tensor(rstd[:, r], rstd[:, r], neg_half_pow[:, r], ALU.pow), ("rstd", q), 1.0)

        def rows_of(t):
            q, b = t // (NT // 4), t % 4
            yield from do("dve", [("rstd", q), *([("xn^T", t - 4)] if t >= 4 else [])], lambda e: e.tensor_scalar(
                xn[:, b, :], x_in[:, t, :], moments[:, t, 0:1], rstd[:, t:t + 1], SUB, MUL), ("xn", t), dve(1, D // 2))

            def transposes(e):
                for k in range(ND):
                    r = e.transpose(bank[b][:, k * P:(k + 1) * P], xn[:, b, k * P:(k + 1) * P], C["ident"])
                return r
            yield from do("pe", [("xn", t), "constants", *([("xn_lo", t - 4)] if t >= 4 else [])], transposes, ("xn^T", t), pe(ND, P, 2))
            src = bank[b][:, :].rearrange("p (k c) -> p k c", k=ND)
            dst = slice(t * P, (t + 1) * P)
            yield from do("act", [("xn^T", t)], lambda e: e.copy(xn_hi[:, :, dst], src), ("xn_hi", t), act(1, D))
            yield from do("dve", [("xn_hi", t)], lambda e: e.tensor_tensor(
                xn_lo[:, :, dst], src, xn_hi[:, :, dst].bitcast(f32), SUB), ("xn_lo", t), dve(1, D))
            ps = bank[4 + t // 8][:, (t % 8) * 64:(t % 8) * 64 + NAB]
            yield from do("pe", [("xn_lo", t), "sw_lo"], project(
                ps, lambda i: (xn_hi[:, i, dst], xn_lo[:, i, dst]),
                lambda i: (sw_hi[:, i, :], sw_lo[:, i, :]), ND), ("ab psum", t), pe(ND, 64, 3))

        def all_rows(par):
            for t in range(par, NT, 2):
                yield from rows_of(t)

        pr.run(all_rows(0), all_rows(1), setup(), layernorm(), loads())

        for hb in range(2):
            now(do("act", [("ab psum", hb * 8 + 7)], lambda e, hb=hb: e.copy(
                ab[:, hb * 8:hb * 8 + 8, :],
                bank[4 + hb][:, :].rearrange("p (t c) -> p t c", t=8)[:, :, 0:NAB]), ("ab", hb)))
        AB = [("ab", 0), ("ab", 1)]
        b_, a_, lg = ab[:, :, 0:HEADS], ab[:, :, HEADS:2 * HEADS], ab[:, :, 2 * HEADS:NAB]

        gates_ready = []

        def decay_gates():
            yield from do("act", AB, lambda e: e.activation(beta[:, :, :], b_, ACT.Exp, scale=-1.0), "exp(-b)")
            yield from do("dve", ["exp(-b)"], lambda e: e.tensor_scalar(beta[:, :, :], beta[:, :, :], 1.0, None, ADD), "1+exp(-b)")
            yield from do("dve", ["1+exp(-b)"], lambda e: e.reciprocal(beta[:, :, :], beta[:, :, :]), "beta")

            def bc(v):
                return v[:, :].rearrange("p (o h) -> p o h", o=1).to_broadcast([P, NT, HEADS])
            y, w, s, acc = t_
            yield from do("act", ["A_log"], lambda e: e.activation(hvec["arate"][:, :], hvec["alog"][:, :], ACT.Exp), "exp(A_log)")
            yield from do("dve", [*AB, "dt_bias"], lambda e: e.tensor_tensor(y[:, :, :], a_, bc(hvec["dtb"]), ADD), "y")
            yield from do("act", ["y"], lambda e: e.activation(w[:, :, :], y[:, :, :], ACT.Abs), "|y|")
            yield from do("act", ["|y|"], lambda e: e.activation(w[:, :, :], w[:, :, :], ACT.Exp, scale=-1.0), "w")
            yield from do("dve", ["w"], lambda e: e.tensor_scalar(s[:, :, :], w[:, :, :], 2.0, None, ADD), "w+2")
            yield from do("dve", ["w+2"], lambda e: e.reciprocal(s[:, :, :], s[:, :, :]), "1/(w+2)")
            yield from do("dve", ["1/(w+2)"], lambda e: e.tensor_tensor(s[:, :, :], w[:, :, :], s[:, :, :], MUL), "s")
            yield from do("dve", ["s"], lambda e: e.tensor_tensor(w[:, :, :], s[:, :, :], s[:, :, :], MUL), "s^2")
            yield from do("dve", ["s^2"], lambda e: e.tensor_scalar(acc[:, :, :], w[:, :, :], 1.0 / (2 * SERIES + 1), 1.0 / (2 * SERIES - 1), MUL, ADD), ("series", SERIES))
            for k in range(SERIES - 1, 0, -1):
                yield from do("dve", [("series", k + 1)], lambda e: e.tensor_tensor(acc[:, :, :], acc[:, :, :], w[:, :, :], MUL), ("series*", k))
                yield from do("dve", [("series*", k)], lambda e, k=k: e.tensor_scalar(acc[:, :, :], acc[:, :, :], 1.0 / (2 * k - 1), None, ADD), ("series", k))
            yield from do("dve", [("series", 1)], lambda e: e.scalar_tensor_tensor(acc[:, :, :], acc[:, :, :], 2.0, s[:, :, :], MUL, MUL), "log1p")
            yield from do("dve", ["log1p"], lambda e: e.scalar_tensor_tensor(acc[:, :, :], y[:, :, :], 0.0, acc[:, :, :], ALU.max, ADD), "softplus")
            yield from do("dve", ["softplus", "exp(A_log)"], lambda e: e.tensor_tensor(acc[:, :, :], acc[:, :, :], bc(hvec["arate"]), MUL), "-g")
            yield from do("dve", ["-g"], lambda e: e.tensor_scalar(g[:, :, :], acc[:, :, :], -1.0, None, MUL), "g")
            yield from do("act", ["g"], lambda e: e.copy(g_hi[:, :, :], g[:, :, :]), "g_hi")
            yield from do("dve", ["g_hi"], lambda e: e.tensor_tensor(g_lo[:, :, :], g[:, :, :], g_hi[:, :, :].bitcast(f32), SUB), "g_lo")
            flat = g[:, :, :].rearrange("p t h -> p (t h)")
            for n, (mask, dst) in enumerate((("upto", decay), ("after", remain), ("ones", total))):
                ps = bank[6][:, 0:NT * HEADS] if n == 0 else bank[n - 1][:, 0:NT * HEADS]
                yield from do("pe", ["g", "constants"], lambda e, m=mask, ps=ps: e.matmul(ps, C[m], flat, start=True, stop=True), ("sum", mask))
                yield from do("act", [("sum", mask)], lambda e, ps=ps, d=dst: e.activation(
                    d[:, :, :].rearrange("p t h -> p (t h)"), ps, ACT.Exp), ("exp sum", mask))
            yield from do("dve", [("exp sum", "upto")], lambda e: e.tensor_scalar(neg_decay[:, :, :], decay[:, :, :], -1.0, None, MUL), "neg_decay")
            gates_ready[:] = ["neg_decay", ("exp sum", "after"), ("exp sum", "ones"), "beta", "g_lo", "after_r"]

        def router():
            def score(e):
                for t in range(NT):
                    r = e.matmul(bank[7][:, 0:EXPERTS], C["ones"], lg[:, t, :], start=t == 0, stop=t == NT - 1)
                return r
            yield from do("pe", [*AB, "constants"], score, "scores psum")
            yield from do("dve", ["scores psum"], lambda e: e.tensor_copy(scores[:, :], bank[7][:, 0:EXPERTS]), "scores")
            yield from do("dve", ["scores"], lambda e: e.max(best[:, :], scores[:, :]), "best")
            yield from do("dve", ["best"], lambda e: e.max_index(expert[:, :], best[:, :], scores[:, :]), "expert")
            yield from do("dve", ["expert"], lambda e: e.tensor_copy(expert_f[:, :], expert[:, :]), "expert_f")
            for k in range(TOP):
                yield from do("dve", ["expert_f"], lambda e, k=k: e.tensor_scalar(
                    pick[:, k, :], C["iota"], expert_f[:, k:k + 1], None, ALU.is_equal), ("pick", k))
                yield from do("dve", [("pick", k)], lambda e, k=k: e.tensor_tensor(
                    picked[:, :, :], lg, pick[:, k:k + 1, :].to_broadcast([P, NT, EXPERTS]), MUL), ("picked", k))
                yield from do("dve", [("picked", k)], lambda e, k=k: e.reduce_sum(rw[:, k, :], picked[:, :, :], AX.X), ("logit", k))
            yield from do("dve", [("logit", 0), ("logit", 1)], lambda e: e.tensor_tensor(lmax[:, :], rw[:, 0, :], rw[:, 1, :], ALU.max), "logit max")
            for k in range(TOP):
                yield from do("dve", ["logit max"], lambda e, k=k: e.tensor_tensor(rw[:, k, :], rw[:, k, :], lmax[:, :], SUB), ("centred", k))
                yield from do("act", [("centred", k)], lambda e, k=k: e.activation(rw[:, k, :], rw[:, k, :], ACT.Exp), ("exp logit", k))
            yield from do("dve", [("exp logit", 0), ("exp logit", 1)], lambda e: e.tensor_tensor(lsum[:, :], rw[:, 0, :], rw[:, 1, :], ADD), "logit sum")
            yield from do("dve", ["logit sum"], lambda e: e.reciprocal(lsum[:, :], lsum[:, :]), "1/logit sum")
            for k in range(TOP):
                yield from do("dve", ["1/logit sum"], lambda e, k=k: e.tensor_tensor(rw[:, k, :], rw[:, k, :], lsum[:, :], MUL), ("rw", k))

        pr.run(decay_gates(), router())
        gates = gates_ready
        pr.fence()
        p1.close()

        p2 = ExitStack()
        w_raw = alloc(p2, "w_raw", [2, ND, P])
        w_hi = {k: alloc(p2, f"w_hi_{k}", [ND, n], f32r) for k, (_, n) in KINDS.items()}
        w_lo = {k: alloc(p2, f"w_lo_{k}", [ND, n], f32r) for k, (_, n) in KINDS.items()}
        pre = alloc(p2, "pre", [2, SB + KW - 1])
        halo = alloc(p2, "halo", [4, KW - 1])
        conv = alloc(p2, "conv", [2, SB])
        kqT = alloc(p2, "kqT", [NBUF, CPS, 2, P])
        vT = alloc(p2, "vT", [2, SB])
        square = alloc(p2, "square", [SB])
        k_tok = alloc(p2, "k_tok", [NBUF, CPS, HD])
        v_tok = alloc(p2, "v_tok", [NBUF, CPS, REP, HD])
        z_gate = alloc(p2, "z_gate", [NBUF, CPS, REP, HD])
        norms = alloc(p2, "norms", [NBUF, 2, CPS])
        k_len = alloc(p2, "k_len", [NBUF, CPS])
        inv_n = alloc(p2, "inv_n", [NBUF, CPS])
        q_eps = alloc(p2, "q_eps", [NBUF, CPS])
        cw = alloc(p2, "cw", [NBUF, CPS, REP])
        gm_hi = alloc(p2, "gm_hi", [NHC, P], f32r)
        gm_lo = alloc(p2, "gm_lo", [NHC, P], f32r)
        E = alloc(p2, "E", [2, NHC, P])
        kq = alloc(p2, "kq", [2, QUAD, 2, P])
        PT = alloc(p2, "PT", [3, NHC, P])
        inv = alloc(p2, "inv", [2, NHC, P])
        Cn = alloc(p2, "Cn", [2, NHC, P])
        X = alloc(p2, "X", [2, NHC, P])
        XT = alloc(p2, "XT", [2, NHC, P])
        Y = alloc(p2, "Y", [2, NHC, P // 2])
        S = alloc(p2, "S", [REP, HD])
        R = alloc(p2, "R", [REP, HD])
        U = alloc(p2, "U", [REP, HD])
        UR = alloc(p2, "UR", [REP, HD])
        O = alloc(p2, "O", [2, QUAD, REP, HD])
        squares = alloc(p2, "squares", [NHC, HD])
        ms = alloc(p2, "ms", [2, NHC])

        A_BANKS, K_BANK, Q_BANK = (0, 1), 6, 7

        def b_banks(par):
            return 2 + 2 * par, 3 + 2 * par

        def weights():
            names = [(gr, kind, part) for gr in range(KEY_HEADS) for kind, (_, width) in KINDS.items() for part in range(width // P)]
            for n, (gr, kind, part) in enumerate(names):
                at = KINDS[kind][0] + part * P
                src, dst = group_w[gr, :, :, at:at + P], w_raw[:, n % 2, :, :]
                yield from dma([("w lo part", *names[n - 2])] if n >= 2 else [], lambda e, dst=dst, src=src: e.dma_start(dst, src),
                               ("w raw", *names[n]), f"w{n % 2}", 3.0)
                if n:
                    yield from split_weights(*names[n - 1], (n - 1) % 2)
            yield from split_weights(*names[-1], (len(names) - 1) % 2)

        def split_weights(gr, kind, part, slot):
            raw = w_raw[:, slot, :, :]
            cols = slice(part * P, (part + 1) * P)
            war = [("last projection", gr - 1, kind)] if gr else []
            yield from do("act", [("w raw", gr, kind, part), *war], lambda e: e.copy(w_hi[kind][:, :, cols], raw), ("w hi", gr, kind, part), act(1, ND * P))
            yield from do("pool", [("w hi", gr, kind, part)], lambda e: e.tensor_tensor(
                w_lo[kind][:, :, cols], raw, w_hi[kind][:, :, cols].bitcast(f32), SUB), ("w lo part", gr, kind, part), pool(1, ND * P))
            if cols.stop == KINDS[kind][1]:
                pr.alias(("w lo", gr, kind), ("w lo part", gr, kind, part))

        CONV = {"k": (0, 0), "q": (1, 1), "v0": (0, 2), "v1": (1, 3)}
        BEFORE = {"k": (-1, "v0"), "q": (-1, "v1"), "v0": (0, "k"), "v1": (0, "q")}

        def unit(u):
            return u // NSB, u % NSB, u % NBUF

        def project_steps(ps, lhs, rhs, n, waits, step, cost):
            for i in range(n):
                yield from do("pe", waits if i == 0 else [], lambda e, i=i: split3(e, ps, lhs(i), rhs(i), i == 0, i == n - 1),
                              step if i == n - 1 else (step, i), cost)

        def conv_stream(kinds):
            for u in range(NU):
                for kind in kinds:
                    yield from convolve(u, kind)

        def convolve(u, kind):
            gr, sb, ub = unit(u)
            s, t = CONV[kind]
            du, bk = BEFORE[kind]
            prev = [("act", u + du, bk)] if u + du >= 0 else []
            if sb == 0:
                yield from do("dve", prev, lambda e: e.memset(pre[:, s, 0:KW - 1], 0.0), ("past", u, kind), 0.07)
            else:
                yield from do("dve", [("history", u - 1, kind), *prev], lambda e: e.tensor_copy(pre[:, s, 0:KW - 1], halo[:, t, :]), ("past", u, kind), 0.07)
            wt = taps[:, 4 * gr + t, :]
            yield from do("dve", [("pre", u, kind), ("past", u, kind)], lambda e: e.tensor_scalar(
                conv[:, s, :], pre[:, s, 0:SB], wt[:, 0:1], None, MUL), ("tap", u, kind, 0), dve(1, SB // 2))
            for j in range(1, KW):
                yield from do("dve", [("tap", u, kind, j - 1)], lambda e, j=j: e.scalar_tensor_tensor(
                    conv[:, s, :], pre[:, s, j:j + SB], wt[:, j:j + 1], conv[:, s, :], MUL, ADD), ("tap", u, kind, j), dve(1, SB))
            yield from do("dve", [], lambda e: e.tensor_copy(halo[:, t, :], pre[:, s, SB:SB + KW - 1]), ("history", u, kind), 0.07)
            yield from do("act", [("tap", u, kind, KW - 1), ("history", u, kind)], lambda e: e.activation(pre[:, s, 0:SB], conv[:, s, :], ACT.Tanh), ("tanh", u, kind), act(1, SB))
            if kind in "kq":
                dst = kqT[:, ub, :, "kq".index(kind), :]
                last = 2 * (u - NBUF) + 1
                war = [("C done", last), ("kq psum", last)] if u >= NBUF else []
                src = lambda a: a.rearrange("p (c t) -> p c t", c=CPS)
            else:
                dst = vT[:, s, :]
                war = [("v^T^T", u - 1, s)] if u else []
                src = lambda a: a
            yield from do("dve", [("tanh", u, kind), *war], lambda e: e.scalar_tensor_tensor(
                dst, src(pre[:, s, 0:SB]), 1.0, src(conv[:, s, :]), ADD, MUL), ("act", u, kind), dve(1, SB))

        def stream_a():
            for u in range(NU):
                yield from stage_a(u)

        def stage_a(u):
            gr, sb, ub = unit(u)
            toks = slice(sb * SB, (sb + 1) * SB)
            last = sb == NSB - 1
            used = 2 * (u - NBUF)
            turn = [0]

            def next_bank():
                turn[0] += 1
                return A_BANKS[turn[0] % 2]

            def proj(kind):
                b = next_bank()
                yield from project_steps(
                    bank[b][:, :], lambda i: (w_hi[kind][:, i, :], w_lo[kind][:, i, :]),
                    lambda i: (xn_hi[:, i, toks], xn_lo[:, i, toks]), ND,
                    [("w lo", gr, kind), *bank_free[b]], ("proj", u, kind), pe(3, SB, 1))
                if last:
                    pr.alias(("last projection", gr, kind), ("proj", u, kind))
                s = CONV[kind][0]
                du, bk = BEFORE[kind]
                war = [("act", u + du, bk)] if u + du >= 0 else []
                bank_free[b] = [("pre", u, kind)]
                yield from do("act", [("proj", u, kind), *war], lambda e: e.copy(pre[:, s, KW - 1:], bank[b][:, :]), ("pre", u, kind), act(1, SB))

            def norm(kind):
                n = "kq".index(kind)
                war = [("norm psum", u - (kind == "k"), "q" if kind == "k" else "k")] if u or n else []
                yield from do("act", [("act", u, kind), *war], lambda e: e.activation(
                    square[:, :].rearrange("p (c t) -> p c t", c=CPS), kqT[:, ub, :, n, :], ACT.Square), ("square", u, kind), act(1, SB))
                b = next_bank()

                def sums(e):
                    for c in range(CPS):
                        r = e.matmul(bank[b][:, c:c + 1], square[:, c * P:(c + 1) * P], C["ones"][:, 0:1], start=True, stop=True)
                    return r
                yield from do("pe", [("square", u, kind), *bank_free[b]], sums, ("norm psum", u, kind), 0.1)
                war = [("D done", used + 1), ("v_tok", u - NBUF, 1), ("v_tok", u - NBUF, 0)] if u >= NBUF else []
                bank_free[b] = [("norm", u, kind)]
                yield from do("dve", [("norm psum", u, kind), *war], lambda e: e.tensor_scalar(
                    norms[:, ub, n, :], bank[b][:, 0:CPS], L2_EPS, None, ADD), ("norm", u, kind), 0.07)
                if kind == "k":
                    yield from do("pool", [("norm", u, "k")], lambda e: e.tensor_tensor(
                        k_len[:, ub, :], norms[:, ub, 0, :], half_pow[:, 0:CPS], ALU.pow), ("k_len", u), 1.0)
                    yield from do("dve", [("norm", u, "k")], lambda e: e.reciprocal(inv_n[:, ub, :], norms[:, ub, 0, :]), ("inv_n", u), 0.1)
                    h0 = REP * gr
                    yield from do("dve", [("inv_n", u)], lambda e: e.tensor_tensor(
                        cw[:, ub, :, :], beta[:, sb * CPS:(sb + 1) * CPS, h0:h0 + REP],
                        inv_n[:, ub, :].rearrange("p (c o) -> p c o", o=1).to_broadcast([P, CPS, REP]), MUL), ("c", u), 0.08)
                else:
                    yield from do("dve", [("norm", u, "q")], lambda e: e.tensor_scalar(
                        q_eps[:, ub, :], norms[:, ub, 1, :], 4 * RMS_EPS * HD, None, MUL), ("q_eps", u), 0.07)

            def tokens_k():
                b = next_bank()

                def fn(e):
                    for c in range(CPS):
                        r = e.transpose(bank[b][:, c * P:(c + 1) * P], kqT[:, ub, c, 0, :], C["ident"])
                    return r
                yield from do("pe", [("act", u, "k"), *bank_free[b]], fn, ("k^T^T", u), pe(CPS, P, 2))
                war = [("C done", used + 1)] if u >= NBUF else []
                bank_free[b] = [("k_tok", u)]
                yield from do("act", [("k^T^T", u), *war], lambda e: e.copy(
                    k_tok[:, ub, :, :], bank[b][:, :].rearrange("p (c d) -> p c d", c=CPS)), ("k_tok", u), act(1, SB))

            def tokens_v(h):
                b = next_bank()
                s = CONV[f"v{h}"][0]

                def fn(e):
                    for c in range(CPS):
                        r = e.transpose(bank[b][:, c * P:(c + 1) * P], vT[:, s, c * P:(c + 1) * P], C["ident"])
                    return r
                yield from do("pe", [("act", u, f"v{h}"), *bank_free[b]], fn, ("v^T^T", u, h), pe(CPS, P, 2))
                war = [("C done", used + 1)] if u >= NBUF else []

                def scaled(e):
                    for c in range(CPS):
                        r = e.mul(v_tok[:, ub, c, h, :], bank[b][:, c * P:(c + 1) * P], k_len[:, ub, c:c + 1])
                    return r
                bank_free[b] = [("v_tok", u, h)]
                yield from do("act", [("v^T^T", u, h), ("k_len", u), *war], scaled, ("v_tok", u, h), act(CPS, P, 1))

            def z(half):
                b = next_bank()
                for c in range(2):
                    t = slice(sb * SB + (2 * half + c) * P, sb * SB + (2 * half + c + 1) * P)
                    yield from project_steps(
                        bank[b][:, c * REP * HD:(c + 1) * REP * HD], lambda i, t=t: (xn_hi[:, i, t], xn_lo[:, i, t]),
                        lambda i: (w_hi["z"][:, i, :], w_lo["z"][:, i, :]), ND,
                        [("w lo", gr, "z"), *bank_free[b]], ("z psum", u, half) if c else ("z psum", u, half, 0), pe(3, REP * HD, 1))
                if last and half:
                    pr.alias(("last projection", gr, "z"), ("z psum", u, half))
                dst = z_gate[:, ub, 2 * half:2 * half + 2, :, :].rearrange("p c h d -> p (c h d)")
                war = [("D done", used + half)] if u >= NBUF else []
                bank_free[b] = [("z_gate", u, half)]
                yield from do("act", [("z psum", u, half), *war], lambda e: e.activation(dst, bank[b][:, :], ACT.Tanh, scale=0.5), ("z tanh", u, half), act(1, SB))
                yield from do("dve", [("z tanh", u, half)], lambda e: e.scalar_tensor_tensor(
                    dst, dst, 1.0, bank[b][:, :], ADD, MUL), ("z_gate", u, half), dve(1, SB))

            yield from proj("k")
            yield from proj("q")
            yield from z(0)
            yield from proj("v0")
            yield from norm("k")
            yield from tokens_k()
            yield from proj("v1")
            yield from norm("q")
            yield from z(1)
            yield from tokens_v(0)
            yield from tokens_v(1)

        def stream_b(par):
            for qd in range(par, NQ, 2):
                yield from stage_b(qd)

        def stage_b(qd):
            u, half, pb = qd // 2, qd % 2, qd % 2
            gr, sb, ub = unit(u)
            cs = [half * QUAD + i for i in range(QUAD)]
            c0, h0 = sb * CPS + cs[0], REP * gr
            YZ, TR = b_banks(pb)
            old = qd - 2

            def rates(src):
                return src[:, c0:c0 + QUAD, h0:h0 + REP].rearrange("p c (h o) -> p c h o", o=1).to_broadcast([P, QUAD, REP, P])

            for name, dst, src in (("gm_hi", gm_hi, g_hi), ("gm_lo", gm_lo, g_lo)):
                war = [("D psum", qd - 1)] if qd else []
                yield from do("pool", [*gates, *war], lambda e, dst=dst, src=src: e.tensor_tensor(
                    dst[:, :, :].rearrange("p (c h) t -> p c h t", c=QUAD),
                    C["upto"].rearrange("p (a b t) -> p a b t", a=1, b=1).to_broadcast([P, QUAD, REP, P]),
                    rates(src.bitcast(f32)), MUL), (name, qd), pool(1, NHC * P))

            def fn(e):
                e.matmul(bank[TR][:, :], after_r[:, :], gm_hi[:, :, :].rearrange("p a t -> p (a t)"), start=True, stop=False)
                return e.matmul(bank[TR][:, :], after_r[:, :], gm_lo[:, :, :].rearrange("p a t -> p (a t)"), start=False, stop=True)
            yield from do("pe", [("gm_lo", qd), *bank_free[TR]], fn, ("D psum", qd), pe(2, NHC * P, 1))
            war = [("PT", old), ("Cn", old)] if old >= 0 else []
            yield from do("act", [("D psum", qd), *war], lambda e: e.activation(
                E[:, pb, :, :].rearrange("p a t -> p (a t)"), bank[TR][:, :], ACT.Exp), ("E", qd), act(1, NHC * P))
            bank_free[TR] = [("E", qd)]

            def fn(e):
                for i, c in enumerate(cs):
                    r = e.matmul(bank[YZ][:, i * 2 * P:(i + 1) * 2 * P], kqT[:, ub, c, 0, :],
                                 kqT[:, ub, c, :, :].rearrange("p a t -> p (a t)"), start=True, stop=True)
                return r
            yield from do("pe", [("act", u, "k"), ("act", u, "q"), *bank_free[YZ]], fn, ("kq psum", qd), pe(QUAD, 2 * P, 4))
            yield from do("dve", [("kq psum", qd), *war], lambda e: e.tensor_tensor(
                kq[:, pb, :, :, :].rearrange("p c a t -> p c (a t)"), bank[YZ][:, :].rearrange("p (c a) -> p c a", c=QUAD),
                C["kq"].rearrange("p (o a) -> p o a", o=1).to_broadcast([P, QUAD, 2 * P]), MUL), ("kq", qd), dve(1, QUAD * 2 * P))
            bank_free[YZ] = [("kq", qd)]

            def fn(e):
                for i, c in enumerate(cs):
                    for h in range(REP):
                        r = e.scalar_tensor_tensor(Cn[:, pb, REP * i + h, :], E[:, pb, REP * i + h, :], cw[:, ub, c, h:h + 1],
                                                   kq[:, pb, i, 0, :], MUL, MUL)
                return r
            war = [("Y psum", old, LEVELS - 1)] if old >= 0 else []
            yield from do("dve", [("E", qd), ("kq", qd), ("c", u), *war], fn, ("Cn", qd), dve(NHC, P))
            yield from do("dve", [("Cn", qd)], lambda e: e.tensor_tensor(
                XT[:, pb, :, :], Cn[:, pb, :, :], C["pairs"].rearrange("p (o t) -> p o t", o=1).to_broadcast([P, NHC, P]), MUL),
               ("pairs", qd), dve(1, NHC * P))
            yield from do("dve", [("pairs", qd)], lambda e: e.tensor_tensor(
                XT[:, pb, :, :], XT[:, pb, :, :], C["ident"].rearrange("p (o t) -> p o t", o=1).to_broadcast([P, NHC, P]), ADD),
               ("XT", qd, 0), dve(1, NHC * P))

            def flip(src, dst, need, name, war=()):
                def fn(e):
                    for a in range(NHC):
                        r = e.transpose(bank[TR][:, a * P:(a + 1) * P], src[:, a, :], C["ident"])
                    return r
                yield from do("pe", [need, *bank_free[TR]], fn, (name, "psum"), pe(NHC, P, 2))
                yield from do("act", [(name, "psum"), *war], lambda e: e.copy(dst.rearrange("p a t -> p (a t)"), bank[TR][:, :]), name, act(1, NHC * P))
                bank_free[TR] = [name]

            yield from flip(XT[:, pb, :, :], X[:, pb, :, :], ("XT", qd, 0), ("X", qd, 0))
            war = [("C done", qd - 3)] if qd >= 3 else []

            def fn(e):
                for i in range(QUAD):
                    r = e.tensor_tensor(PT[:, qd % 3, REP * i:REP * i + REP, :], E[:, pb, REP * i:REP * i + REP, :],
                                        kq[:, pb, i, 1:2, :].to_broadcast([P, REP, P]), MUL)
                return r
            yield from do("pool", [("E", qd), ("kq", qd), *war], fn, ("PT", qd), pool(2, 2 * P))
            def level(lev):
                s = 1 << lev
                nb = P // (2 * s)

                def halves(a):
                    return a.rearrange("p (b i s) -> p b i s", b=nb, i=2)[:, :, 0, :]

                def fn(e):
                    for a in range(NHC):
                        r = e.matmul(bank[YZ][:, a * P // 2:(a + 1) * P // 2], Cn[:, pb, a, :], halves(X[:, pb, a, :]), start=True, stop=True)
                    return r
                yield from do("pe", [("X", qd, lev - 1), ("Cn", qd), *bank_free[YZ]], fn, ("Y psum", qd, lev), pe(NHC, P // 2, 4))
                war = [("Z psum", qd, lev - 1)] if lev > 1 else ([("Z psum", old, LEVELS - 1)] if old >= 0 else [])
                yield from do("dve", [("Y psum", qd, lev), *war], lambda e: e.tensor_tensor(
                    Y[:, pb, :, :], bank[YZ][:, 0:NHC * P // 2].rearrange("p (a m) -> p a m", a=NHC),
                    C[f"rows{lev}"].rearrange("p (o m) -> p o m", o=1).to_broadcast([P, NHC, P // 2]), MUL), ("Y", qd, lev), dve(1, NHC * P // 2))

                def fn(e):
                    for a in range(NHC):
                        r = e.matmul(bank[YZ][:, (NHC + a) * P // 2:(NHC + a + 1) * P // 2], XT[:, pb, a, :], Y[:, pb, a, :], start=True, stop=True)
                    return r
                yield from do("pe", [("Y", qd, lev), ("XT", qd, lev - 1)], fn, ("Z psum", qd, lev), pe(NHC, P // 2, 4))
                view = X[:, pb, :, :].rearrange("p a (b i s) -> p (a b) i s", b=nb, i=2)[:, :, 0, :]
                z = bank[YZ][:, NHC * P // 2:].rearrange("p (ab s) -> p ab s", s=s)
                yield from do("dve", [("Z psum", qd, lev)], lambda e: e.tensor_tensor(view, view, z, ADD), ("X", qd, lev), dve(1, NHC * P // 2))
                bank_free[YZ] = [("X", qd, lev)]
                if lev < LEVELS - 1:
                    yield from flip(X[:, pb, :, :], XT[:, pb, :, :], ("X", qd, lev), ("XT", qd, lev))
                else:
                    war = [("C done", qd - 2)] if qd >= 2 else []
                    yield from flip(X[:, pb, :, :], inv[:, pb, :, :], ("X", qd, lev), ("inverse", qd), war)

            for lev in range(1, LEVELS):
                yield from level(lev)

        def stream_c():
            for qd in range(NQ):
                yield from stage_c(qd)

        def stage_c(qd):
            u, half, pb = qd // 2, qd % 2, qd % 2
            gr, sb, ub = unit(u)
            Sf = S[:, :, :].rearrange("p h d -> p (h d)")
            if sb == 0 and half == 0:
                yield from do("dve", [("queries", qd - 1, QUAD - 1), ("S", qd - 1, QUAD - 1)] if qd else [], lambda e: e.memset(S[:, :, :], 0.0), ("S", qd, -1), 0.3)
            else:
                pr.alias(("S", qd, -1), ("S", qd - 1, QUAD - 1))
            def chunk(i):
                c = half * QUAD + i
                cg, h0 = sb * CPS + c, REP * gr
                before = (qd, i - 1) if i else ((qd - 1, QUAD - 1) if qd else None)
                after = lambda name: [(name, *before)] if before else []
                yield from do("pe", [("S", qd, i - 1), ("act", u, "k"), *bank_free[K_BANK]], lambda e: e.matmul(
                    bank[K_BANK][:, 0:REP * HD], kqT[:, ub, c, 0, :], Sf, start=True, stop=True), ("keys", qd, i), pe(1, REP * HD, 4))

                def fn(e):
                    for h in range(REP):
                        r = e.scalar_tensor_tensor(R[:, h, :], bank[K_BANK][:, h * HD:(h + 1) * HD], neg_decay[:, cg, h0 + h:h0 + h + 1],
                                                   v_tok[:, ub, c, h, :], MUL, ADD)
                    return r
                yield from do("dve", [("keys", qd, i), ("v_tok", u, 0), ("v_tok", u, 1), *after("W psum")], fn, ("R", qd, i), dve(REP, HD))
                yield from do("pe", [("act", u, "q"), *bank_free[Q_BANK]], lambda e: e.matmul(
                    bank[Q_BANK][:, 0:REP * HD], kqT[:, ub, c, 1, :], Sf, start=True, stop=True), ("queries", qd, i), pe(1, REP * HD, 4))

                def fn(e):
                    for h in range(REP):
                        r = e.mul(O[:, pb, i, h, :], bank[Q_BANK][:, h * HD:(h + 1) * HD], decay[:, cg, h0 + h:h0 + h + 1])
                    return r
                yield from do("act", [("queries", qd, i), *([("og stored", qd - 2)] if qd >= 2 else [])], fn, ("QS", qd, i), act(REP, HD, 1))

                def fn(e):
                    for h in range(REP):
                        r = e.matmul(bank[K_BANK][:, (REP + h) * HD:(REP + h + 1) * HD], inv[:, pb, REP * i + h, :], R[:, h, :], start=True, stop=True)
                    return r
                yield from do("pe", [("R", qd, i), ("inverse", qd)], fn, ("W psum", qd, i), pe(REP, HD, 4))

                def fn(e):
                    for h in range(REP):
                        r = e.mul(U[:, h, :], bank[K_BANK][:, (REP + h) * HD:(REP + h + 1) * HD], cw[:, ub, c, h:h + 1])
                    return r
                yield from do("act", [("W psum", qd, i), *after("O psum"), *after("UR")], fn, ("U", qd, i), act(REP, HD, 1))

                def fn(e):
                    for h in range(REP):
                        r = e.tensor_scalar(UR[:, h, :], U[:, h, :], remain[:, cg, h0 + h:h0 + h + 1], None, MUL)
                    return r
                yield from do("dve", [("U", qd, i), *after("state psum")], fn, ("UR", qd, i), dve(REP, HD // 2))
                yield from do("pe", [("UR", qd, i), ("k_tok", u)], lambda e: e.matmul(
                    bank[K_BANK][:, 0:REP * HD], k_tok[:, ub, c, :], UR[:, :, :].rearrange("p h d -> p (h d)"), start=True, stop=True),
                    ("state psum", qd, i), pe(1, REP * HD, 4))

                def fn(e):
                    for h in range(REP):
                        r = e.scalar_tensor_tensor(S[:, h, :], S[:, h, :], total[:, cg, h0 + h:h0 + h + 1],
                                                   bank[K_BANK][:, h * HD:(h + 1) * HD], MUL, ADD)
                    return r
                yield from do("dve", [("state psum", qd, i), ("queries", qd, i)], fn, ("S", qd, i), dve(REP, HD))
                bank_free[K_BANK] = [("S", qd, i)]

                def fn(e):
                    for h in range(REP):
                        r = e.matmul(bank[Q_BANK][:, (REP + h) * HD:(REP + h + 1) * HD], PT[:, qd % 3, REP * i + h, :], U[:, h, :], start=True, stop=True)
                    return r
                yield from do("pe", [("U", qd, i), ("PT", qd), ("QS", qd, i)], fn, ("O psum", qd, i), pe(REP, HD, 4))
                if i == QUAD - 1:
                    pr.alias(("C done", qd), ("O psum", qd, i))
                yield from do("dve", [("O psum", qd, i), ("QS", qd, i)], lambda e: e.tensor_tensor(
                    O[:, pb, i, :, :].rearrange("p h d -> p (h d)"), O[:, pb, i, :, :].rearrange("p h d -> p (h d)"),
                    bank[Q_BANK][:, REP * HD:2 * REP * HD], ADD), ("O", qd, i), dve(1, REP * HD))
                bank_free[Q_BANK] = [("O", qd, i)]

            for i in range(QUAD):
                yield from chunk(i)

        def stream_d():
            def quad(qd):
                u, half, pb = qd // 2, qd % 2, qd % 2
                gr, sb, ub = unit(u)

                def fn(e):
                    for i in range(QUAD):
                        for h in range(REP):
                            r = e.activation(squares[:, REP * i + h, :], O[:, pb, i, h, :], ACT.Square, accum_out=ms[:, pb, REP * i + h:REP * i + h + 1])
                    return r
                yield from do("act", [("O", qd, 0), ("O", qd, 1), *([("ms", qd - 1)] if qd else []), *([("og", qd - 2)] if qd >= 2 else [])],
                              fn, ("ms", qd), act(NHC, 2 * HD))
                m3 = ms[:, pb, :].rearrange("p (c h) -> p c h", c=QUAD)
                qe = q_eps[:, ub, half * QUAD:(half + 1) * QUAD].rearrange("p (c o) -> p c o", o=1).to_broadcast([P, QUAD, REP])
                yield from do("dve", [("ms", qd), ("q_eps", u)], lambda e: e.scalar_tensor_tensor(m3, m3, 4.0 / HD, qe, MUL, ADD), ("ms+", qd), 0.07)
                yield from do("pool", [("ms+", qd)], lambda e: e.tensor_tensor(ms[:, pb, :], ms[:, pb, :], neg_half_pow[:, 0:NHC], ALU.pow), ("factor", qd), 1.0)

                def fn(e):
                    for i in range(QUAD):
                        for h in range(REP):
                            r = e.scalar_tensor_tensor(O[:, pb, i, h, :], O[:, pb, i, h, :], ms[:, pb, REP * i + h:REP * i + h + 1],
                                                       z_gate[:, ub, half * QUAD + i, h, :], MUL, MUL)
                    return r
                yield from do("dve", [("factor", qd), ("z_gate", u, half)], fn, ("og", qd), dve(NHC, HD))
                pr.alias(("D done", qd), ("og", qd))
                t0 = sb * SB + half * QUAD * P
                dst = og_dram[t0:t0 + QUAD * P, REP * gr * HD:REP * (gr + 1) * HD].rearrange("(c p) d -> p c d", p=P)
                yield from dma([("og", qd)], lambda e: e.dma_start(dst, O[:, pb, :, :, :].rearrange("p c h d -> p c (h d)")),
                               ("og stored", qd), f"og{pb}", 3.0)

            for qd in range(NQ):
                yield from quad(qd)

        NU, NQ = KEY_HEADS * NSB, KEY_HEADS * NSB * 2
        pr.run(stream_c(), stream_b(0), stream_b(1), conv_stream(("k", "v0")), conv_stream(("q", "v1")), stream_d(), stream_a(), weights())
        pr.fence()
        p2.close()
        att.close()

        gate_acc = alloc(top, "gate_acc", [NT, D])
        p3 = ExitStack()
        FP = 8
        FW = DFF // FP
        NF = FW // P
        raw = alloc(p3, "ffn_raw", [2, ND * FW])
        fw = {(n, s): alloc(p3, f"ffn_w{n}_{s}", [2, ND * FW], f32r) for n in (1, 2) for s in ("hi", "lo")}

        def rows(a, m):
            return a.rearrange("p (k n) -> p k n", k=ND if m == 1 else NF)
        bias1 = alloc(p3, "bias1", [TOP, DFF // P])
        bias2 = alloc(p3, "bias2", [TOP, D])
        hid = alloc(p3, "hid", [2, SB])
        h_hi = alloc(p3, "h_hi", [2, NF, SB], f32r)
        h_lo = alloc(p3, "h_lo", [2, NF, SB], f32r)
        th3 = alloc(p3, "th3", [D])
        index = {}
        parts = [(k, f) for k in range(TOP) for f in range(FP)]
        blocks = [(n, sb) for n in range(len(parts)) for sb in range(NSB)]

        def load_index(e):
            index.update({k: e.value_load(expert[0:1, k:k + 1], min_val=0, max_val=EXPERTS - 1) for k in range(TOP)})
        pr.wait("sp", "expert")
        pr.queue["sp"].append(load_index)
        for i in range(8):
            bank_free[i] = []

        def part_weights():
            for n in range(len(parts)):
                for m in (1, 2):
                    yield from one_load(n, m)
                    if 2 * n + m > 1:
                        yield from one_split(*((n, 1) if m == 2 else (n - 1, 2)))
                if n == 0:
                    yield from biases()
            yield from one_split(len(parts) - 1, 2)

        def one_load(n, m):
            k, f = parts[n]
            i = 2 * n + m - 1
            if m == 1:
                src = lambda: w1[bass.ds(index[k], 1), :, f * FW:(f + 1) * FW].rearrange("e (a p) n -> p (e a) n", p=P)
            else:
                src = lambda: w2[bass.ds(index[k], 1), f * FW:(f + 1) * FW, :].rearrange("e (a p) n -> p (e a) n", p=P)
            yield from dma([("ffn lo", i - 2)] if i >= 2 else [], lambda e: e.dma_start(rows(raw[:, i % 2, :], m), src()),
                           ("ffn raw", i), f"ffn{i % 2}", 4.0)

        def one_split(n, m):
            i = 2 * n + m - 1
            war = [("part done", n - 2, m)] if n >= 2 else []
            hi, lo = fw[m, "hi"][:, n % 2, :], fw[m, "lo"][:, n % 2, :]
            yield from do("act", [("ffn raw", i), *war], lambda e: e.copy(hi, raw[:, i % 2, :]), ("ffn hi", i), act(1, ND * FW))
            yield from do("pool", [("ffn hi", i)], lambda e: e.tensor_tensor(lo, raw[:, i % 2, :], hi.bitcast(f32), SUB), ("ffn lo", i), pool(1, ND * FW))

        def biases():
            for k in range(TOP):
                yield from dma([], lambda e, k=k: e.dma_start(bias1[:, k, :], b1[bass.ds(index[k], 1), :, :].rearrange("e p n -> p (e n)")), ("bias1", k), f"b1{k}")
                yield from dma([], lambda e, k=k: e.dma_start(bias2[:, k, :], b2[bass.ds(index[k], 1), :].rearrange("e n -> (e n)").partition_broadcast(P)),
                               ("bias2", k), f"b2{k}")

        def accumulator():
            for t in range(NT):
                yield from do("dve", [("bias2", 0), ("rw", 0)], lambda e, t=t: e.tensor_scalar(
                    gate_acc[:, t, :], bias2[:, 0, :], rw[:, 0, t:t + 1], None, MUL), ("bias a", t), dve(1, D // 2))
                yield from do("dve", [("bias2", 1), ("rw", 1), ("bias a", t)], lambda e, t=t: e.scalar_tensor_tensor(
                    gate_acc[:, t, :], bias2[:, 1, :], rw[:, 1, t:t + 1], gate_acc[:, t, :], MUL, ADD), ("acc", -1, t), dve(1, D))

        def hidden():
            for j in range(len(blocks)):
                for ft in range(NF):
                    yield from hidden_tile(j, ft)

        def hidden_tile(j, ft):
            n, sb = blocks[j]
            k, f = parts[n]
            i = j * NF + ft
            b, hb, buf = i % 4, j % 2, i % 2
            toks = slice(sb * SB, (sb + 1) * SB)
            fs = slice(ft * P, (ft + 1) * P)
            yield from project_steps(
                bank[b][:, :], lambda a: (rows(fw[1, "hi"][:, n % 2, :], 1)[:, a, fs], rows(fw[1, "lo"][:, n % 2, :], 1)[:, a, fs]),
                lambda a: (xn_hi[:, a, toks], xn_lo[:, a, toks]), ND, [("ffn lo", 2 * n), *bank_free[b]], ("hidden psum", i), pe(3, SB, 1))
            if sb == NSB - 1 and ft == NF - 1:
                pr.alias(("part done", n, 1), ("hidden psum", i))
            bank_free[b] = [("gelu", i)]
            war = [("h lo", i - 2)] if i >= 2 else []
            yield from do("act", [("hidden psum", i), ("bias1", k), *war], lambda e: e.activation(
                hid[:, buf, :], bank[b][:, :], ACT.Gelu_apprx_tanh, bias=bias1[:, k, f * NF + ft:f * NF + ft + 1]), ("gelu", i), act(1, SB))
            war = [("y psum", j - 2, CPS - 1)] if j >= 2 else []
            yield from do("act", [("gelu", i), *war], lambda e: e.copy(h_hi[:, hb, ft, :], hid[:, buf, :]), ("h hi", i), act(1, SB))
            yield from do("dve", [("h hi", i)], lambda e: e.tensor_tensor(
                h_lo[:, hb, ft, :], hid[:, buf, :], h_hi[:, hb, ft, :].bitcast(f32), SUB), ("h lo", i), dve(1, SB))

        def down():
            for j in range(len(blocks)):
                for c in range(CPS):
                    yield from down_tile(j, c)

        def down_tile(j, c):
            n, sb = blocks[j]
            k, f = parts[n]
            hb, b, t = j % 2, 4 + c % 4, sb * CPS + c
            ts = slice(c * P, (c + 1) * P)
            yield from project_steps(
                bank[b][:, :], lambda i: (h_hi[:, hb, i, ts], h_lo[:, hb, i, ts]),
                lambda i: (rows(fw[2, "hi"][:, n % 2, :], 2)[:, i, :], rows(fw[2, "lo"][:, n % 2, :], 2)[:, i, :]), NF,
                [("ffn lo", 2 * n + 1), ("h lo", (j + 1) * NF - 1), *bank_free[b]], ("y psum", j, c), pe(3, D, 1))
            if sb == NSB - 1 and c == CPS - 1:
                pr.alias(("part done", n, 2), ("y psum", j, c))
            bank_free[b] = [("acc", n, t)]
            yield from do("dve", [("y psum", j, c), ("acc", n - 1, t), ("rw", k)], lambda e: e.scalar_tensor_tensor(
                gate_acc[:, t, :], bank[b][:, :], rw[:, k, t:t + 1], gate_acc[:, t, :], MUL, ADD), ("acc", n, t), dve(1, D))
            if n == len(parts) - 1:
                war = [("gate", t - 1)] if t else []
                yield from do("act", [("acc", n, t), *war], lambda e: e.activation(th3[:, :], gate_acc[:, t, :], ACT.Tanh, scale=0.5), ("gate tanh", t), act(1, D))
                yield from do("dve", [("gate tanh", t)], lambda e: e.scalar_tensor_tensor(
                    gate_acc[:, t, :], th3[:, :], 1.0, gate_acc[:, t, :], ADD, MUL), ("gate", t), dve(1, D))

        pr.run(hidden(), down(), part_weights(), accumulator())
        pr.fence()
        p3.close()
        xn_life.close()

        p4 = ExitStack()
        WO = 4
        wo_raw = alloc(p4, "wo_raw", [2, HEADS // WO, D])
        wo_hi = alloc(p4, "wo_hi", [HEADS, D], f32r)
        wo_lo = alloc(p4, "wo_lo", [HEADS, D], f32r)
        nw = alloc(p4, "nw", [1])
        og_in = alloc(p4, "og_in", [2, HEADS * HD])
        x_res = alloc(p4, "x_res", [2, D])
        ogT_hi = alloc(p4, "ogT_hi", [2, HEADS, P], f32r)
        ogT_lo = alloc(p4, "ogT_lo", [2, HEADS, P], f32r)
        y_out = alloc(p4, "y_out", [2, D])
        for i in range(8):
            bank_free[i] = []
        def loads4():
            for t in range(NT):
                yield from dma([("og^T", t - 2, 3)] if t >= 2 else [], lambda e, t=t: e.dma_start(
                    og_in[:, t % 2, :], og_dram[t * P:(t + 1) * P, :]), ("og in", t), f"ogin{t % 2}")
                yield from dma([("out sum", t - 2)] if t >= 2 else [], lambda e, t=t: e.dma_start(
                    x_res[:, t % 2, :], x[0, t * P:(t + 1) * P, :]), ("x res", t), f"xres{t % 2}", 2.0)

        def output_weights():
            yield from dma([], lambda e: e.dma_start(nw[:, :], norm_w.rearrange("(p o) -> p o", o=1)), "norm weight", "nw", 2.0)
            for m in range(WO):
                yield from output_part(m)

        def output_part(m):
            hs = slice(m * HEADS // WO, (m + 1) * HEADS // WO)
            r = wo_raw[:, m % 2, :, :]
            yield from dma([("wo lo", m - 2)] if m >= 2 else [], lambda e: e.dma_start(
                r, w_out[hs.start * HD:hs.stop * HD, :].rearrange("(a p) n -> p a n", p=P)), ("wo raw", m), f"wo{m % 2}", 5.0)
            yield from do("dve", [("wo raw", m), "norm weight"], lambda e: e.tensor_scalar(r, r, nw[:, 0:1], None, MUL), ("wo scaled", m), dve(1, D * 2))
            yield from do("act", [("wo scaled", m)], lambda e: e.copy(wo_hi[:, hs, :], r), ("wo hi", m), act(1, D * 4))
            yield from do("pool", [("wo hi", m)], lambda e: e.tensor_tensor(wo_lo[:, hs, :], r, wo_hi[:, hs, :].bitcast(f32), SUB), ("wo lo", m), pool(1, D * 4))

        def turn():
            for t in range(NT):
                for m in range(4):
                    yield from turn_part(t, m)

        def turn_part(t, m):
            tb = t % 2
            hs = slice(4 * m, 4 * m + 4)

            def fn(e):
                for h in range(4):
                    r = e.transpose(bank[m][:, h * P:(h + 1) * P], og_in[:, tb, (4 * m + h) * P:(4 * m + h + 1) * P], C["ident"])
                return r
            yield from do("pe", [("og in", t), *bank_free[m]], fn, ("og^T", t, m), pe(4, P, 2))
            war = [("s psum", t - 2)] if t >= 2 else []
            src = bank[m][:, :].rearrange("p (h t) -> p h t", h=4)
            bank_free[m] = [("ogT lo", t, m)]
            yield from do("act", [("og^T", t, m), *war], lambda e: e.copy(ogT_hi[:, tb, hs, :], src), ("ogT hi", t, m), act(1, SB))
            yield from do("dve", [("ogT hi", t, m)], lambda e: e.tensor_tensor(
                ogT_lo[:, tb, hs, :], src, ogT_hi[:, tb, hs, :].bitcast(f32), SUB), ("ogT lo", t, m), dve(1, SB))

        def finish():
            for t in range(NT):
                yield from finish_tile(t)

        def finish_tile(t):
            tb = t % 2
            b = 4 + tb
            for m in range(4):
                for i in range(4 * m, 4 * m + 4):
                    yield from do("pe", [("ogT lo", t, m), ("wo lo", m * WO // 4), *(bank_free[b] if i == 0 else [])], lambda e, i=i: split3(
                        e, bank[b][:, :], (ogT_hi[:, tb, i, :], ogT_lo[:, tb, i, :]), (wo_hi[:, i, :], wo_lo[:, i, :]), i == 0, i == HEADS - 1),
                        ("s psum", t) if i == HEADS - 1 else ("s psum", t, i), pe(3, D, 1))
            bank_free[b] = [("gated", t)]
            war = [("out stored", t - 2)] if t >= 2 else []
            yield from do("dve", [("s psum", t), *war], lambda e: e.scalar_tensor_tensor(
                y_out[:, tb, :], bank[b][:, :], 0.5, gate_acc[:, t, :], MUL, MUL), ("gated", t), dve(1, D))
            yield from do("pool", [("gated", t), ("x res", t)], lambda e: e.tensor_tensor(
                y_out[:, tb, :], y_out[:, tb, :], x_res[:, tb, :], ADD), ("out sum", t), pool(1, D))
            yield from dma([("out sum", t)], lambda e: e.dma_start(out[0, t * P:(t + 1) * P, :], y_out[:, tb, :]), ("out stored", t), f"out{tb}")

        pr.run(finish(), turn(), output_weights(), loads4())
        pr.wait("sp", ("out stored", NT - 1), ("out stored", NT - 2), ("og stored", NQ - 1), ("og stored", NQ - 2))

        block = top.enter_context(nc.Block())
        for name, key in (("sync", "sp"), ("tensor", "pe"), ("scalar", "act"), ("vector", "dve"), ("gpsimd", "pool")):
            def run(e, key=key):
                for op in pr.queue[key]:
                    op(e)
            dict(sync=block.sync, tensor=block.tensor, scalar=block.scalar, vector=block.vector, gpsimd=block.gpsimd)[name](run)
        p4.close()


def kernel(L0_attn_hidden_states, L0_attn_W_qkv, L0_attn_W_z, L0_attn_W_b, L0_attn_W_a, L0_attn_conv_w, L0_attn_dt_bias,
           L0_attn_A_log, L0_attn_norm_weight, L0_attn_W_out, L0_ffn_gate_w, L0_ffn_w1, L0_ffn_b1, L0_ffn_w2, L0_ffn_b2):
    import concourse.bacc as bacc
    from concourse.bass_utils import run_bass_kernel_spmd

    wqkv = np.asarray(L0_attn_W_qkv)
    wz = np.asarray(L0_attn_W_z)
    kd = KEY_HEADS * HD
    groups = []
    for gr in range(KEY_HEADS):
        qs, ks = slice(gr * HD, (gr + 1) * HD), slice(kd + gr * HD, kd + (gr + 1) * HD)
        vs = slice(2 * kd + REP * gr * HD, 2 * kd + REP * (gr + 1) * HD)
        cols = np.concatenate([wqkv[:, ks], wqkv[:, qs], wqkv[:, vs], wz[:, REP * gr * HD:REP * (gr + 1) * HD]], 1)
        groups.append(cols.reshape(ND, P, GW).transpose(1, 0, 2))
    cw = np.asarray(L0_attn_conv_w)
    tiles = []
    for gr in range(KEY_HEADS):
        for at in (kd + gr * HD, gr * HD, 2 * kd + REP * gr * HD, 2 * kd + (REP * gr + 1) * HD):
            tiles.append(cw[at:at + HD])
    const, where = constants()
    arrays = {
        "x": np.asarray(L0_attn_hidden_states),
        "small_w": np.concatenate([np.asarray(L0_attn_W_b), np.asarray(L0_attn_W_a), np.asarray(L0_ffn_gate_w).T], 1),
        "group_w": np.stack(groups),
        "conv_w": np.stack(tiles, 1),
        "dt_bias": np.asarray(L0_attn_dt_bias),
        "a_log": np.asarray(L0_attn_A_log),
        "norm_w": np.asarray(L0_attn_norm_weight),
        "w_out": np.asarray(L0_attn_W_out),
        "w1": np.asarray(L0_ffn_w1),
        "b1": np.asarray(L0_ffn_b1).reshape(EXPERTS, DFF // P, P).transpose(0, 2, 1),
        "w2": np.asarray(L0_ffn_w2),
        "b2": np.asarray(L0_ffn_b2),
        "const": const,
    }
    arrays = {k: np.ascontiguousarray(v) for k, v in arrays.items()}
    nc = bacc.Bacc("TRN2", target_bir_lowering=False, num_devices=1)
    f32 = mybir.dt.float32
    aps = {k: nc.dram_tensor(k, v.shape, f32, kind="ExternalInput").ap() for k, v in arrays.items()}
    out = nc.dram_tensor("out", (1, T, D), f32, kind="ExternalOutput").ap()
    og_dram = nc.dram_tensor("og_dram", (T, HEADS * HD), f32, kind="Internal").ap()
    build(nc, where=where, og_dram=og_dram, out=out, **aps)
    r = run_bass_kernel_spmd(nc, [arrays], core_ids=[0])
    return r.results[0]["out"]
```

```python
from contextlib import ExitStack

import concourse.bass as bass
import numpy as np
from concourse import mybir

P = 128
T, D = 2048, 512
KEY_HEADS, HEADS, HD = 8, 16, 128
KW = 4
EXPERTS, DFF, TOP = 8, 2048, 2
LN_EPS, L2_EPS, RMS_EPS = 1e-5, 1e-6, 1e-6
NT = T // P
ND = D // P
SB = 512
NSB = T // SB
CPS = SB // P
REP = HEADS // KEY_HEADS
QUAD = 2
NHC = QUAD * REP
NAB = 2 * HEADS + EXPERTS
NBUF = 3
LEVELS = 7
SERIES = 9
KINDS = {"k": (0, P), "q": (P, P), "v0": (2 * P, P), "v1": (3 * P, P), "z": (4 * P, REP * HD)}
GW = 4 * P + REP * HD


def constants():
    i = np.arange(P)
    parts = {
        "ident": np.eye(P),
        "one": np.ones((P, 1)),
        "kq": np.concatenate([-(i[:, None] < i[None, :]).astype(float), (i[:, None] <= i[None, :])], 1),
    }
    bit = (i[:, None] >> np.arange(LEVELS + 1)) & 1
    parts["odd"], parts["even"] = bit[:, :LEVELS], 1 - bit[:, :LEVELS]
    parts["same"] = bit[:, :LEVELS] == bit[:, 1:]
    parts["diff"] = bit[:, :LEVELS] != bit[:, 1:]
    for lev in range(LEVELS):
        block = i >> lev
        parts[f"join{lev}"] = (block[:, None] ^ 1) == block[None, :]
    parts["ones"] = np.ones((P, P))
    parts["after"] = i[:, None] > i[None, :]
    parts["iota"] = np.broadcast_to(np.arange(EXPERTS), (P, EXPERTS))
    at, where = 0, {}
    for name, a in parts.items():
        where[name] = (at, at + a.shape[1])
        at += a.shape[1]
    where["upto"] = (where["kq"][0] + P, where["kq"][1])
    return np.concatenate([np.asarray(a, np.float32) for a in parts.values()], 1), where


class Program:
    HOP, OWN = 0.3, 0.1

    def __init__(self, nc, ctx):
        self.nc, self.ctx = nc, ctx
        self.queue = {e: [] for e in ("pe", "act", "dve", "pool", "sp")}
        self.sem = {e: ctx.enter_context(nc.semaphore(f"s_{e}")) for e in ("pe", "act", "dve", "pool")}
        self.count, self.done, self.seen = {}, {}, {}
        self.clock = {e: 0.0 for e in self.queue}
        self.end = {}

    def wait(self, engine, *steps):
        for step in steps:
            sem, value = self.done[step]
            if self.seen.get((engine, sem), 0) < value:
                self.seen[engine, sem] = value
                self.queue[engine].append(lambda e, s=self.sem[sem], v=value: e.wait_ge(s, v))

    def alias(self, name, step):
        self.done[name], self.end[name] = self.done[step], self.end[step]

    def start(self, engine, waits):
        at = self.clock[engine]
        for w in waits:
            if w not in self.done:
                return None
            at = max(at, self.end[w] + (self.OWN if self.done[w][0] == engine else self.HOP))
        return at

    def issue(self, engine, lane, waits, fn, step, cost):
        at = self.start(engine, waits)
        self.wait(engine, *waits)
        by = 1 if lane is None else 16
        sem = engine if lane is None else lane
        if sem not in self.sem:
            self.sem[sem] = self.ctx.enter_context(self.nc.semaphore(f"s_dma_{lane}"))
        self.count[sem] = self.count.get(sem, 0) + by
        self.done[step] = (sem, self.count[sem])
        self.end[step] = at + cost
        self.clock[engine] = at + (cost if lane is None else 0.05)
        self.queue[engine].append(lambda e, s=self.sem[sem], by=by: fn(e).then_inc(s, by))

    def do(self, engine, waits, fn, step, cost=0.2):
        yield engine, None, waits, fn, step, cost

    def dma(self, waits, fn, step, lane, cost=3.0):
        yield "sp", lane, waits, fn, step, cost

    def run(self, *streams):
        heads = {n: op for n, s in enumerate(streams) if (op := next(s, None)) is not None}
        while heads:
            ready = [(at, n) for n, op in heads.items() if (at := self.start(op[0], op[2])) is not None]
            assert ready, ("no step can go on", {n: op[4] for n, op in heads.items()})
            first = min(at for at, _ in ready)
            n = min((n for at, n in ready if at <= first + 0.02))
            self.issue(*heads[n])
            heads[n] = next(streams[n], None)
            if heads[n] is None:
                del heads[n]

    def fence(self, engines=("pe", "act", "dve", "pool", "sp")):
        for sem, value in self.count.items():
            self.done["fence", sem] = (sem, value)
        for engine in engines:
            self.wait(engine, *[("fence", sem) for sem in self.count])
        now = max(self.clock.values())
        self.clock = {e: now for e in self.clock}


def pe(n, cols, passes):
    return n * passes * max(cols, P) / 2400


def dve(n, cols, scalar=False):
    return n * ((0.13 if scalar else 0.07) + cols / 960)


def act(n, cols, scales=0):
    return n * (0.09 + 0.05 * scales + cols / 1200)


def pool(n, cols):
    return n * (0.1 + cols * 1.75e-3)


def build(nc, x, small_w, group_w, conv_w, dt_bias, a_log, norm_w, w_out, w1, b1, w2, b2, const, where, og_dram, out):
    f32, f32r, u32 = mybir.dt.float32, mybir.dt.float32r, mybir.dt.uint32
    ALU, ACT, AX = mybir.AluOpType, mybir.ActivationFunctionType, mybir.AxisListType
    MUL, ADD, SUB = ALU.mult, ALU.add, ALU.subtract

    top = ExitStack()
    with top:
        pr = Program(nc, top)
        do, dma = pr.do, pr.dma

        def now(*steps):
            for s in steps:
                for op in s:
                    pr.issue(*op)

        def alloc(ctx, name, free, dtype=f32, side="left"):
            return ctx.enter_context(nc.sbuf_tensor(name, [P, *free], dtype, side=side))

        bank = [top.enter_context(nc.psum_tensor(f"bank{i}", [P, 512], f32)) for i in range(8)]
        bank_free = {i: [] for i in range(8)}

        kept = where["ones"][0]
        cst = alloc(top, "cst", [kept])
        C = {n: cst[:, a:b] for n, (a, b) in where.items() if b <= kept}
        xn_life = ExitStack()
        xn_hi = alloc(xn_life, "xn_hi", [ND, T], f32r, side="right")
        xn_lo = alloc(xn_life, "xn_lo", [ND, T], f32r, side="right")
        rw = alloc(top, "rw", [TOP, NT])
        expert = alloc(top, "expert", [8], u32)

        def split3(e, ps, lhs, rhs, first, last):
            (lh, ll), (rh, rl) = lhs, rhs
            e.matmul(ps, lh, rh, start=first, stop=False)
            e.matmul(ps, lh, rl, start=False, stop=False)
            return e.matmul(ps, ll, rh, start=False, stop=last)

        def project(ps, lhs, rhs, n):
            def fn(e):
                for i in range(n):
                    r = split3(e, ps, lhs(i), rhs(i), i == 0, i == n - 1)
                return r
            return fn

        att = ExitStack()
        g_hi = alloc(att, "g_hi", [NT, HEADS], f32r)
        g_lo = alloc(att, "g_lo", [NT, HEADS], f32r)
        beta = alloc(att, "beta", [NT, HEADS])
        decay = alloc(att, "decay", [NT, HEADS])
        neg_decay = alloc(att, "neg_decay", [NT, HEADS])
        remain = alloc(att, "remain", [NT, HEADS])
        total = alloc(att, "total", [NT, HEADS])
        after_r = alloc(att, "after_r", [P], f32r)
        taps = alloc(att, "taps", [4 * KEY_HEADS, KW])
        half_pow = alloc(att, "half_pow", [CPS])
        neg_half_pow = alloc(att, "neg_half_pow", [CPS])

        p2 = ExitStack()
        w_raw = alloc(p2, "w_raw", [2, ND, P])
        w_hi = {k: alloc(p2, f"w_hi_{k}", [ND, n], f32r) for k, (_, n) in KINDS.items()}
        w_lo = {k: alloc(p2, f"w_lo_{k}", [ND, n], f32r) for k, (_, n) in KINDS.items()}
        pre = alloc(p2, "pre", [2, SB + KW - 1])
        halo = alloc(p2, "halo", [4, KW - 1])
        conv = alloc(p2, "conv", [2, SB])
        kqT = alloc(p2, "kqT", [NBUF, CPS, 2, P])
        square = alloc(p2, "square", [SB])
        k_tok = alloc(p2, "k_tok", [NBUF, CPS, HD])
        v_tok = alloc(p2, "v_tok", [NBUF, CPS, REP, HD])
        z_gate = alloc(p2, "z_gate", [NBUF, CPS, REP, HD])
        norms = alloc(p2, "norms", [NBUF, 2, CPS])
        k_len = alloc(p2, "k_len", [NBUF, CPS])
        inv_n = alloc(p2, "inv_n", [CPS])
        q_eps = alloc(p2, "q_eps", [NBUF, CPS])
        cw = alloc(p2, "cw", [NBUF, CPS, REP])
        c_rem = alloc(p2, "c_rem", [NBUF, CPS, REP])
        ms = alloc(p2, "ms", [2, NHC])

        p1 = ExitStack()
        cst1 = alloc(p1, "cst1", [const.shape[1] - kept])
        C.update({n: cst1[:, a - kept:b - kept] for n, (a, b) in where.items() if a >= kept})
        x_in = alloc(p1, "x_in", [NT, D])
        stats = alloc(p1, "stats", [NT, 6])
        moments = alloc(p1, "moments", [NT, 2])
        rstd = alloc(p1, "rstd", [NT])
        sw = alloc(p1, "sw", [ND, NAB])
        sw_hi = alloc(p1, "sw_hi", [ND, NAB], f32r)
        sw_lo = alloc(p1, "sw_lo", [ND, NAB], f32r)
        ab_T = alloc(p1, "ab_T", [SB])
        ab = alloc(p1, "ab", [NT, NAB])
        hvec = {n: alloc(p1, n, [HEADS]) for n in ("dtb", "alog", "arate")}
        t_ = [alloc(p1, f"tmp{i}", [NT, HEADS]) for i in range(4)]
        g = alloc(p1, "g", [NT, HEADS])
        scores = alloc(p1, "scores", [EXPERTS])
        best = alloc(p1, "best", [8])
        expert_f = alloc(p1, "expert_f", [8])
        pick = alloc(p1, "pick", [TOP, EXPERTS])
        picked = alloc(p1, "picked", [NT, EXPERTS])
        lmax = alloc(p1, "lmax", [NT])
        lsum = alloc(p1, "lsum", [NT])

        XPARTS = 8

        def loads():
            n = NT // XPARTS
            for q in range(XPARTS):
                dst = x_in[:, q * n:(q + 1) * n, :]
                src = x[0, q * n * P:(q + 1) * n * P, :].rearrange("(a p) d -> p a d", p=P)
                yield from dma([], lambda e, dst=dst, src=src: e.dma_start(dst, src), ("x", q), f"x{q}", 6.0 + 2 * q)
                if q == 0:
                    yield from dma([], lambda e: e.dma_start(cst[:, :], const[:, 0:kept]), "constants", "const")
                    yield from dma([], lambda e: e.dma_start(cst1[:, :], const[:, kept:]), "constants 1", "const1")
                    yield from dma([], lambda e: e.dma_start(sw[:, :, :], small_w.rearrange("(k p) n -> p k n", p=P)), "small weights", "sw")
            yield from dma([], lambda e: e.dma_start(hvec["dtb"][:, :], dt_bias[:].partition_broadcast(P)), "dt_bias", "dtb")
            yield from dma([], lambda e: e.dma_start(hvec["alog"][:, :], a_log[:].partition_broadcast(P)), "A_log", "alog")
            yield from dma([], lambda e: e.dma_start(taps[:, :, :], conv_w[:, :, :]), "conv weights", "taps")

        def setup():
            yield from do("pool", [], lambda e: e.memset(neg_half_pow[:, :], -0.5), "neg_half_pow")
            yield from do("pool", [], lambda e: e.memset(half_pow[:, :], 0.5), "half_pow")
            yield from do("act", ["small weights"], lambda e: e.copy(sw_hi[:, :, :], sw[:, :, :]), "sw_hi")
            yield from do("pool", ["sw_hi"], lambda e: e.tensor_tensor(sw_lo[:, :, :], sw[:, :, :], sw_hi[:, :, :].bitcast(f32), SUB), "sw_lo")
            yield from do("act", ["constants 1"], lambda e: e.copy(after_r[:, :], C["after"]), "after_r")
            yield from do("dve", ["conv weights"], lambda e: e.tensor_scalar(taps[:, :, :], taps[:, :, :], 0.5, None, MUL), "taps")

        def layernorm():
            n = NT // XPARTS
            for q in range(XPARTS):
                for t in range(q * n, (q + 1) * n):
                    yield from do("dve", [("x", q)], lambda e, t=t: e.bn_stats(stats[:, t, :], x_in[:, t, :]), ("stats", t), dve(1, D))
                    yield from do("dve", [("stats", t)], lambda e, t=t: e.bn_aggr(moments[:, t, :], stats[:, t, :]), ("moments", t), 0.07)
                r = slice(q * n, (q + 1) * n)
                yield from do("dve", [("moments", q * n + n - 1)],
                              lambda e, r=r: e.tensor_scalar(rstd[:, r], moments[:, r, 1], LN_EPS, None, ADD), ("var", q), 0.07)
                yield from do("pool", [("var", q), "neg_half_pow"],
                              lambda e, r=r: e.tensor_tensor(rstd[:, r], rstd[:, r], neg_half_pow[:, 0:n], ALU.pow), ("rstd", q), 1.0)

        def rows_of(t):
            q, b = t // (NT // XPARTS), 2 + t % 4
            yield from do("dve", [("rstd", q)], lambda e: e.tensor_scalar(
                x_in[:, t, :], x_in[:, t, :], moments[:, t, 0:1], rstd[:, t:t + 1], SUB, MUL), ("xn", t), dve(1, D // 2, True))

            def transposes(e):
                for k in range(ND):
                    r = e.transpose(bank[b][:, k * P:(k + 1) * P], x_in[:, t, k * P:(k + 1) * P], C["ident"])
                return r
            yield from do("pe", [("xn", t), "constants", *([("xn_lo", t - 4)] if t >= 4 else [])], transposes, ("xn^T", t), pe(ND, P, 2))
            src = bank[b][:, :].rearrange("p (k c) -> p k c", k=ND)
            dst = slice(t * P, (t + 1) * P)
            yield from do("act", [("xn^T", t)], lambda e: e.copy(xn_hi[:, :, dst], src), ("xn_hi", t), act(1, D))
            yield from do("dve", [("xn_hi", t)], lambda e: e.tensor_tensor(
                xn_lo[:, :, dst], src, xn_hi[:, :, dst].bitcast(f32), SUB), ("xn_lo", t), dve(1, D))

        def all_rows(par):
            for t in range(par, NT, 2):
                yield from rows_of(t)

        def xn_ready(sb):
            return [("xn_lo", t) for t in range(sb * CPS, (sb + 1) * CPS)]

        def small_projections():
            for sb in range(NSB):
                yield from small_projection(sb)

        def small_projection(sb):
            toks = slice(sb * SB, (sb + 1) * SB)
            war = [("ab^T", sb - 1)] if sb else []
            yield from do("pe", ["sw_lo", *xn_ready(sb), *war], project(
                bank[6][0:NAB, :], lambda i: (sw_hi[:, i, :], sw_lo[:, i, :]),
                lambda i: (xn_hi[:, i, toks], xn_lo[:, i, toks]), ND), ("ab^T psum", sb), pe(3 * ND, SB, 1))
            war = [("ab psum", sb - 1)] if sb else []
            yield from do("act", [("ab^T psum", sb), *war], lambda e: e.copy(ab_T[0:NAB, :], bank[6][0:NAB, :]), ("ab^T", sb), act(1, SB))
            half = sb * 2 // NSB

            def fn(e):
                for c in range(CPS):
                    at = (sb * CPS + c) % 8 * 64
                    r = e.transpose(bank[7][:, at:at + NAB], ab_T[0:NAB, c * P:(c + 1) * P], C["ident"][0:NAB, 0:NAB])
                return r
            yield from do("pe", [("ab^T", sb), *([("ab", 0)] if half else [])], fn, ("ab psum", sb), pe(CPS, P, 2))
            if (sb + 1) * 2 % NSB == 0:
                yield from do("act", [("ab psum", sb)], lambda e: e.copy(
                    ab[:, half * 8:half * 8 + 8, :], bank[7][:, :].rearrange("p (t c) -> p t c", t=8)[:, :, 0:NAB]), ("ab", half), act(1, 8 * NAB))

        AB = [("ab", 0), ("ab", 1)]
        b_, a_, lg = ab[:, :, 0:HEADS], ab[:, :, HEADS:2 * HEADS], ab[:, :, 2 * HEADS:NAB]

        def decay_gates():
            yield from do("act", AB, lambda e: e.activation(beta[:, :, :], b_, ACT.Exp, scale=-1.0), "exp(-b)")
            yield from do("dve", ["exp(-b)"], lambda e: e.tensor_scalar(beta[:, :, :], beta[:, :, :], 1.0, None, ADD), "1+exp(-b)")
            yield from do("dve", ["1+exp(-b)"], lambda e: e.reciprocal(beta[:, :, :], beta[:, :, :]), "beta")

            def bc(v):
                return v[:, :].rearrange("p (o h) -> p o h", o=1).to_broadcast([P, NT, HEADS])
            y, w, s, acc = t_
            yield from do("act", ["A_log"], lambda e: e.activation(hvec["arate"][:, :], hvec["alog"][:, :], ACT.Exp), "exp(A_log)")
            yield from do("dve", [*AB, "dt_bias"], lambda e: e.tensor_tensor(y[:, :, :], a_, bc(hvec["dtb"]), ADD), "y")
            yield from do("act", ["y"], lambda e: e.activation(w[:, :, :], y[:, :, :], ACT.Abs), "|y|")
            yield from do("act", ["|y|"], lambda e: e.activation(w[:, :, :], w[:, :, :], ACT.Exp, scale=-1.0), "w")
            yield from do("dve", ["w"], lambda e: e.tensor_scalar(s[:, :, :], w[:, :, :], 2.0, None, ADD), "w+2")
            yield from do("dve", ["w+2"], lambda e: e.reciprocal(s[:, :, :], s[:, :, :]), "1/(w+2)")
            yield from do("dve", ["1/(w+2)"], lambda e: e.tensor_tensor(s[:, :, :], w[:, :, :], s[:, :, :], MUL), "s")
            yield from do("dve", ["s"], lambda e: e.tensor_tensor(w[:, :, :], s[:, :, :], s[:, :, :], MUL), "s^2")
            yield from do("dve", ["s^2"], lambda e: e.tensor_scalar(acc[:, :, :], w[:, :, :], 1.0 / (2 * SERIES + 1), 1.0 / (2 * SERIES - 1), MUL, ADD), ("series", SERIES))
            for k in range(SERIES - 1, 0, -1):
                yield from do("dve", [("series", k + 1)], lambda e: e.tensor_tensor(acc[:, :, :], acc[:, :, :], w[:, :, :], MUL), ("series*", k))
                yield from do("dve", [("series*", k)], lambda e, k=k: e.tensor_scalar(acc[:, :, :], acc[:, :, :], 1.0 / (2 * k - 1), None, ADD), ("series", k))
            yield from do("dve", [("series", 1)], lambda e: e.scalar_tensor_tensor(acc[:, :, :], acc[:, :, :], 2.0, s[:, :, :], MUL, MUL), "log1p")
            yield from do("dve", ["log1p"], lambda e: e.scalar_tensor_tensor(acc[:, :, :], y[:, :, :], 0.0, acc[:, :, :], ALU.max, ADD), "softplus")
            yield from do("dve", ["softplus", "exp(A_log)"], lambda e: e.tensor_tensor(acc[:, :, :], acc[:, :, :], bc(hvec["arate"]), MUL), "-g")
            yield from do("dve", ["-g"], lambda e: e.tensor_scalar(g[:, :, :], acc[:, :, :], -1.0, None, MUL), "g")
            yield from do("act", ["g"], lambda e: e.copy(g_hi[:, :, :], g[:, :, :]), "g_hi")
            yield from do("dve", ["g_hi"], lambda e: e.tensor_tensor(g_lo[:, :, :], g[:, :, :], g_hi[:, :, :].bitcast(f32), SUB), "g_lo")
            flat = g[:, :, :].rearrange("p t h -> p (t h)")
            for n, (mask, dst) in enumerate((("upto", decay), ("after", remain), ("ones", total))):
                ps = (bank[6][:, 0:NT * HEADS], bank[2][:, 0:NT * HEADS], bank[4][:, 0:NT * HEADS])[n]
                yield from do("pe", ["g", "constants", "constants 1"], lambda e, m=mask, ps=ps: e.matmul(ps, C[m], flat, start=True, stop=True), ("sum", mask))
                yield from do("act", [("sum", mask)], lambda e, ps=ps, d=dst: e.activation(
                    d[:, :, :].rearrange("p t h -> p (t h)"), ps, ACT.Exp), ("exp sum", mask))
            yield from do("dve", [("exp sum", "upto")], lambda e: e.tensor_scalar(neg_decay[:, :, :], decay[:, :, :], -1.0, None, MUL), "neg_decay")

        def router():
            def score(e):
                for t in range(NT):
                    r = e.matmul(bank[7][:, 0:EXPERTS], C["ones"], lg[:, t, :], start=t == 0, stop=t == NT - 1)
                return r
            yield from do("pe", [*AB, "constants 1"], score, "scores psum")
            yield from do("dve", ["scores psum"], lambda e: e.tensor_copy(scores[:, :], bank[7][:, 0:EXPERTS]), "scores")
            yield from do("dve", ["scores"], lambda e: e.max(best[:, :], scores[:, :]), "best")
            yield from do("dve", ["best"], lambda e: e.max_index(expert[:, :], best[:, :], scores[:, :]), "expert")
            yield from do("dve", ["expert"], lambda e: e.tensor_copy(expert_f[:, :], expert[:, :]), "expert_f")
            for k in range(TOP):
                yield from do("dve", ["expert_f", "constants 1"], lambda e, k=k: e.tensor_scalar(
                    pick[:, k, :], C["iota"], expert_f[:, k:k + 1], None, ALU.is_equal), ("pick", k))
                yield from do("dve", [("pick", k)], lambda e, k=k: e.tensor_tensor(
                    picked[:, :, :], lg, pick[:, k:k + 1, :].to_broadcast([P, NT, EXPERTS]), MUL), ("picked", k))
                yield from do("dve", [("picked", k)], lambda e, k=k: e.reduce_sum(rw[:, k, :], picked[:, :, :], AX.X), ("logit", k))
            yield from do("dve", [("logit", 0), ("logit", 1)], lambda e: e.tensor_tensor(lmax[:, :], rw[:, 0, :], rw[:, 1, :], ALU.max), "logit max")
            for k in range(TOP):
                yield from do("dve", ["logit max"], lambda e, k=k: e.tensor_tensor(rw[:, k, :], rw[:, k, :], lmax[:, :], SUB), ("centred", k))
                yield from do("act", [("centred", k)], lambda e, k=k: e.activation(rw[:, k, :], rw[:, k, :], ACT.Exp), ("exp logit", k))
            yield from do("dve", [("exp logit", 0), ("exp logit", 1)], lambda e: e.tensor_tensor(lsum[:, :], rw[:, 0, :], rw[:, 1, :], ADD), "logit sum")
            yield from do("dve", ["logit sum"], lambda e: e.reciprocal(lsum[:, :], lsum[:, :]), "1/logit sum")
            for k in range(TOP):
                yield from do("dve", ["1/logit sum"], lambda e, k=k: e.tensor_tensor(rw[:, k, :], rw[:, k, :], lsum[:, :], MUL), ("rw", k))

        gates = ["neg_decay", ("exp sum", "after"), ("exp sum", "ones"), "beta", "g_lo", "after_r", "half_pow", ("rw", 0), ("rw", 1)]
        p1.close()

        p1.close()

        p2b = ExitStack()
        gm_hi = alloc(p2b, "gm_hi", [NHC, P], f32r)
        gm_lo = alloc(p2b, "gm_lo", [NHC, P], f32r)
        E = alloc(p2b, "E", [4, NHC, P])
        kq = alloc(p2b, "kq", [2, QUAD, 2, P])
        inv = alloc(p2b, "inv", [2, NHC, P])
        Cn = alloc(p2b, "Cn", [2, QUAD, REP, P])
        L = alloc(p2b, "L", [2, 2, QUAD, P])
        L_odd = alloc(p2b, "L_odd", [2, QUAD, P])
        first = alloc(p2b, "first", [2, QUAD, P])
        second = alloc(p2b, "second", [2, QUAD, P])
        second_T = alloc(p2b, "second_T", [2, QUAD, P])
        keep_1 = alloc(p2b, "keep_1", [2, QUAD, P])
        keep_2 = alloc(p2b, "keep_2", [2, QUAD, P])
        Y = alloc(p2b, "Y", [2, QUAD, P])
        S = alloc(p2b, "S", [REP, HD])
        R = alloc(p2b, "R", [REP, HD])
        U = alloc(p2b, "U", [REP, HD])
        O = alloc(p2b, "O", [2, QUAD, REP, HD])
        squares = alloc(p2b, "squares", [HD])

        A_BANKS, K_BANK, Q_BANK = (0, 1), 6, 7

        def b_banks(par):
            return 2 + 2 * par, 3 + 2 * par

        def weights():
            names = [(gr, kind, part) for gr in range(KEY_HEADS) for kind, (_, width) in KINDS.items() for part in range(width // P)]
            for n, (gr, kind, part) in enumerate(names):
                at = KINDS[kind][0] + part * P
                src, dst = group_w[gr, :, :, at:at + P], w_raw[:, n % 2, :, :]
                yield from dma([("w lo part", *names[n - 2])] if n >= 2 else [], lambda e, dst=dst, src=src: e.dma_start(dst, src),
                               ("w raw", *names[n]), f"w{n % 2}", 3.0)
                if n:
                    yield from split_weights(*names[n - 1], (n - 1) % 2)
            yield from split_weights(*names[-1], (len(names) - 1) % 2)

        def split_weights(gr, kind, part, slot):
            raw = w_raw[:, slot, :, :]
            cols = slice(part * P, (part + 1) * P)
            war = [("last projection", gr - 1, kind)] if gr else []
            yield from do("act", [("w raw", gr, kind, part), *war], lambda e: e.copy(w_hi[kind][:, :, cols], raw), ("w hi", gr, kind, part), act(1, ND * P))
            yield from do("pool", [("w hi", gr, kind, part)], lambda e: e.tensor_tensor(
                w_lo[kind][:, :, cols], raw, w_hi[kind][:, :, cols].bitcast(f32), SUB), ("w lo part", gr, kind, part), pool(1, ND * P))
            if cols.stop == KINDS[kind][1]:
                pr.alias(("w lo", gr, kind), ("w lo part", gr, kind, part))

        CONV = {"k": (0, 0), "q": (1, 1), "v0": (0, 2), "v1": (1, 3)}
        BEFORE = {"k": (-1, "v0"), "q": (-1, "v1"), "v0": (0, "k"), "v1": (0, "q")}

        def unit(u):
            return u // NSB, u % NSB, u % NBUF

        def project_steps(ps, lhs, rhs, n, waits, step, cost):
            for i in range(n):
                yield from do("pe", waits if i == 0 else [], lambda e, i=i: split3(e, ps, lhs(i), rhs(i), i == 0, i == n - 1),
                              step if i == n - 1 else (step, i), cost)

        def conv_stream(kinds):
            for u in range(NU):
                for kind in kinds:
                    yield from convolve(u, kind)

        def convolve(u, kind):
            gr, sb, ub = unit(u)
            s, t = CONV[kind]
            du, bk = BEFORE[kind]
            prev = [("act", u + du, bk)] if u + du >= 0 else []
            if sb == 0:
                yield from do("dve", prev, lambda e: e.memset(pre[:, s, 0:KW - 1], 0.0), ("past", u, kind), 0.07)
            else:
                yield from do("dve", [("history", u - 1, kind), *prev], lambda e: e.tensor_copy(pre[:, s, 0:KW - 1], halo[:, t, :]), ("past", u, kind), 0.07)
            wt = taps[:, 4 * gr + t, :]
            turned = [("v^T^T", u - 1, s)] if u and kind in "kq" else []
            yield from do("dve", [("pre", u, kind), ("past", u, kind), "taps", *turned], lambda e: e.tensor_scalar(
                conv[:, s, :], pre[:, s, 0:SB], wt[:, 0:1], None, MUL), ("tap", u, kind, 0), dve(1, SB // 2, True))
            for j in range(1, KW):
                yield from do("dve", [("tap", u, kind, j - 1)], lambda e, j=j: e.scalar_tensor_tensor(
                    conv[:, s, :], pre[:, s, j:j + SB], wt[:, j:j + 1], conv[:, s, :], MUL, ADD), ("tap", u, kind, j), dve(1, SB, True))
            yield from do("dve", [], lambda e: e.tensor_copy(halo[:, t, :], pre[:, s, SB:SB + KW - 1]), ("history", u, kind), 0.07)
            yield from do("act", [("tap", u, kind, KW - 1), ("history", u, kind)], lambda e: e.activation(pre[:, s, 0:SB], conv[:, s, :], ACT.Tanh), ("tanh", u, kind), act(1, SB))
            if kind in "kq":
                dst = kqT[:, ub, :, "kq".index(kind), :]
                last = 2 * (u - NBUF) + 1
                war = [("C done", last), ("kq psum", last)] if u >= NBUF else []
                src = lambda a: a.rearrange("p (c t) -> p c t", c=CPS)
            else:
                dst = conv[:, s, :]
                war = []
                src = lambda a: a
            yield from do("dve", [("tanh", u, kind), *war], lambda e: e.scalar_tensor_tensor(
                dst, src(pre[:, s, 0:SB]), 1.0, src(conv[:, s, :]), ADD, MUL), ("act", u, kind), dve(1, SB))

        def masked_rates():
            for qd in range(NQ):
                yield from masked_rate(qd)

        def masked_rate(qd):
            u, half = qd // 2, qd % 2
            gr, sb, ub = unit(u)
            c0, h0 = sb * CPS + half * QUAD, REP * gr

            def rates(src):
                return src[:, c0:c0 + QUAD, h0:h0 + REP].rearrange("p c (h o) -> p c h o", o=1).to_broadcast([P, QUAD, REP, P])

            for name, dst, src in (("gm_hi", gm_hi, g_hi), ("gm_lo", gm_lo, g_lo)):
                war = [("D psum", qd - 1)] if qd else []
                yield from do("pool", [*gates, *war], lambda e, dst=dst, src=src: e.tensor_tensor(
                    dst[:, :, :].rearrange("p (c h) t -> p c h t", c=QUAD),
                    C["upto"].rearrange("p (a b t) -> p a b t", a=1, b=1).to_broadcast([P, QUAD, REP, P]),
                    rates(src.bitcast(f32)), MUL), (name, qd), pool(1, NHC * P))

        def pair_matrices(qd):
            u, half, pb = qd // 2, qd % 2, qd % 2
            gr, sb, ub = unit(u)
            b = A_BANKS[1]

            def fn(e):
                e.matmul(bank[b][:, :], after_r[:, :], gm_hi[:, :, :].rearrange("p a t -> p (a t)"), start=True, stop=False)
                return e.matmul(bank[b][:, :], after_r[:, :], gm_lo[:, :, :].rearrange("p a t -> p (a t)"), start=False, stop=True)
            yield from do("pe", [("gm_lo", qd), *bank_free[b]], fn, ("D psum", qd), pe(2, NHC * P, 1))
            bank_free[b] = [("E", qd)]
            war = [("C done", qd - 4)] if qd >= 4 else []
            yield from do("act", [("D psum", qd), *war], lambda e: e.activation(
                E[:, qd % 4, :, :].rearrange("p a t -> p (a t)"), bank[b][:, :], ACT.Exp), ("E", qd), act(1, NHC * P))

            def fn(e):
                for i in range(QUAD):
                    c = half * QUAD + i
                    r = e.matmul(bank[b][:, i * 2 * P:(i + 1) * 2 * P], kqT[:, ub, c, 0, :],
                                 kqT[:, ub, c, :, :].rearrange("p a t -> p (a t)"), start=True, stop=True)
                return r
            yield from do("pe", [("act", u, "k"), ("act", u, "q"), *bank_free[b]], fn, ("kq psum", qd), pe(QUAD, 2 * P, 4))
            bank_free[b] = [("kq", qd)]
            war = [("PT", qd - 2), ("Cn", qd - 2)] if qd >= 2 else []
            yield from do("dve", [("kq psum", qd), *gates, *war], lambda e: e.tensor_tensor(
                kq[:, pb, :, :, :].rearrange("p c a t -> p c (a t)"), bank[b][:, :].rearrange("p (c a) -> p c a", c=QUAD),
                C["kq"].rearrange("p (o a) -> p o a", o=1).to_broadcast([P, QUAD, 2 * P]), MUL), ("kq", qd), dve(1, QUAD * 2 * P))

        def scaled_pairs():
            for qd in range(NQ):
                yield from scaled_pair(qd)

        def scaled_pair(qd):
            u, half, pb = qd // 2, qd % 2, qd % 2
            gr, sb, ub = unit(u)

            def fn(e):
                for i in range(QUAD):
                    for h in range(REP):
                        r = e.scalar_tensor_tensor(Cn[:, pb, i, h, :], E[:, qd % 4, REP * i + h, :], cw[:, ub, half * QUAD + i, h:h + 1],
                                                   kq[:, pb, i, 0, :], MUL, MUL)
                return r
            war = [("L", qd - 2, LEVELS - 1)] if qd >= 2 else []
            yield from do("dve", [("E", qd), ("kq", qd), ("c", u), *war], fn, ("Cn", qd), dve(NHC, P, True))

            def fn(e):
                for i in range(QUAD):
                    r = e.tensor_tensor(E[:, qd % 4, REP * i:REP * i + REP, :], E[:, qd % 4, REP * i:REP * i + REP, :],
                                        kq[:, pb, i, 1:2, :].to_broadcast([P, REP, P]), MUL)
                return r
            yield from do("pool", [("E", qd), ("kq", qd), ("Cn", qd)], fn, ("PT", qd), pool(2, 2 * P))

        def stream_a(part):
            for u in range(NU):
                yield from stage_a(u, part)

        def stage_a(u, part):
            gr, sb, ub = unit(u)
            toks = slice(sb * SB, (sb + 1) * SB)
            last = sb == NSB - 1
            used = 2 * (u - NBUF)
            def proj(kind):
                b = A_BANKS[part]
                yield from project_steps(
                    bank[b][:, :], lambda i: (w_hi[kind][:, i, :], w_lo[kind][:, i, :]),
                    lambda i: (xn_hi[:, i, toks], xn_lo[:, i, toks]), ND,
                    [("w lo", gr, kind), *xn_ready(sb), *bank_free[b]], ("proj", u, kind), pe(3, SB, 1))
                if last:
                    pr.alias(("last projection", gr, kind), ("proj", u, kind))
                s = CONV[kind][0]
                du, bk = BEFORE[kind]
                war = [("act", u + du, bk)] if u + du >= 0 else []
                bank_free[b] = [("pre", u, kind)]
                yield from do("act", [("proj", u, kind), *war], lambda e: e.copy(pre[:, s, KW - 1:], bank[b][:, :]), ("pre", u, kind), act(1, SB))

            def norm(kind):
                n = "kq".index(kind)
                war = [("norm psum", u - (kind == "k"), "q" if kind == "k" else "k")] if u or n else []
                yield from do("act", [("act", u, kind), *war], lambda e: e.activation(
                    square[:, :].rearrange("p (c t) -> p c t", c=CPS), kqT[:, ub, :, n, :], ACT.Square), ("square", u, kind), act(1, SB))
                b = A_BANKS[part]

                def sums(e):
                    for c in range(CPS):
                        r = e.matmul(bank[b][:, c:c + 1], square[:, c * P:(c + 1) * P], C["one"], start=True, stop=True)
                    return r
                yield from do("pe", [("square", u, kind), *bank_free[b]], sums, ("norm psum", u, kind), 0.1)
                war = [("D done", used + 1), ("v_tok", u - NBUF, 1), ("v_tok", u - NBUF, 0)] if u >= NBUF else []
                bank_free[b] = [("norm", u, kind)]
                yield from do("dve", [("norm psum", u, kind), *war], lambda e: e.tensor_scalar(
                    norms[:, ub, n, :], bank[b][:, 0:CPS], L2_EPS, None, ADD), ("norm", u, kind), 0.07)
                if kind == "k":
                    yield from do("pool", [("norm", u, "k"), "half_pow"], lambda e: e.tensor_tensor(
                        k_len[:, ub, :], norms[:, ub, 0, :], half_pow[:, :], ALU.pow), ("k_len", u), 1.0)
                    yield from do("dve", [("norm", u, "k"), *([("c", u - 1)] if u else [])], lambda e: e.reciprocal(inv_n[:, :], norms[:, ub, 0, :]), ("inv_n", u), 0.1)
                    h0 = REP * gr
                    yield from do("dve", [("inv_n", u), *gates], lambda e: e.tensor_tensor(
                        cw[:, ub, :, :], beta[:, sb * CPS:(sb + 1) * CPS, h0:h0 + REP],
                        inv_n[:, :].rearrange("p (c o) -> p c o", o=1).to_broadcast([P, CPS, REP]), MUL), ("c", u), 0.08)
                    yield from do("dve", [("c", u)], lambda e: e.tensor_tensor(
                        c_rem[:, ub, :, :], cw[:, ub, :, :], remain[:, sb * CPS:(sb + 1) * CPS, h0:h0 + REP], MUL), ("c rem", u), 0.08)
                else:
                    yield from do("dve", [("norm", u, "q")], lambda e: e.tensor_scalar(
                        q_eps[:, ub, :], norms[:, ub, 1, :], 4 * RMS_EPS * HD, None, MUL), ("q_eps", u), 0.07)

            def tokens_k():
                b = A_BANKS[part]

                def fn(e):
                    for c in range(CPS):
                        r = e.transpose(bank[b][:, c * P:(c + 1) * P], kqT[:, ub, c, 0, :], C["ident"])
                    return r
                yield from do("pe", [("act", u, "k"), *bank_free[b]], fn, ("k^T^T", u), pe(CPS, P, 2))
                war = [("C done", used + 1)] if u >= NBUF else []
                bank_free[b] = [("k_tok", u)]
                yield from do("act", [("k^T^T", u), *war], lambda e: e.copy(
                    k_tok[:, ub, :, :], bank[b][:, :].rearrange("p (c d) -> p c d", c=CPS)), ("k_tok", u), act(1, SB))

            def tokens_v(h):
                b = A_BANKS[part]
                s = CONV[f"v{h}"][0]

                def fn(e):
                    for c in range(CPS):
                        r = e.transpose(bank[b][:, c * P:(c + 1) * P], conv[:, s, c * P:(c + 1) * P], C["ident"])
                    return r
                yield from do("pe", [("act", u, f"v{h}"), *bank_free[b]], fn, ("v^T^T", u, h), pe(CPS, P, 2))
                war = [("C done", used + 1)] if u >= NBUF else []

                def scaled(e):
                    for c in range(CPS):
                        r = e.mul(v_tok[:, ub, c, h, :], bank[b][:, c * P:(c + 1) * P], k_len[:, ub, c:c + 1])
                    return r
                bank_free[b] = [("v_tok", u, h)]
                yield from do("act", [("v^T^T", u, h), ("k_len", u), *war], scaled, ("v_tok", u, h), act(CPS, P, 1))

            def z(half):
                b = A_BANKS[part]
                for c in range(2):
                    t = slice(sb * SB + (2 * half + c) * P, sb * SB + (2 * half + c + 1) * P)
                    yield from project_steps(
                        bank[b][:, c * REP * HD:(c + 1) * REP * HD], lambda i, t=t: (xn_hi[:, i, t], xn_lo[:, i, t]),
                        lambda i: (w_hi["z"][:, i, :], w_lo["z"][:, i, :]), ND,
                        [("w lo", gr, "z"), *xn_ready(sb), *bank_free[b]], ("z psum", u, half) if c else ("z psum", u, half, 0), pe(3, REP * HD, 1))
                if last and half:
                    pr.alias(("last projection", gr, "z"), ("z psum", u, half))
                dst = z_gate[:, ub, 2 * half:2 * half + 2, :, :].rearrange("p c h d -> p (c h d)")
                war = [("D done", used + half)] if u >= NBUF else []
                bank_free[b] = [("z_gate", u, half)]
                yield from do("act", [("z psum", u, half), *war], lambda e: e.activation(dst, bank[b][:, :], ACT.Tanh, scale=0.5), ("z tanh", u, half), act(1, SB))
                yield from do("dve", [("z tanh", u, half)], lambda e: e.scalar_tensor_tensor(
                    dst, dst, 1.0, bank[b][:, :], ADD, MUL), ("z_gate", u, half), dve(1, SB))

            if part == 0:
                for kind in ("k", "q", "v0", "v1"):
                    yield from proj(kind)
            else:
                yield from norm("k")
                yield from tokens_k()
                yield from pair_matrices(2 * u)
                yield from norm("q")
                yield from z(0)
                yield from pair_matrices(2 * u + 1)
                yield from tokens_v(0)
                yield from z(1)
                yield from tokens_v(1)

        def stream_b(par):
            for qd in range(par, NQ, 2):
                yield from stage_b(qd)

        def stage_b(qd):
            u, half, pb = qd // 2, qd % 2, qd % 2
            gr, sb, ub = unit(u)
            YZ, TR = b_banks(pb)
            old = qd - 2

            def two(a):
                return a.rearrange("p (o t) -> p o t", o=1).to_broadcast([P, QUAD, P])

            def flip(src, need, name):
                def fn(e):
                    for i in range(QUAD):
                        r = e.transpose(bank[TR][:, i * P:(i + 1) * P], src(i), C["ident"])
                    return r
                yield from do("pe", [*need, *bank_free[TR]], fn, name, pe(QUAD, P, 2))

            flipped = bank[TR][:, 0:QUAD * P].rearrange("p (c t) -> p c t", c=QUAD)

            def join_rows(lev):
                dst = L[:, pb, lev % 2, :, :]
                reader = ("Y psum", qd, lev - 2) if lev >= 2 else (("Y psum", old, LEVELS - 1 - (lev + 1) % 2) if old >= 0 else None)
                yield from do("act", [("-A_b", qd), *([reader] if reader else [])], lambda e: e.mul(
                    dst, Cn[:, pb, :, 0, :], C["even"][:, lev:lev + 1]), ("L even", qd, lev), act(1, QUAD * P, 1))
                if lev == 0:
                    yield from do("dve", [("L even", qd, lev)], lambda e: e.scalar_tensor_tensor(
                        dst, Cn[:, pb, :, 1, :], C["odd"][:, lev:lev + 1], dst, MUL, ADD), ("L rows", qd, lev), dve(1, QUAD * P, True))
                else:
                    war = [("L", qd, lev - 1)]
                    yield from do("pool", [("-A_b", qd), *war], lambda e: e.tensor_tensor(
                        L_odd[:, pb, :, :], Cn[:, pb, :, 1, :], C["odd"][:, lev:lev + 1].rearrange("p (o t) -> p o t", o=1).to_broadcast([P, QUAD, P]), MUL),
                        ("L odd", qd, lev), pool(1, QUAD * P))
                    yield from do("pool", [("L even", qd, lev), ("L odd", qd, lev)], lambda e: e.tensor_tensor(
                        dst, dst, L_odd[:, pb, :, :], ADD), ("L rows", qd, lev), pool(1, QUAD * P))
                yield from do("pool", [("L rows", qd, lev)], lambda e: e.tensor_tensor(
                    dst, dst, two(C[f"join{lev}"]), MUL), ("L", qd, lev), pool(1, QUAD * P))

            yield from flip(lambda i: Cn[:, pb, i, 1, :], [("Cn", qd)], ("A_b psum", qd))
            yield from do("act", [("A_b psum", qd)], lambda e: e.copy(Cn[:, pb, :, 1, :], flipped), ("-A_b", qd), act(1, QUAD * P))
            bank_free[TR] = [("-A_b", qd)]
            yield from join_rows(0)
            yield from join_rows(1)

            yield from flip(lambda i: L[:, pb, 0, i, :], [("L", qd, 0)], ("Y psum", qd, 0))
            bank_free[TR] = [("second", qd, 0)]
            war = [("inverse psum", old)] if old >= 0 else []
            for name, dst, rows, war in (("first", first, "diff", war), ("second", second, "same", [("second", old, LEVELS - 1)] if old >= 0 else [])):
                yield from do("dve", [("Y psum", qd, 0), *war], lambda e, dst=dst, rows=rows: e.scalar_tensor_tensor(
                    dst[:, pb, :, :], flipped, C[rows][:, 0:1], two(C["ident"]), MUL, ADD), (name, qd, 0), dve(1, QUAD * P, True))

            def level(lev):
                def fn(e):
                    for i in range(QUAD):
                        r = e.matmul(bank[YZ][:, i * P:(i + 1) * P], L[:, pb, lev % 2, i, :], first[:, pb, i, :], start=True, stop=True)
                    return r
                yield from do("pe", [("first", qd, lev - 1), ("L", qd, lev), *bank_free[YZ]], fn, ("Y psum", qd, lev), pe(QUAD, P, 4))
                yield from flip(lambda i: second[:, pb, i, :], [("second", qd, lev - 1)], ("second^T psum", qd, lev))
                war = [("Z psum", old, LEVELS - 1)] if lev == 1 and old >= 0 else []
                yield from do("act", [("Y psum", qd, lev), *war], lambda e: e.copy(
                    Y[:, pb, :, :], bank[YZ][:, 0:QUAD * P].rearrange("p (c t) -> p c t", c=QUAD)), ("Y", qd, lev), act(1, QUAD * P))
                yield from do("act", [("second^T psum", qd, lev)], lambda e: e.copy(second_T[:, pb, :, :], flipped), ("second^T", qd, lev), act(1, QUAD * P))
                bank_free[TR] = [("second^T", qd, lev)]
                for name, keep, rows in (("keep_1", keep_1, "same"), ("keep_2", keep_2, "diff")):
                    yield from do("act", [("first", qd, lev - 1), ("second", qd, lev - 1)], lambda e, keep=keep, rows=rows: e.mul(
                        keep[:, pb, :, :], first[:, pb, :, :], C[rows][:, lev:lev + 1]), (name, qd, lev), act(1, QUAD * P, 1))

                def fn(e):
                    for i in range(QUAD):
                        r = e.matmul(bank[YZ][:, (QUAD + i) * P:(QUAD + i + 1) * P], second_T[:, pb, i, :], Y[:, pb, i, :], start=True, stop=True)
                    return r
                yield from do("pe", [("Y", qd, lev), ("second^T", qd, lev)], fn, ("Z psum", qd, lev), pe(QUAD, P, 4))
                z = bank[YZ][:, QUAD * P:].rearrange("p (c t) -> p c t", c=QUAD)
                last = lev == LEVELS - 1
                yield from do("dve", [("Z psum", qd, lev)], lambda e: e.tensor_tensor(
                    second[:, pb, :, :], z, second[:, pb, :, :], ADD), ("joined", qd, lev), dve(1, QUAD * P))
                bank_free[YZ] = [("joined", qd, lev)]
                yield from do("dve", [("joined", qd, lev), ("keep_1", qd, lev), ("keep_2", qd, lev)], lambda e: e.scalar_tensor_tensor(
                    first[:, pb, :, :], second[:, pb, :, :], C["diff"][:, lev:lev + 1], keep_1[:, pb, :, :], MUL, ADD),
                    ("first", qd, lev), dve(1, QUAD * P, True))
                dst = inv[:, pb, :, :].rearrange("p (c h) t -> p c h t", h=REP)[:, :, 1, :] if last else second[:, pb, :, :]
                war = [("C done", qd - 2)] if last and qd >= 2 else []
                yield from do("dve", [("joined", qd, lev), ("first", qd, lev), *war], lambda e: e.scalar_tensor_tensor(
                    dst, second[:, pb, :, :], C["same"][:, lev:lev + 1], keep_2[:, pb, :, :], MUL, ADD),
                    ("second", qd, lev), dve(1, QUAD * P, True))

            for lev in range(1, LEVELS):
                if lev < LEVELS - 1:
                    yield from join_rows_after(lev, level, join_rows)
                else:
                    yield from level(lev)
            yield from flip(lambda i: first[:, pb, i, :], [("first", qd, LEVELS - 1)], ("inverse psum", qd))
            war = [("C done", qd - 2)] if qd >= 2 else []
            yield from do("act", [("inverse psum", qd), *war], lambda e: e.copy(
                inv[:, pb, :, :].rearrange("p (c h) t -> p c h t", h=REP)[:, :, 0, :], flipped), ("inverse a", qd), act(1, QUAD * P))
            bank_free[TR] = [("inverse a", qd)]

        def join_rows_after(lev, level, join_rows):
            steps = level(lev)
            yield next(steps)
            yield from join_rows(lev + 1)
            yield from steps

        def stream_c():
            for qd in range(NQ):
                yield from stage_c(qd)

        def stage_c(qd):
            u, half, pb = qd // 2, qd % 2, qd % 2
            gr, sb, ub = unit(u)
            Sf = S[:, :, :].rearrange("p h d -> p (h d)")
            if sb == 0 and half == 0:
                yield from do("dve", [("queries", qd - 1, QUAD - 1), ("S", qd - 1, QUAD - 1)] if qd else gates, lambda e: e.memset(S[:, :, :], 0.0), ("S", qd, -1), 0.3)
            else:
                pr.alias(("S", qd, -1), ("S", qd - 1, QUAD - 1))
            def chunk(i):
                c = half * QUAD + i
                cg, h0 = sb * CPS + c, REP * gr
                before = (qd, i - 1) if i else ((qd - 1, QUAD - 1) if qd else None)
                after = lambda name: [(name, *before)] if before else []
                yield from do("pe", [("S", qd, i - 1), ("act", u, "k"), *bank_free[K_BANK]], lambda e: e.matmul(
                    bank[K_BANK][:, 0:REP * HD], kqT[:, ub, c, 0, :], Sf, start=True, stop=True), ("keys", qd, i), pe(1, REP * HD, 4))

                def fn(e):
                    for h in range(REP):
                        r = e.scalar_tensor_tensor(R[:, h, :], bank[K_BANK][:, h * HD:(h + 1) * HD], neg_decay[:, cg, h0 + h:h0 + h + 1],
                                                   v_tok[:, ub, c, h, :], MUL, ADD)
                    return r
                yield from do("dve", [("keys", qd, i), ("v_tok", u, 0), ("v_tok", u, 1), *after("state psum")], fn, ("R", qd, i), dve(REP, HD, True))
                yield from do("pe", [("act", u, "q"), *bank_free[Q_BANK]], lambda e: e.matmul(
                    bank[Q_BANK][:, 0:REP * HD], kqT[:, ub, c, 1, :], Sf, start=True, stop=True), ("queries", qd, i), pe(1, REP * HD, 4))

                def fn(e):
                    for h in range(REP):
                        r = e.mul(O[:, pb, i, h, :], bank[Q_BANK][:, h * HD:(h + 1) * HD], decay[:, cg, h0 + h:h0 + h + 1])
                    return r
                yield from do("act", [("queries", qd, i), *([("og stored", qd - 2)] if qd >= 2 else [])], fn, ("QS", qd, i), act(REP, HD, 1))

                def fn(e):
                    for h in range(REP):
                        r = e.matmul(bank[K_BANK][:, (REP + h) * HD:(REP + h + 1) * HD], inv[:, pb, REP * i + h, :], R[:, h, :], start=True, stop=True)
                    return r
                yield from do("pe", [("R", qd, i), ("inverse a", qd), ("second", qd, LEVELS - 1)], fn, ("W psum", qd, i), pe(REP, HD, 4))

                def fn(e):
                    for h in range(REP):
                        r = e.mul(R[:, h, :], bank[K_BANK][:, (REP + h) * HD:(REP + h + 1) * HD], c_rem[:, ub, c, h:h + 1])
                    return r
                yield from do("act", [("W psum", qd, i), ("c rem", u)], fn, ("UR", qd, i), act(REP, HD, 1))
                def fn(e):
                    for h in range(REP):
                        r = e.mul(U[:, h, :], bank[K_BANK][:, (REP + h) * HD:(REP + h + 1) * HD], cw[:, ub, c, h:h + 1])
                    return r
                yield from do("act", [("W psum", qd, i), *after("O psum")], fn, ("U", qd, i), act(REP, HD, 1))

                yield from do("pe", [("UR", qd, i), ("U", qd, i), ("k_tok", u)], lambda e: e.matmul(
                    bank[K_BANK][:, 0:REP * HD], k_tok[:, ub, c, :], R[:, :, :].rearrange("p h d -> p (h d)"), start=True, stop=True),
                    ("state psum", qd, i), pe(1, REP * HD, 4))

                def fn(e):
                    for h in range(REP):
                        r = e.scalar_tensor_tensor(S[:, h, :], S[:, h, :], total[:, cg, h0 + h:h0 + h + 1],
                                                   bank[K_BANK][:, h * HD:(h + 1) * HD], MUL, ADD)
                    return r
                yield from do("dve", [("state psum", qd, i), ("queries", qd, i)], fn, ("S", qd, i), dve(REP, HD, True))
                bank_free[K_BANK] = [("S", qd, i)]

                def fn(e):
                    for h in range(REP):
                        r = e.matmul(bank[Q_BANK][:, (REP + h) * HD:(REP + h + 1) * HD], E[:, qd % 4, REP * i + h, :], U[:, h, :], start=True, stop=True)
                    return r
                yield from do("pe", [("U", qd, i), ("PT", qd), ("QS", qd, i)], fn, ("O psum", qd, i), pe(REP, HD, 4))
                if i == QUAD - 1:
                    pr.alias(("C done", qd), ("O psum", qd, i))
                yield from do("dve", [("O psum", qd, i), ("QS", qd, i)], lambda e: e.tensor_tensor(
                    O[:, pb, i, :, :].rearrange("p h d -> p (h d)"), O[:, pb, i, :, :].rearrange("p h d -> p (h d)"),
                    bank[Q_BANK][:, REP * HD:2 * REP * HD], ADD), ("O", qd, i), dve(1, REP * HD))
                bank_free[Q_BANK] = [("O", qd, i)]

            for i in range(QUAD):
                yield from chunk(i)

        def stream_d():
            def quad(qd):
                u, half, pb = qd // 2, qd % 2, qd % 2
                gr, sb, ub = unit(u)

                for n in range(NHC):
                    war = [("ms", qd, n - 1)] if n else [*([("ms", qd - 1, NHC - 1)] if qd else []), *([("og", qd - 2)] if qd >= 2 else [])]
                    yield from do("act", [("O", qd, n // REP), *war], lambda e, n=n: e.activation(
                        squares[:, :], O[:, pb, n // REP, n % REP, :], ACT.Square, accum_out=ms[:, pb, n:n + 1]), ("ms", qd, n), act(1, 2 * HD))
                m3 = ms[:, pb, :].rearrange("p (c h) -> p c h", c=QUAD)
                qe = q_eps[:, ub, half * QUAD:(half + 1) * QUAD].rearrange("p (c o) -> p c o", o=1).to_broadcast([P, QUAD, REP])
                yield from do("dve", [("ms", qd, NHC - 1), ("q_eps", u)], lambda e: e.scalar_tensor_tensor(m3, m3, 4.0 / HD, qe, MUL, ADD), ("ms+", qd), 0.07)
                yield from do("pool", [("ms+", qd)], lambda e: e.tensor_tensor(ms[:, pb, :], ms[:, pb, :], neg_half_pow[:, 0:NHC], ALU.pow), ("factor", qd), 1.0)

                def fn(e):
                    for i in range(QUAD):
                        for h in range(REP):
                            r = e.scalar_tensor_tensor(O[:, pb, i, h, :], O[:, pb, i, h, :], ms[:, pb, REP * i + h:REP * i + h + 1],
                                                       z_gate[:, ub, half * QUAD + i, h, :], MUL, MUL)
                    return r
                yield from do("dve", [("factor", qd), ("z_gate", u, half)], fn, ("og", qd), dve(NHC, HD, True))
                pr.alias(("D done", qd), ("og", qd))
                t0 = sb * SB + half * QUAD * P
                dst = og_dram[t0:t0 + QUAD * P, REP * gr * HD:REP * (gr + 1) * HD].rearrange("(c p) d -> p c d", p=P)
                yield from dma([("og", qd)], lambda e: e.dma_start(dst, O[:, pb, :, :, :].rearrange("p c h d -> p c (h d)")),
                               ("og stored", qd), f"og{pb}", 3.0)

            for qd in range(NQ):
                yield from quad(qd)

        NU, NQ = KEY_HEADS * NSB, KEY_HEADS * NSB * 2
        pr.run(all_rows(0), all_rows(1), setup(), layernorm(), loads(), small_projections(), decay_gates(), router(),
               stream_b(0), stream_b(1), stream_c(), scaled_pairs(), masked_rates(), stream_a(1), conv_stream(("k", "v0")), conv_stream(("q", "v1")), stream_d(), stream_a(0), weights())
        pr.fence()
        p2b.close()
        p2.close()
        att.close()

        gate_acc = alloc(top, "gate_acc", [NT, D])
        WO = 4
        wo_hi = [alloc(top, f"wo_hi{m}", [HEADS // WO, D], f32r) for m in range(WO // 2)]
        wo_lo = [alloc(top, f"wo_lo{m}", [HEADS // WO, D], f32r) for m in range(WO // 2)]
        wo_raw = [alloc(top, "wo_raw0", [HEADS // WO, D])]
        nw = alloc(top, "nw", [1])
        p3 = ExitStack()
        FP = 8
        FW = DFF // FP
        NF = FW // P
        raw = alloc(p3, "ffn_raw", [2, ND * FW])
        fw = {(n, s): alloc(p3, f"ffn_w{n}_{s}", [2, ND * FW], f32r) for n in (1, 2) for s in ("hi", "lo")}

        def rows(a, m):
            return a.rearrange("p (k n) -> p k n", k=ND if m == 1 else NF)
        bias1 = alloc(p3, "bias1", [TOP, DFF // P])
        bias2 = alloc(p3, "bias2", [TOP, D])
        hid = alloc(p3, "hid", [2, SB])
        h_hi = alloc(p3, "h_hi", [2, NF, SB], f32r)
        h_lo = alloc(p3, "h_lo", [2, NF, SB], f32r)
        th3 = bias2[:, 0, :]
        index = {}
        parts = [(k, f) for k in range(TOP) for f in range(FP)]
        blocks = [(n, sb) for n in range(len(parts)) for sb in range(NSB)]

        def load_index(e):
            index.update({k: e.value_load(expert[0:1, k:k + 1], min_val=0, max_val=EXPERTS - 1) for k in range(TOP)})
        pr.wait("sp", "expert")
        pr.queue["sp"].append(load_index)
        for i in range(8):
            bank_free[i] = []

        def part_weights():
            for n in range(len(parts)):
                for m in (1, 2):
                    yield from one_load(n, m)
                    if 2 * n + m > 1:
                        yield from one_split(*((n, 1) if m == 2 else (n - 1, 2)))
                if n == 0:
                    yield from biases()
            yield from one_split(len(parts) - 1, 2)

        def one_load(n, m):
            k, f = parts[n]
            i = 2 * n + m - 1
            if m == 1:
                src = lambda: w1[bass.ds(index[k], 1), :, f * FW:(f + 1) * FW].rearrange("e (a p) n -> p (e a) n", p=P)
            else:
                src = lambda: w2[bass.ds(index[k], 1), f * FW:(f + 1) * FW, :].rearrange("e (a p) n -> p (e a) n", p=P)
            yield from dma([("ffn lo", i - 2)] if i >= 2 else [], lambda e: e.dma_start(rows(raw[:, i % 2, :], m), src()),
                           ("ffn raw", i), f"ffn{i % 2}", 4.0)

        def one_split(n, m):
            i = 2 * n + m - 1
            war = [("part done", n - 2, m)] if n >= 2 else []
            hi, lo = fw[m, "hi"][:, n % 2, :], fw[m, "lo"][:, n % 2, :]
            yield from do("act", [("ffn raw", i), *war], lambda e: e.copy(hi, raw[:, i % 2, :]), ("ffn hi", i), act(1, ND * FW))
            yield from do("pool", [("ffn hi", i)], lambda e: e.tensor_tensor(lo, raw[:, i % 2, :], hi.bitcast(f32), SUB), ("ffn lo", i), pool(1, ND * FW))

        def biases():
            for k in range(TOP):
                yield from dma([], lambda e, k=k: e.dma_start(bias1[:, k, :], b1[bass.ds(index[k], 1), :, :].rearrange("e p n -> p (e n)")), ("bias1", k), f"b1{k}")
                yield from dma([], lambda e, k=k: e.dma_start(bias2[:, k, :], b2[bass.ds(index[k], 1), :].rearrange("e n -> (e n)").partition_broadcast(P)),
                               ("bias2", k), f"b2{k}")

        def accumulator():
            for t in range(NT):
                yield from do("dve", [("bias2", 0), ("rw", 0)], lambda e, t=t: e.tensor_scalar(
                    gate_acc[:, t, :], bias2[:, 0, :], rw[:, 0, t:t + 1], None, MUL), ("bias a", t), dve(1, D // 2))
                yield from do("dve", [("bias2", 1), ("rw", 1), ("bias a", t)], lambda e, t=t: e.scalar_tensor_tensor(
                    gate_acc[:, t, :], bias2[:, 1, :], rw[:, 1, t:t + 1], gate_acc[:, t, :], MUL, ADD), ("acc", -1, t), dve(1, D))

        def output_weights():
            for m in range(WO // 2):
                yield from load_output_part(m, 0)
                yield from output_part(m, 0, "pool")
            yield from load_output_part(WO // 2, 0)

        def load_output_part(m, slot):
            hs = slice(m * HEADS // WO, (m + 1) * HEADS // WO)
            war = [("wo lo", m - 1)] if m and slot == 0 else []
            yield from dma(war, lambda e: e.dma_start(
                wo_raw[slot][:, :, :], w_out[hs.start * HD:hs.stop * HD, :].rearrange("(a p) n -> p a n", p=P)), ("wo raw", m), f"wo{slot}", 10.0)
            if m == 0:
                yield from dma([], lambda e: e.dma_start(nw[:, :], norm_w.rearrange("(p o) -> p o", o=1)), "norm weight", "nw", 2.0)

        def output_part(m, slot, engine):
            hi, lo = wo_hi[m][:, :, :], wo_lo[m][:, :, :]
            raw = wo_raw[slot][:, :, :]
            yield from do("dve", [("wo raw", m), "norm weight"], lambda e: e.tensor_scalar(raw, raw, nw[:, 0:1], None, MUL), ("wo scaled", m), dve(1, D * 2))
            yield from do("act", [("wo scaled", m)], lambda e: e.copy(hi, raw), ("wo hi", m), act(1, D * 4))
            yield from do(engine, [("wo hi", m)], lambda e: e.tensor_tensor(lo, raw, hi.bitcast(f32), SUB), ("wo lo", m), pool(1, D * 4))

        def hidden():
            for j in range(len(blocks)):
                for ft in range(NF):
                    yield from hidden_tile(j, ft)

        def hidden_tile(j, ft):
            n, sb = blocks[j]
            k, f = parts[n]
            i = j * NF + ft
            b, hb, buf = i % 4, j % 2, i % 2
            toks = slice(sb * SB, (sb + 1) * SB)
            fs = slice(ft * P, (ft + 1) * P)
            yield from project_steps(
                bank[b][:, :], lambda a: (rows(fw[1, "hi"][:, n % 2, :], 1)[:, a, fs], rows(fw[1, "lo"][:, n % 2, :], 1)[:, a, fs]),
                lambda a: (xn_hi[:, a, toks], xn_lo[:, a, toks]), ND, [("ffn lo", 2 * n), *bank_free[b]], ("hidden psum", i), pe(3, SB, 1))
            if sb == NSB - 1 and ft == NF - 1:
                pr.alias(("part done", n, 1), ("hidden psum", i))
            bank_free[b] = [("gelu", i)]
            war = [("h lo", i - 2)] if i >= 2 else []
            yield from do("act", [("hidden psum", i), ("bias1", k), *war], lambda e: e.activation(
                hid[:, buf, :], bank[b][:, :], ACT.Gelu_apprx_tanh, bias=bias1[:, k, f * NF + ft:f * NF + ft + 1]), ("gelu", i), act(1, SB))
            war = [("y psum", j - 2, CPS - 1)] if j >= 2 else []
            yield from do("act", [("gelu", i), *war], lambda e: e.copy(h_hi[:, hb, ft, :], hid[:, buf, :]), ("h hi", i), act(1, SB))
            yield from do("dve", [("h hi", i)], lambda e: e.tensor_tensor(
                h_lo[:, hb, ft, :], hid[:, buf, :], h_hi[:, hb, ft, :].bitcast(f32), SUB), ("h lo", i), dve(1, SB))

        def down():
            for j in range(len(blocks)):
                for c in range(CPS):
                    yield from down_tile(j, c)

        def down_tile(j, c):
            n, sb = blocks[j]
            k, f = parts[n]
            hb, b, t = j % 2, 4 + c % 4, sb * CPS + c
            ts = slice(c * P, (c + 1) * P)
            yield from project_steps(
                bank[b][:, :], lambda i: (h_hi[:, hb, i, ts], h_lo[:, hb, i, ts]),
                lambda i: (rows(fw[2, "hi"][:, n % 2, :], 2)[:, i, :], rows(fw[2, "lo"][:, n % 2, :], 2)[:, i, :]), NF,
                [("ffn lo", 2 * n + 1), ("h lo", (j + 1) * NF - 1), *bank_free[b]], ("y psum", j, c), pe(3, D, 1))
            if sb == NSB - 1 and c == CPS - 1:
                pr.alias(("part done", n, 2), ("y psum", j, c))
            bank_free[b] = [("acc", n, t)]
            yield from do("dve", [("y psum", j, c), ("acc", n - 1, t), ("rw", k)], lambda e: e.scalar_tensor_tensor(
                gate_acc[:, t, :], bank[b][:, :], rw[:, k, t:t + 1], gate_acc[:, t, :], MUL, ADD), ("acc", n, t), dve(1, D, True))
            if n == len(parts) - 1:
                war = [("gate", t - 1)] if t else [("acc", -1, NT - 1)]
                yield from do("act", [("acc", n, t), *war], lambda e: e.activation(th3, gate_acc[:, t, :], ACT.Tanh, scale=0.5), ("gate tanh", t), act(1, D))
                yield from do("dve", [("gate tanh", t)], lambda e: e.scalar_tensor_tensor(
                    gate_acc[:, t, :], th3, 1.0, gate_acc[:, t, :], ADD, MUL), ("gate", t), dve(1, D))

        pr.run(hidden(), down(), part_weights(), accumulator(), output_weights())
        pr.fence()
        p3.close()
        xn_life.close()

        p4 = ExitStack()
        wo_raw.append(alloc(p4, "wo_raw1", [HEADS // WO, D]))
        wo_hi += [alloc(p4, f"wo_hi{m}", [HEADS // WO, D], f32r) for m in range(WO // 2, WO)]
        wo_lo += [alloc(p4, f"wo_lo{m}", [HEADS // WO, D], f32r) for m in range(WO // 2, WO)]
        og_in = alloc(p4, "og_in", [2, HEADS * HD])
        x_res = alloc(p4, "x_res", [2, D])
        ogT_hi = alloc(p4, "ogT_hi", [2, HEADS, P], f32r)
        ogT_lo = alloc(p4, "ogT_lo", [2, HEADS, P], f32r)
        y_out = alloc(p4, "y_out", [2, D])
        for i in range(8):
            bank_free[i] = []
        def more_output_weights():
            yield from load_output_part(WO - 1, 1)
            yield from output_part(WO // 2, 0, "dve")
            yield from output_part(WO - 1, 1, "dve")

        def loads4():
            for t in range(NT):
                yield from dma([("og^T", t - 2, 3)] if t >= 2 else [], lambda e, t=t: e.dma_start(
                    og_in[:, t % 2, :], og_dram[t * P:(t + 1) * P, :]), ("og in", t), f"ogin{t % 2}")
                yield from dma([("out sum", t - 2)] if t >= 2 else [], lambda e, t=t: e.dma_start(
                    x_res[:, t % 2, :], x[0, t * P:(t + 1) * P, :]), ("x res", t), f"xres{t % 2}", 2.0)

        def turn():
            for t in range(NT):
                for m in range(4):
                    yield from turn_part(t, m)

        def turn_part(t, m):
            tb = t % 2
            hs = slice(4 * m, 4 * m + 4)

            def fn(e):
                for h in range(4):
                    r = e.transpose(bank[m][:, h * P:(h + 1) * P], og_in[:, tb, (4 * m + h) * P:(4 * m + h + 1) * P], C["ident"])
                return r
            yield from do("pe", [("og in", t), *bank_free[m]], fn, ("og^T", t, m), pe(4, P, 2))
            war = [("s psum", t - 2)] if t >= 2 else []
            src = bank[m][:, :].rearrange("p (h t) -> p h t", h=4)
            bank_free[m] = [("ogT lo", t, m)]
            yield from do("act", [("og^T", t, m), *war], lambda e: e.copy(ogT_hi[:, tb, hs, :], src), ("ogT hi", t, m), act(1, SB))
            yield from do("dve", [("ogT hi", t, m)], lambda e: e.tensor_tensor(
                ogT_lo[:, tb, hs, :], src, ogT_hi[:, tb, hs, :].bitcast(f32), SUB), ("ogT lo", t, m), dve(1, SB))

        def finish():
            for t in range(NT):
                yield from finish_tile(t)

        def finish_tile(t):
            tb = t % 2
            b = 4 + tb
            for m in range(4):
                for i in range(4 * m, 4 * m + 4):
                    yield from do("pe", [("ogT lo", t, m), ("wo lo", m * WO // 4), *(bank_free[b] if i == 0 else [])], lambda e, i=i: split3(
                        e, bank[b][:, :], (ogT_hi[:, tb, i, :], ogT_lo[:, tb, i, :]), (wo_hi[i // 4][:, i % 4, :], wo_lo[i // 4][:, i % 4, :]), i == 0, i == HEADS - 1),
                        ("s psum", t) if i == HEADS - 1 else ("s psum", t, i), pe(3, D, 1))
            bank_free[b] = [("gated", t)]
            war = [("out stored", t - 2)] if t >= 2 else []
            yield from do("dve", [("s psum", t), *war], lambda e: e.scalar_tensor_tensor(
                y_out[:, tb, :], bank[b][:, :], 0.5, gate_acc[:, t, :], MUL, MUL), ("gated", t), dve(1, D))
            yield from do("pool", [("gated", t), ("x res", t)], lambda e: e.tensor_tensor(
                y_out[:, tb, :], y_out[:, tb, :], x_res[:, tb, :], ADD), ("out sum", t), pool(1, D))
            yield from dma([("out sum", t)], lambda e: e.dma_start(out[0, t * P:(t + 1) * P, :], y_out[:, tb, :]), ("out stored", t), f"out{tb}")

        pr.run(more_output_weights(), finish(), turn(), loads4())
        pr.wait("sp", ("out stored", NT - 1), ("out stored", NT - 2), ("og stored", NQ - 1), ("og stored", NQ - 2))

        block = top.enter_context(nc.Block())
        for name, key in (("sync", "sp"), ("tensor", "pe"), ("scalar", "act"), ("vector", "dve"), ("gpsimd", "pool")):
            def run(e, key=key):
                for op in pr.queue[key]:
                    op(e)
            dict(sync=block.sync, tensor=block.tensor, scalar=block.scalar, vector=block.vector, gpsimd=block.gpsimd)[name](run)
        p4.close()


def kernel(L0_attn_hidden_states, L0_attn_W_qkv, L0_attn_W_z, L0_attn_W_b, L0_attn_W_a, L0_attn_conv_w, L0_attn_dt_bias,
           L0_attn_A_log, L0_attn_norm_weight, L0_attn_W_out, L0_ffn_gate_w, L0_ffn_w1, L0_ffn_b1, L0_ffn_w2, L0_ffn_b2):
    import concourse.bacc as bacc
    from concourse.bass_utils import run_bass_kernel_spmd

    wqkv = np.asarray(L0_attn_W_qkv)
    wz = np.asarray(L0_attn_W_z)
    kd = KEY_HEADS * HD
    groups = []
    for gr in range(KEY_HEADS):
        qs, ks = slice(gr * HD, (gr + 1) * HD), slice(kd + gr * HD, kd + (gr + 1) * HD)
        vs = slice(2 * kd + REP * gr * HD, 2 * kd + REP * (gr + 1) * HD)
        cols = np.concatenate([wqkv[:, ks], wqkv[:, qs], wqkv[:, vs], wz[:, REP * gr * HD:REP * (gr + 1) * HD]], 1)
        groups.append(cols.reshape(ND, P, GW).transpose(1, 0, 2))
    cw = np.asarray(L0_attn_conv_w)
    tiles = []
    for gr in range(KEY_HEADS):
        for at in (kd + gr * HD, gr * HD, 2 * kd + REP * gr * HD, 2 * kd + (REP * gr + 1) * HD):
            tiles.append(cw[at:at + HD])
    const, where = constants()
    arrays = {
        "x": np.asarray(L0_attn_hidden_states),
        "small_w": np.concatenate([np.asarray(L0_attn_W_b), np.asarray(L0_attn_W_a), np.asarray(L0_ffn_gate_w).T], 1),
        "group_w": np.stack(groups),
        "conv_w": np.stack(tiles, 1),
        "dt_bias": np.asarray(L0_attn_dt_bias),
        "a_log": np.asarray(L0_attn_A_log),
        "norm_w": np.asarray(L0_attn_norm_weight),
        "w_out": np.asarray(L0_attn_W_out),
        "w1": np.asarray(L0_ffn_w1),
        "b1": np.asarray(L0_ffn_b1).reshape(EXPERTS, DFF // P, P).transpose(0, 2, 1),
        "w2": np.asarray(L0_ffn_w2),
        "b2": np.asarray(L0_ffn_b2),
        "const": const,
    }
    arrays = {k: np.ascontiguousarray(v) for k, v in arrays.items()}
    nc = bacc.Bacc("TRN2", target_bir_lowering=False, num_devices=1)
    f32 = mybir.dt.float32
    aps = {k: nc.dram_tensor(k, v.shape, f32, kind="ExternalInput").ap() for k, v in arrays.items()}
    out = nc.dram_tensor("out", (1, T, D), f32, kind="ExternalOutput").ap()
    og_dram = nc.dram_tensor("og_dram", (T, HEADS * HD), f32, kind="Internal").ap()
    build(nc, where=where, og_dram=og_dram, out=out, **aps)
    r = run_bass_kernel_spmd(nc, [arrays], core_ids=[0])
    return r.results[0]["out"]
```
